# Optimizing a Trainium2 kernel written in Bass

```python
import numpy as np
import jax
import jax.numpy as jnp

def _softmax(x, axis=-1):
    return jax.nn.softmax(x, axis=axis)

def _gelu(x):
    return jax.nn.gelu(x, approximate=True)

def _silu(x):
    return jax.nn.silu(x)

def _sigmoid(x):
    return jax.nn.sigmoid(x)

def _layernorm(x, axis=-1, eps=1e-05):
    m = jnp.mean(x, axis=axis, keepdims=True)
    v = jnp.var(x, axis=axis, keepdims=True)
    return (x - m) / jnp.sqrt(v + eps)

def _scatter_add(tgt, idx, src, axis=0):
    return tgt.at[idx].add(src)

def _segment_sum(src, seg, n):
    return jax.ops.segment_sum(src, seg, n)
kernel_name = 'mk_seq_preln_d1_jaxref_r4_9157f5'

def setup_inputs(seed: int=0):
    np.random.seed(seed)
    _w = jnp.asarray

    def _L0_attn_setup():
        import jax, jax.numpy as jnp
        import numpy as np
        HID = 512
        D_SSM = 1024
        G = 1
        S = 128
        H = 64
        P = D_SSM // H
        K = 4
        EPS = 1e-05
        CONV_DIM = D_SSM + 2 * G * S
        PROJ = 2 * D_SSM + 2 * G * S + H
        MULT = [0.25, 0.5, 0.75, 1.0, 1.25]

        def _mup_vector():
            v = np.ones(PROJ, np.float32)
            gs = G * S
            v[:D_SSM] *= MULT[0]
            v[D_SSM:2 * D_SSM] *= MULT[1]
            v[2 * D_SSM:2 * D_SSM + gs] *= MULT[2]
            v[2 * D_SSM + gs:2 * D_SSM + 2 * gs] *= MULT[3]
            v[2 * D_SSM + 2 * gs:] *= MULT[4]
            return jnp.asarray(v)

        def _reference_tuple_inner(hidden_states, residual, W_in, conv_w, conv_b, A_log, D, dt_bias, norm_w, W_out, mup_vector):
            B, L, _ = hidden_states.shape
            Hg = H // G
            proj = hidden_states @ W_in * mup_vector
            z, xBC, dt = jnp.split(proj, [D_SSM, D_SSM + CONV_DIM], axis=-1)
            xp = jnp.pad(xBC, ((0, 0), (K - 1, 0), (0, 0)))
            conv = conv_b + sum((conv_w[:, k] * xp[:, k:k + L] for k in range(K)))
            xBC = jax.nn.silu(conv)
            x = xBC[..., :D_SSM].reshape(B, L, G, Hg, P)
            Bm = xBC[..., D_SSM:D_SSM + G * S].reshape(B, L, G, S)
            Cm = xBC[..., D_SSM + G * S:].reshape(B, L, G, S)
            dt = jax.nn.softplus(dt + dt_bias).reshape(B, L, G, Hg)
            dA = jnp.exp(dt * (-jnp.exp(A_log)).reshape(G, Hg))
            xs = (x.transpose(1, 0, 2, 3, 4), Bm.transpose(1, 0, 2, 3), Cm.transpose(1, 0, 2, 3), dA.transpose(1, 0, 2, 3), dt.transpose(1, 0, 2, 3))

            def step(state, inp):
                x_t, B_t, C_t, dA_t, dt_t = inp
                state = state * dA_t[..., None, None] + (dt_t[..., None] * x_t)[..., None] * B_t[:, :, None, None, :]
                y_t = jnp.einsum('bghps,bgs->bghp', state, C_t)
                return (state, y_t)
            state0 = jnp.zeros((B, G, Hg, P, S), hidden_states.dtype)
            _, ys = jax.lax.scan(step, state0, xs)
            y = ys.transpose(1, 0, 2, 3, 4) + D.reshape(G, Hg)[..., None] * x
            y = y.reshape(B, L, D_SSM)
            g = y * jax.nn.silu(z)
            g = g * jax.lax.rsqrt(jnp.mean(jnp.square(g), axis=-1, keepdims=True) + EPS) * norm_w
            out = g @ W_out
            return (out, residual)
        key = jax.random.key(seed)
        ks = jax.random.split(key, 10)
        B, L = (2, 512)
        return {'hidden_states': jax.random.normal(ks[0], (B, L, HID), jnp.float32), 'residual': jax.random.normal(ks[1], (B, L, HID), jnp.float32), 'W_in': jax.random.normal(ks[2], (HID, PROJ), jnp.float32) * 0.02, 'conv_w': jax.random.normal(ks[3], (CONV_DIM, K), jnp.float32) * 0.2, 'conv_b': jax.random.normal(ks[4], (CONV_DIM,), jnp.float32) * 0.02, 'A_log': jax.random.uniform(ks[5], (H,), jnp.float32, 0.0, 1.0), 'D': jax.random.normal(ks[6], (H,), jnp.float32) * 0.5, 'dt_bias': jax.random.normal(ks[7], (H,), jnp.float32) * 0.5, 'norm_w': jnp.ones((D_SSM,), jnp.float32), 'W_out': jax.random.normal(ks[8], (D_SSM, HID), jnp.float32) * 0.02, 'mup_vector': _mup_vector()}
    _L0_attn_in = _L0_attn_setup()

    def _L0_ffn_setup():
        import jax, jax.numpy as jnp
        import numpy as np
        HIDDEN = 512
        INTER = 1408
        B, S = (2, 512)

        def _ternary(key, shape):
            return jax.random.randint(key, shape, -1, 2).astype(jnp.float32)
        key = jax.random.key(seed)
        ks = jax.random.split(key, 7)
        x = jax.random.normal(ks[0], (B, S, HIDDEN), dtype=jnp.float32)
        gate_w = _ternary(ks[1], (INTER, HIDDEN))
        up_w = _ternary(ks[2], (INTER, HIDDEN))
        down_w = _ternary(ks[3], (HIDDEN, INTER))
        gate_s = jax.random.uniform(ks[4], (INTER,), minval=0.01, maxval=0.1, dtype=jnp.float32)
        up_s = jax.random.uniform(ks[5], (INTER,), minval=0.01, maxval=0.1, dtype=jnp.float32)
        down_s = jax.random.uniform(ks[6], (HIDDEN,), minval=0.01, maxval=0.1, dtype=jnp.float32)
        return {'x': x, 'gate_w': gate_w, 'up_w': up_w, 'down_w': down_w, 'gate_s': gate_s, 'up_s': up_s, 'down_s': down_s}
    _L0_ffn_in = _L0_ffn_setup()
    _d = {'L0_attn_hidden_states': _L0_attn_in['hidden_states'], 'L0_attn_residual': _L0_attn_in['residual'], 'L0_attn_W_in': _L0_attn_in['W_in'], 'L0_attn_conv_w': _L0_attn_in['conv_w'], 'L0_attn_conv_b': _L0_attn_in['conv_b'], 'L0_attn_A_log': _L0_attn_in['A_log'], 'L0_attn_D': _L0_attn_in['D'], 'L0_attn_dt_bias': _L0_attn_in['dt_bias'], 'L0_attn_norm_w': _L0_attn_in['norm_w'], 'L0_attn_W_out': _L0_attn_in['W_out'], 'L0_attn_mup_vector': _L0_attn_in['mup_vector'], 'L0_ffn_gate_w': _L0_ffn_in['gate_w'], 'L0_ffn_up_w': _L0_ffn_in['up_w'], 'L0_ffn_down_w': _L0_ffn_in['down_w'], 'L0_ffn_gate_s': _L0_ffn_in['gate_s'], 'L0_ffn_up_s': _L0_ffn_in['up_s'], 'L0_ffn_down_s': _L0_ffn_in['down_s']}
    _x0 = _d['L0_attn_hidden_states']
    _d['L0_attn_hidden_states'] = jax.random.normal(jax.random.fold_in(jax.random.key(seed), 1), (2, 1024, 512), dtype=_x0.dtype)
    del _x0
    return _d

def reference(L0_attn_hidden_states, L0_attn_residual, L0_attn_W_in, L0_attn_conv_w, L0_attn_conv_b, L0_attn_A_log, L0_attn_D, L0_attn_dt_bias, L0_attn_norm_w, L0_attn_W_out, L0_attn_mup_vector, L0_ffn_gate_w, L0_ffn_up_w, L0_ffn_down_w, L0_ffn_gate_s, L0_ffn_up_s, L0_ffn_down_s):

    def _L0_attn_ref(hidden_states, residual, W_in, conv_w, conv_b, A_log, D, dt_bias, norm_w, W_out, mup_vector):
        import jax, jax.numpy as jnp
        import numpy as np
        HID = 512
        D_SSM = 1024
        G = 1
        S = 128
        H = 64
        P = D_SSM // H
        K = 4
        EPS = 1e-05
        CONV_DIM = D_SSM + 2 * G * S
        PROJ = 2 * D_SSM + 2 * G * S + H
        MULT = [0.25, 0.5, 0.75, 1.0, 1.25]

        def _mup_vector():
            v = np.ones(PROJ, np.float32)
            gs = G * S
            v[:D_SSM] *= MULT[0]
            v[D_SSM:2 * D_SSM] *= MULT[1]
            v[2 * D_SSM:2 * D_SSM + gs] *= MULT[2]
            v[2 * D_SSM + gs:2 * D_SSM + 2 * gs] *= MULT[3]
            v[2 * D_SSM + 2 * gs:] *= MULT[4]
            return jnp.asarray(v)

        def _reference_tuple_inner(hidden_states, residual, W_in, conv_w, conv_b, A_log, D, dt_bias, norm_w, W_out, mup_vector):
            B, L, _ = hidden_states.shape
            Hg = H // G
            proj = hidden_states @ W_in * mup_vector
            z, xBC, dt = jnp.split(proj, [D_SSM, D_SSM + CONV_DIM], axis=-1)
            xp = jnp.pad(xBC, ((0, 0), (K - 1, 0), (0, 0)))
            conv = conv_b + sum((conv_w[:, k] * xp[:, k:k + L] for k in range(K)))
            xBC = jax.nn.silu(conv)
            x = xBC[..., :D_SSM].reshape(B, L, G, Hg, P)
            Bm = xBC[..., D_SSM:D_SSM + G * S].reshape(B, L, G, S)
            Cm = xBC[..., D_SSM + G * S:].reshape(B, L, G, S)
            dt = jax.nn.softplus(dt + dt_bias).reshape(B, L, G, Hg)
            dA = jnp.exp(dt * (-jnp.exp(A_log)).reshape(G, Hg))
            xs = (x.transpose(1, 0, 2, 3, 4), Bm.transpose(1, 0, 2, 3), Cm.transpose(1, 0, 2, 3), dA.transpose(1, 0, 2, 3), dt.transpose(1, 0, 2, 3))

            def step(state, inp):
                x_t, B_t, C_t, dA_t, dt_t = inp
                state = state * dA_t[..., None, None] + (dt_t[..., None] * x_t)[..., None] * B_t[:, :, None, None, :]
                y_t = jnp.einsum('bghps,bgs->bghp', state, C_t)
                return (state, y_t)
            state0 = jnp.zeros((B, G, Hg, P, S), hidden_states.dtype)
            _, ys = jax.lax.scan(step, state0, xs)
            y = ys.transpose(1, 0, 2, 3, 4) + D.reshape(G, Hg)[..., None] * x
            y = y.reshape(B, L, D_SSM)
            g = y * jax.nn.silu(z)
            g = g * jax.lax.rsqrt(jnp.mean(jnp.square(g), axis=-1, keepdims=True) + EPS) * norm_w
            out = g @ W_out
            return (out, residual)
        return _reference_tuple_inner(hidden_states, residual, W_in, conv_w, conv_b, A_log, D, dt_bias, norm_w, W_out, mup_vector)[0]

    def _L0_ffn_ref(x, gate_w, up_w, down_w, gate_s, up_s, down_s):
        import jax, jax.numpy as jnp
        import numpy as np
        HIDDEN = 512
        INTER = 1408
        B, S = (2, 512)

        def _ternary(key, shape):
            return jax.random.randint(key, shape, -1, 2).astype(jnp.float32)
        b, s, h = x.shape
        xf = x.reshape(b * s, h)
        g = jnp.einsum('th,ih->ti', xf, gate_w) * gate_s
        u = jnp.einsum('th,ih->ti', xf, up_w) * up_s
        hdn = jax.nn.silu(g) * u
        out = jnp.einsum('ti,hi->th', hdn, down_w) * down_s
        return out.reshape(b, s, -1)
    x = L0_attn_hidden_states
    x = x + _L0_attn_ref(_layernorm(x, axis=-1), L0_attn_residual, L0_attn_W_in, L0_attn_conv_w, L0_attn_conv_b, L0_attn_A_log, L0_attn_D, L0_attn_dt_bias, L0_attn_norm_w, L0_attn_W_out, L0_attn_mup_vector)
    x = x + _L0_ffn_ref(_layernorm(x, axis=-1), L0_ffn_gate_w, L0_ffn_up_w, L0_ffn_down_w, L0_ffn_gate_s, L0_ffn_up_s, L0_ffn_down_s)
    return x

_drawn_inputs = setup_inputs


def setup_inputs(seed=0):
    import zlib

    import numpy as np

    out = dict(_drawn_inputs(seed))
    spreads = {'L0_attn_norm_w': (1.0, 0.2)}
    factors = {'L0_attn_A_log': 8.0, 'L0_attn_dt_bias': 4.11}
    for name, (base, spread) in spreads.items():
        noise = np.random.default_rng([zlib.crc32(name.encode()), seed]).standard_normal(out[name].shape)
        drawn = base * np.exp(spread * noise) if base else spread * noise
        out[name] = jnp.asarray(drawn.astype(out[name].dtype))
    for name, factor in factors.items():
        out[name] = (out[name] * factor).astype(out[name].dtype)
    return out
```

```python
import concourse.bass as bass
from concourse import mybir
from contextlib import ExitStack
import numpy as np

F32 = mybir.dt.float32
F32R = mybir.dt.float32r
ACT = mybir.ActivationFunctionType
ALU = mybir.AluOpType

P = 128
BATCH, LEN, HID = 2, 1024, 512
D_SSM, STATE, HEADS, TAPS = 1024, 128, 64, 4
HEAD = D_SSM // HEADS
INTER = 1408
EPS = 1e-5

BLOCKS = LEN // P
TOK = BATCH * P
KT = HID // P
ZT = D_SSM // P
CT = ZT + 2
PT = ZT + CT + 1
COLS = PT * P
GROUPS = 8
GH = HEADS // GROUPS
RING = 4
PAIRS = 10
AHEAD = 1
LOGN = 12

C_MUP, C_CW, C_CB, C_D, C_NW, C_DTB, C_ALOG = 0, PT, PT + 4 * CT, PT + 5 * CT, PT + 5 * CT + ZT, PT + 5 * CT + 2 * ZT, PT + 5 * CT + 2 * ZT + 1
C_N = C_ALOG + 1

MT = INTER // P
BT = 512
NB = BATCH * LEN // BT
TT = BT // P


def log1p_coefficients():
    k = np.arange(LOGN)
    nodes = 0.5 + 0.5 * np.cos(np.pi * (2 * k + 1) / (2 * LOGN))
    cheb = np.polynomial.chebyshev.Chebyshev.fit(nodes, np.log1p(nodes) / nodes, LOGN - 1, domain=[0, 1])
    return [float(c) for c in cheb.convert(kind=np.polynomial.Polynomial, domain=[-1, 1], window=[-1, 1]).coef]


def mixer_phase(nc, x, w_in, w_out, packed, decay_dram, x1_dram):
    with ExitStack() as ctx:
        def sb(name, shape, dt=F32):
            return ctx.enter_context(nc.sbuf_tensor(name, shape, dt))

        def sem(name):
            return ctx.enter_context(nc.semaphore(name))

        win_hi, win_lo = sb("win_hi", [P, KT, COLS], F32R), sb("win_lo", [P, KT, COLS], F32R)
        wout_hi, wout_lo = sb("wout_hi", [P, ZT, HID], F32R), sb("wout_lo", [P, ZT, HID], F32R)
        ring = sb("ring", [P, RING, GH, P])
        eye = sb("eye", [P, GH, P])
        cin = sb("cin", [P, CT, BATCH, P + TAPS - 1])
        cx = sb("cx", [P, CT, BATCH, P])
        sz = sb("sz", [P, ZT, BATCH, P])
        xn_hi, xn_lo = sb("xn_hi", [P, KT, TOK], F32R), sb("xn_lo", [P, KT, TOK], F32R)
        xpad = sb("xpad", [P, HEADS, 2 * HEAD])
        rows = sb("rows", [P, D_SSM])
        state = sb("state", [P, BATCH, D_SSM])
        gated = sb("gated", [P, ZT, P])
        g_hi, g_lo = sb("g_hi", [P, ZT, P], F32R), sb("g_lo", [P, ZT, P], F32R)
        xin = sb("xin", [P, BATCH, HID])
        xres = sb("xres", [P, BATCH, HID])
        osc = sb("osc", [P, HID])
        dt_v, dt_e, dt_p = sb("dt_v", [P, TOK]), sb("dt_e", [P, TOK]), sb("dt_p", [P, TOK])
        dt_run = sb("dt_run", [P, TOK])
        decay = sb("decay", [P, TOK])
        first = sb("first", [P, TOK])
        tok = sb("tok", [P, BATCH, 3 * P])
        to_end = sb("to_end", [P, HEADS])
        whole = sb("whole", [P, BATCH, HEADS])
        consts = sb("consts", [P, C_N])
        neg_a = sb("neg_a", [P, 1])
        stats, moments = sb("stats", [P, BATCH, 6]), sb("moments", [P, BATCH, 2])
        spread, rstd = sb("spread", [P, BATCH]), sb("rstd", [P, BATCH])
        gvar, rs = sb("gvar", [P, BATCH]), sb("rs", [P, BATCH])
        minus_half, eps = sb("minus_half", [P, BATCH]), sb("eps", [P, BATCH])
        log_terms = sb("log_terms", [P, LOGN + 1])
        ones = sb("ones", [P, 1])
        last_row = sb("last_row", [P, P])

        def pb(name, banks=1):
            return ctx.enter_context(nc.psum_tensor(name, [P, 512 * banks], F32))

        ps_proj = [pb("ps_proj0"), pb("ps_proj1")]
        ps_tok, ps_out = pb("ps_tok"), pb("ps_out")
        ps_x, ps_y = pb("ps_x", 2), pb("ps_y", 2)

        consts_in = sem("consts_in")
        staged = [sem(f"staged{n}") for n in range(RING)]
        hi_made, lo_made = sem("hi_made"), sem("lo_made")
        zeroed, filled = sem("zeroed"), sem("filled")
        a_made, a_negated = sem("a_made"), sem("a_negated")
        x_in, xres_in = sem("x_in"), sem("xres_in")
        ring_in = [sem(f"ring_in{n}") for n in range(RING)]
        decay_out, x1_out = sem("decay_out"), sem("x1_out")
        stats_made, stats_seen, moments_made, eps_added, rstd_made = sem("stats_made"), sem("stats_seen"), sem("moments_made"), sem("eps_added"), sem("rstd_made")
        xn_made, xn_turned, xn_hi_made, xn_split = sem("xn_made"), sem("xn_turned"), sem("xn_hi_made"), sem("xn_split")
        projected, evacuated = sem("projected"), sem("evacuated")
        dt_abs, dt_exp, soft_step, dt_made, decay_made, decay_cut, run_made = (
            sem("dt_abs"), sem("dt_exp"), sem("soft_step"), sem("dt_made"), sem("decay_made"), sem("decay_cut"), sem("run_made"))
        tap_first, tap_made, conv_made, halo_kept = sem("tap_first"), sem("tap_made"), sem("conv_made"), sem("halo_kept")
        tok_turned, x_turned, tok_kept, whole_made, whole_kept = (
            sem("tok_turned"), sem("x_turned"), sem("tok_kept"), sem("whole_made"), sem("whole_kept"))
        xpad_made, carry_made, carry_scaled, carry_added = sem("xpad_made"), sem("carry_made"), sem("carry_scaled"), sem("carry_added")
        scanned, end_kept, mixed = sem("scanned"), sem("end_kept"), sem("mixed")
        ring_free = sem("ring_free")
        xw_made, update_made, state_faded, state_made = sem("xw_made"), sem("update_made"), sem("state_faded"), sem("state_made")
        y_made, gate_made, g_hi_made, g_split, squared, sq_step, sq_summed = (
            sem("y_made"), sem("gate_made"), sem("g_hi_made"), sem("g_split"), sem("squared"), sem("sq_step"), sem("sq_summed"))
        ss_made, gvar_made, gvar_eps, rs_made, out_made, out_scaled, x1_made = (
            sem("ss_made"), sem("gvar_made"), sem("gvar_eps"), sem("rs_made"), sem("out_made"), sem("out_scaled"), sem("x1_made"))

        x_by_block = x.rearrange("b (i p) h -> i p b h", p=P)
        x1_by_block = x1_dram.rearrange("b (i p) h -> i p b h", p=P)
        w_in_t = w_in.rearrange("(k p) n -> p k n", p=P)
        w_out_t = w_out.rearrange("(k p) n -> p k n", p=P)
        log_c = log1p_coefficients()

        XB = ZT * P
        pieces = [("in", 2 * XB, 256), ("dt", 2 * XB + 256, 64)]
        pieces += [("in", XB + 256 * n, 256) for n in range(4)] + [("in", 256 * n, 256) for n in range(4)]
        pieces += [("out", n, 2) for n in range(4)]

        def staging(n):
            kind, at, width = pieces[n]
            slot = ring[:, n % RING, :, :].rearrange("p g t -> p (g t)")
            if kind == "out":
                return slot.rearrange("p (k n) -> p k n", k=2)
            w = 256 if kind == "in" else P
            return slot[:, 0:KT * w].rearrange("p (k n) -> p k n", k=KT)

        def event_tiles(e):
            if e == 0:
                return [PT - 1]
            if e == 1:
                return [2 * ZT, 2 * ZT + 1]
            if e < 6:
                return [ZT + 2 * (e - 2), ZT + 2 * (e - 2) + 1]
            return [2 * (e - 6), 2 * (e - 6) + 1]

        EVENT_PIECE = [1, 0, 2, 3, 4, 5, 6, 7, 8, 9]
        CONV_ORDER = [ZT, ZT + 1] + list(range(ZT))

        eye1 = eye[:, 0, :]
        flat = "p g t -> p (g t)"
        SLOT_USES = 2 * GROUPS // RING

        def in_dest(w, n):
            kind, at, width = pieces[n]
            return w[:, :, COLS - P:COLS] if kind == "dt" else w[:, :, at:at + width]

        def piece_landed(n):
            return 16 * sum(2 if pieces[m][0] == "dt" else 1 for m in range(n % RING, n + 1, RING))

        def col(at):
            return consts[:, at:at + 1]

        block = ctx.enter_context(nc.Block())

        @block.sync
        def _(sp):
            sp.dma_start(xin[:], x_by_block[0]).then_inc(x_in, 16)
            sp.dma_start(consts[:], packed).then_inc(consts_in, 16)
            for n, (kind, at, width) in enumerate(pieces):
                if n >= RING:
                    sp.wait_ge(lo_made, n - RING + 1)
                if kind == "in":
                    sp.dma_start(staging(n), w_in_t[:, :, at:at + width]).then_inc(staged[n % RING], 16)
                elif kind == "dt":
                    for half in range(2):
                        sp.dma_start(staging(n)[:, :, half * HEADS:(half + 1) * HEADS],
                                     w_in_t[:, :, at:at + width]).then_inc(staged[n % RING], 16)
                else:
                    sp.dma_start(staging(n), w_out_t[:, 2 * at:2 * at + 2, :]).then_inc(staged[n % RING], 16)
            sp.wait_ge(lo_made, len(pieces))
            sp.sem_inc(ring_free, RING)

            def store_decay(j):
                sp.wait_ge(decay_cut, 2 * j + 2)
                for b in range(BATCH):
                    sp.dma_start(decay_dram[bass.ds(j, 1), b, :, :].rearrange("a h t -> (a h) t"),
                                 decay[0:HEADS, b * P:(b + 1) * P]).then_inc(decay_out, 16)

            def load_decays(i, n):
                b, g = n // GROUPS, n % GROUPS
                sp.wait_ge(ring_free, 2 * GROUPS * i + n + 1)
                src = decay_dram[bass.ds(i, 1), b, g * GH:(g + 1) * GH, :].rearrange("a h t -> a (h t)")
                sp.dma_start(ring[:, n % RING, :, :].rearrange(flat),
                             src.to_broadcast([P, GH * P])).then_inc(ring_in[n % RING], 16)

            def body(i, last):
                if not last:
                    sp.wait_ge(xn_turned, 2 * i + 2)
                    sp.dma_start(xin[:], x_by_block[bass.ds(i + 1, 1)].rearrange("a p b h -> (a p) b h")).then_inc(x_in, 16)
                sp.wait_ge(decay_out, 32 * i + 32)
                for n in range(12):
                    load_decays(i, n)
                if not last:
                    store_decay(i + 1)
                sp.wait_ge(x1_out, AHEAD + 32 * i)
                sp.dma_start(xres[:], x_by_block[bass.ds(i, 1)].rearrange("a p b h -> (a p) b h")).then_inc(xres_in, 16)
                for n in range(12, 16):
                    load_decays(i, n)

            store_decay(0)
            with sp.Fori(0, BLOCKS - 1) as i:
                body(i, False)
            body(BLOCKS - 1, True)

        @block.gpsimd
        def _(pool):
            for free in (state_faded, rs_made, x1_made):
                pool.sem_inc(free, AHEAD)
            pool.memset(minus_half[:], -0.5).then_inc(zeroed, 1)
            pool.memset(eye[:], 0.0).then_inc(zeroed, 1)
            pool.memset(last_row[:], 0.0).then_inc(zeroed, 1)
            pool.memset(cin[:, :, :, 0:TAPS - 1], 0.0).then_inc(zeroed, 1)
            pool.memset(first[:], 0.0).then_inc(zeroed, 1)
            pool.memset(ones[:], 1.0).then_inc(zeroed, 1)
            pool.memset(xpad[:], 0.0).then_inc(zeroed, 1)
            pool.memset(state[:], 0.0).then_inc(zeroed, 1)
            pool.memset(eps[:], EPS).then_inc(zeroed, 1)
            for n, c in enumerate(log_c + [0.0]):
                pool.memset(log_terms[:, n:n + 1], c).then_inc(zeroed, 1)
            pool.wait_ge(zeroed, 9 + LOGN + 1)
            pool.affine_select(out=eye[:], in_=eye[:], compare_op=ALU.not_equal, fill=1.0, base=0,
                               pattern=[[0, GH], [-1, P]], channel_multiplier=1).then_inc(filled, 1)
            pool.affine_select(out=last_row[:], in_=last_row[:], compare_op=ALU.not_equal, fill=1.0, base=1 - P,
                               pattern=[[0, P]], channel_multiplier=1).then_inc(filled, 1)
            pool.wait_ge(a_made, 1)
            pool.tensor_scalar(neg_a[:], neg_a[:], -1.0, None, ALU.mult).then_inc(a_negated, 1)

            def norm_scale(j):
                pool.wait_ge(moments_made, 2 * j + 2)
                pool.tensor_tensor(spread[:], moments[:, :, 1], eps[:], ALU.add).then_inc(eps_added, 1)
                pool.wait_ge(eps_added, j + 1)
                pool.tensor_tensor(rstd[:], spread[:], minus_half[:], ALU.pow).then_inc(rstd_made, 1)

            STEPS = 2 * LOGN - 1

            def term(n):
                return log_terms[:, n:n + 1].to_broadcast([P, TOK])

            def softplus(j):
                pool.wait_ge(dt_exp, j + 1)
                pool.tensor_tensor(dt_p[:], dt_e[:], term(LOGN - 1), ALU.mult).then_inc(soft_step, 1)
                done = 1
                for n in reversed(range(LOGN - 1)):
                    pool.wait_ge(soft_step, STEPS * j + done)
                    pool.tensor_tensor(dt_p[:], dt_p[:], term(n), ALU.add).then_inc(soft_step, 1)
                    pool.wait_ge(soft_step, STEPS * j + done + 1)
                    pool.tensor_tensor(dt_p[:], dt_p[:], dt_e[:], ALU.mult).then_inc(soft_step, 1)
                    done += 2
                pool.wait_ge(soft_step, STEPS * j + done)
                pool.wait_ge(tok_turned, 2 * j)
                pool.tensor_tensor(dt_run[:], dt_v[:], dt_p[:], ALU.add).then_inc(dt_made, 1)

            def cut_decay(j):
                pool.wait_ge(decay_made, j + 1)
                starts = decay[:].rearrange("p (b t) -> p b t", b=BATCH)[:, :, 0:1]
                kept = first[:].rearrange("p (b t) -> p b t", b=BATCH)[:, :, 0:1]
                zero = log_terms[:, LOGN:LOGN + 1].unsqueeze(1).to_broadcast([P, BATCH, 1])
                pool.tensor_tensor(kept, starts, zero, ALU.add).then_inc(decay_cut, 1)
                pool.wait_ge(decay_cut, 2 * j + 1)
                pool.tensor_tensor(starts, starts, kept, ALU.subtract).then_inc(decay_cut, 1)

            def fade_state(i, b):
                pool.wait_ge(whole_kept, i + 1)
                pool.wait_ge(carry_made, 2 * i + b + 1)
                s = state[:, b, :].rearrange("p (h d) -> p h d", h=HEADS)
                pool.tensor_tensor(s, s, whole[:, b, :].unsqueeze(2).to_broadcast([P, HEADS, HEAD]),
                                   ALU.mult).then_inc(state_faded, 1)

            def square_sum(i, b):
                c = 2 * i + b
                pool.wait_ge(squared, c + 1)
                pool.tensor_tensor(gated[:, 0:4, :], gated[:, 0:4, :], gated[:, 4:8, :], ALU.add).then_inc(sq_step, 1)
                pool.wait_ge(sq_step, 2 * c + 1)
                pool.tensor_tensor(gated[:, 0:2, :], gated[:, 0:2, :], gated[:, 2:4, :], ALU.add).then_inc(sq_step, 1)
                pool.wait_ge(sq_step, 2 * c + 2)
                pool.tensor_tensor(gated[:, 0, :], gated[:, 0, :], gated[:, 1, :], ALU.add).then_inc(sq_summed, 1)

            def finish(i, b):
                c = 2 * i + b
                pool.wait_ge(gvar_made, AHEAD + c + 1)
                pool.tensor_tensor(gvar[:, b:b + 1], gvar[:, b:b + 1], eps[:, 0:1], ALU.add).then_inc(gvar_eps, 1)
                pool.wait_ge(gvar_eps, c + 1)
                pool.tensor_tensor(rs[:, b:b + 1], gvar[:, b:b + 1], minus_half[:, 0:1], ALU.pow).then_inc(rs_made, 1)
                pool.wait_ge(out_scaled, AHEAD + c + 1)
                pool.wait_ge(xres_in, 16 * i + 16)
                pool.tensor_tensor(xres[:, b, :], xres[:, b, :], osc[:], ALU.add).then_inc(x1_made, 1)

            def body(i, last):
                if not last:
                    norm_scale(i + 1)
                fade_state(i, 0)
                if not last:
                    softplus(i + 1)
                    cut_decay(i + 1)
                fade_state(i, 1)
                square_sum(i, 0)
                finish(i, 0)
                square_sum(i, 1)
                finish(i, 1)

            norm_scale(0)
            softplus(0)
            cut_decay(0)
            with pool.Fori(0, BLOCKS - 1) as i:
                body(i, False)
            body(BLOCKS - 1, True)

        @block.scalar
        def _(act):
            for free in (gvar_made, out_scaled, x1_out):
                act.sem_inc(free, AHEAD)
            act.wait_ge(consts_in, 16)
            act.activation(neg_a[:], col(C_ALOG), ACT.Exp).then_inc(a_made, 1)

            def weight_hi(n):
                act.wait_ge(staged[n % RING], piece_landed(n))
                if pieces[n][0] != "out":
                    act.activation(in_dest(win_hi, n), staging(n), ACT.Copy).then_inc(hi_made, 1)
                    return
                for half in range(2):
                    k = 2 * pieces[n][1] + half
                    made = act.activation(wout_hi[:, k, :], staging(n)[:, half, :], ACT.Copy, scale=col(C_NW + k))
                made.then_inc(hi_made, 1)

            def norm_hi(j, b):
                act.wait_ge(xn_turned, 2 * j + b + 1)
                act.activation(xn_hi[:, :, b * P:(b + 1) * P], ps_proj[b][:].rearrange("p (k t) -> p k t", k=KT),
                               ACT.Copy).then_inc(xn_hi_made, 1)

            def evacuate(j, e):
                act.wait_ge(projected, PAIRS * j + e + 1)
                if e == 0:
                    act.wait_ge(dt_made, j)
                    v = dict(bias=col(C_DTB), scale=col(C_MUP + PT - 1))
                    act.activation(dt_e[:], ps_proj[0][:, 0:TOK], ACT.Abs, **v).then_inc(dt_abs, 1)
                    act.activation(dt_v[:], ps_proj[0][:, 0:TOK], ACT.Relu, **v).then_inc(evacuated, 1)
                    act.wait_ge(dt_abs, j + 1)
                    act.activation(dt_e[:], dt_e[:], ACT.Exp, scale=-1.0).then_inc(dt_exp, 1)
                    return
                if e == 1:
                    act.wait_ge(halo_kept, j)
                if e == 6:
                    act.wait_ge(gate_made, 2 * j)
                for half, m in enumerate(event_tiles(e)):
                    src = ps_proj[e % 2][:, half * TOK:(half + 1) * TOK].rearrange("p (b t) -> p b t", b=BATCH)
                    if m < ZT:
                        made = act.activation(sz[:, m, :, :], src, ACT.Silu, scale=col(C_MUP + m))
                    else:
                        made = act.activation(cin[:, m - ZT, :, TAPS - 1:], src, ACT.Copy, scale=col(C_MUP + m))
                made.then_inc(evacuated, 1)

            def make_decay(j):
                act.wait_ge(dt_made, j + 1)
                act.wait_ge(decay_out, 32 * j)
                act.wait_ge(run_made, j)
                act.activation(decay[:], dt_run[:], ACT.Exp, scale=neg_a[:]).then_inc(decay_made, 1)

            def conv(i, last):
                act.wait_ge(y_made, AHEAD + 2 * i)
                act.wait_ge(evacuated, PAIRS * i + 6)
                for m in CONV_ORDER:
                    act.activation(cx[:, m, :, :], cin[:, m, :, 0:P], ACT.Identity, bias=col(C_CB + m),
                                   scale=col(C_CW + 4 * m)).then_inc(tap_first, 1)
                for n, m in enumerate(CONV_ORDER):
                    act.wait_ge(tap_made, 30 * i + 20 + n + 1)
                    act.activation(cx[:, m, :, :], cx[:, m, :, :], ACT.Silu).then_inc(conv_made, 1)
                if not last:
                    act.activation(cin[:, :, :, 0:TAPS - 1], cin[:, :, :, P:], ACT.Copy).then_inc(halo_kept, 1)

            def keep_tok(i, b):
                act.wait_ge(tok_turned, 2 * i + b + 1)
                act.activation(tok[:, b, :], ps_tok[:, 0:3 * P], ACT.Copy).then_inc(tok_kept, 1)

            def keep_whole(i):
                act.wait_ge(whole_made, i + 1)
                act.wait_ge(state_faded, AHEAD + 2 * i)
                act.activation(whole[:], ps_tok[:, 3 * P:].rearrange("p (b h) -> p b h", b=BATCH),
                               ACT.Copy).then_inc(whole_kept, 1)

            def gate_hi(i, b):
                c = 2 * i + b
                act.wait_ge(gate_made, c + 1)
                act.wait_ge(out_made, AHEAD + c)
                act.activation(g_hi[:], gated[:], ACT.Copy).then_inc(g_hi_made, 1)
                act.wait_ge(g_split, c + 1)
                act.activation(gated[:], gated[:], ACT.Square).then_inc(squared, 1)

            def scale_out(i, b):
                c = 2 * i + b
                act.wait_ge(ss_made, AHEAD + c + 1)
                act.wait_ge(rs_made, AHEAD + c)
                act.activation(gvar[:, b:b + 1], ps_tok[:, b:b + 1], ACT.Copy, scale=1.0 / D_SSM).then_inc(gvar_made, 1)
                act.wait_ge(out_made, AHEAD + c + 1)
                act.wait_ge(rs_made, AHEAD + c + 1)
                act.wait_ge(x1_made, AHEAD + c)
                act.activation(osc[:], ps_out[:], ACT.Copy, scale=rs[:, b:b + 1]).then_inc(out_scaled, 1)

            def store_x1(i, b):
                act.wait_ge(x1_made, AHEAD + 2 * i + b + 1)
                act.dma_start(x1_by_block[bass.ds(i, 1), :, b, :].rearrange("a p h -> (a p) h"),
                              xres[:, b, :]).then_inc(x1_out, 16)

            def body(i, last):
                conv(i, last)
                keep_tok(i, 0)
                keep_tok(i, 1)
                if not last:
                    norm_hi(i + 1, 0)
                    norm_hi(i + 1, 1)
                keep_whole(i)
                if not last:
                    for e in range(4):
                        evacuate(i + 1, e)
                    make_decay(i + 1)
                    for e in range(4, 6):
                        evacuate(i + 1, e)
                gate_hi(i, 0)
                scale_out(i, 0)
                gate_hi(i, 1)
                store_x1(i, 0)
                if not last:
                    evacuate(i + 1, 6)
                    evacuate(i + 1, 7)
                scale_out(i, 1)
                if not last:
                    evacuate(i + 1, 8)
                    evacuate(i + 1, 9)
                store_x1(i, 1)

            weight_hi(0)
            weight_hi(1)
            norm_hi(0, 0)
            norm_hi(0, 1)
            for e in range(PAIRS):
                weight_hi(e + 2)
                if e == 1:
                    act.wait_ge(zeroed, 4)
                evacuate(0, e)
                if e == 5:
                    act.wait_ge(a_negated, 1)
                    make_decay(0)
            for n in range(PAIRS + 2, len(pieces)):
                weight_hi(n)
            with act.Fori(0, BLOCKS - 1) as i:
                body(i, False)
            body(BLOCKS - 1, True)
            act.wait_ge(x1_out, AHEAD + 32 * BLOCKS)

        @block.vector
        def _(dve):
            def weight_lo(n):
                dve.wait_ge(hi_made, n + 1)
                if pieces[n][0] != "out":
                    dve.tensor_tensor(in_dest(win_lo, n), staging(n), in_dest(win_hi, n), ALU.subtract).then_inc(lo_made, 1)
                    return
                for half in range(2):
                    k = 2 * pieces[n][1] + half
                    made = dve.scalar_tensor_tensor(wout_lo[:, k, :], staging(n)[:, half, :], col(C_NW + k),
                                                    wout_hi[:, k, :], ALU.mult, ALU.subtract)
                made.then_inc(lo_made, 1)

            def norm_stats(j):
                dve.wait_ge(x_in, 16 * j + 16)
                for b in range(BATCH):
                    dve.bn_stats(stats[:, b, :], xin[:, b, :]).then_inc(stats_made, 1)
                dve.wait_ge(stats_made, 2 * j + 2)
                dve.sem_inc(stats_seen, 1)
                for b in range(BATCH):
                    dve.bn_aggr(moments[:, b, :], stats[:, b, :]).then_inc(moments_made, 1)

            def normalise(j):
                dve.wait_ge(rstd_made, j + 1)
                for b in range(BATCH):
                    dve.tensor_scalar(xin[:, b, :], xin[:, b, :], moments[:, b, 0:1], rstd[:, b:b + 1],
                                      ALU.subtract, ALU.mult).then_inc(xn_made, 1)

            def norm_lo(j, b):
                dve.wait_ge(xn_hi_made, 2 * j + b + 1)
                t = slice(b * P, (b + 1) * P)
                dve.tensor_tensor(xn_lo[:, :, t], ps_proj[b][:].rearrange("p (k t) -> p k t", k=KT), xn_hi[:, :, t],
                                  ALU.subtract).then_inc(xn_split, 1)

            def run_decay(j):
                dve.wait_ge(decay_cut, 2 * j + 2)
                h = slice(HEADS, P)
                dve.tensor_tensor_scan(dt_run[h, :], decay[h, :], first[h, :], 0.0, ALU.mult, ALU.add).then_inc(run_made, 1)

            def conv(i):
                for k in range(1, TAPS):
                    for n, m in enumerate(CONV_ORDER):
                        if k == 1:
                            dve.wait_ge(tap_first, CT * i + n + 1)
                        else:
                            dve.wait_ge(tap_made, 30 * i + CT * (k - 2) + n + 1)
                        dve.scalar_tensor_tensor(cx[:, m, :, :], cin[:, m, :, k:k + P], col(C_CW + 4 * m + k),
                                                 cx[:, m, :, :], ALU.mult, ALU.add).then_inc(tap_made, 1)

            by_pair = xpad[:].rearrange("p (q o) d -> p q (o d)", o=2)
            PAIR = HEADS // 2

            def xpad_half(odd):
                at = odd * 3 * HEAD
                return by_pair[:, :, at:at + HEAD]

            def pick(by_head, odd):
                v = by_head.rearrange("p (q o) -> p q o", o=2)[:, :, odd:odd + 1]
                return v.to_broadcast([P, PAIR, HEAD])

            def by_head_half(t, odd):
                return t.rearrange("p (q o d) -> p q o d", o=2, d=HEAD)[:, :, odd, :]

            def make_xpad(i, b):
                c = 2 * i + b
                dve.wait_ge(x_turned, c + 1)
                dve.wait_ge(tok_kept, c + 1)
                dve.wait_ge(ring_free, RING + GROUPS * c)
                for odd in range(2):
                    dve.tensor_tensor(xpad_half(odd), by_head_half(ps_x[:], odd), pick(tok[:, b, P:P + HEADS], odd),
                                      ALU.mult).then_inc(xpad_made, 1)

            def scale_carry(i, b):
                c = 2 * i + b
                dve.wait_ge(carry_made, c + 1)
                v = "p (h d) -> p h d"
                run = tok[:, b, P + HEADS:2 * P].unsqueeze(2).to_broadcast([P, HEADS, HEAD])
                dve.tensor_tensor(rows[:].rearrange(v, d=HEAD), ps_x[:].rearrange(v, d=HEAD), run,
                                  ALU.mult).then_inc(carry_scaled, 1)

            def scan(i, n):
                dve.wait_ge(ring_in[n % RING], 16 * (SLOT_USES * i + n // RING + 1))
                slot = ring[:, n % RING, :, :].rearrange(flat)
                dve.tensor_tensor_scan(slot, slot, eye[:].rearrange(flat), 0.0, ALU.mult, ALU.add).then_inc(scanned, 1)

            def mix(i, n):
                b, g = n // GROUPS, n % GROUPS
                slot = ring[:, n % RING, :, :]
                dve.wait_ge(scanned, 2 * GROUPS * i + n + 1)
                dve.tensor_copy(to_end[:, g * GH:(g + 1) * GH], slot[:, :, P - 1]).then_inc(end_kept, 1)
                dve.wait_ge(end_kept, 2 * GROUPS * i + n + 1)
                dve.tensor_tensor(slot, slot, tok[:, b, 2 * P:].unsqueeze(1).to_broadcast([P, GH, P]),
                                  ALU.mult).then_inc(mixed, 1)

            def make_xw(i, b):
                c = 2 * i + b
                dve.wait_ge(end_kept, GROUPS * (c + 1))
                dve.wait_ge(carry_added, c + 1)
                for odd in range(2):
                    dve.tensor_tensor(by_head_half(rows[:], odd), xpad_half(odd), pick(to_end[:], odd),
                                      ALU.mult).then_inc(xw_made, 1)

            def update_state(i, b):
                c = 2 * i + b
                dve.wait_ge(update_made, c + 1)
                dve.wait_ge(state_faded, AHEAD + c + 1)
                dve.tensor_tensor(state[:, b, :], state[:, b, :], ps_x[:], ALU.add).then_inc(state_made, 1)

            def make_y(i, b):
                c = 2 * i + b
                dve.wait_ge(ring_free, RING + GROUPS * c + GROUPS)
                dve.wait_ge(ss_made, AHEAD + c)
                for m in range(ZT):
                    made = dve.scalar_tensor_tensor(gated[:, m, :], cx[:, m, b, :], col(C_D + m),
                                                    ps_y[:, m * P:(m + 1) * P], ALU.mult, ALU.add)
                made.then_inc(y_made, 1)

            def gate(i, b):
                c = 2 * i + b
                dve.wait_ge(y_made, AHEAD + c + 1)
                dve.wait_ge(evacuated, PAIRS * i + PAIRS)
                dve.tensor_tensor(gated[:], gated[:], sz[:, :, b, :], ALU.mult).then_inc(gate_made, 1)

            def gate_lo(i, b):
                c = 2 * i + b
                dve.wait_ge(g_hi_made, c + 1)
                dve.tensor_tensor(g_lo[:], gated[:], g_hi[:], ALU.subtract).then_inc(g_split, 1)

            def body(i, last):
                if not last:
                    norm_stats(i + 1)
                conv(i)
                if not last:
                    normalise(i + 1)
                make_xpad(i, 0)
                scan(i, 0)
                scan(i, 1)
                scale_carry(i, 0)
                if not last:
                    norm_lo(i + 1, 0)
                    norm_lo(i + 1, 1)
                for g in range(GROUPS):
                    mix(i, g)
                    if g + 2 < GROUPS:
                        scan(i, g + 2)
                make_xw(i, 0)
                scan(i, GROUPS)
                scan(i, GROUPS + 1)
                update_state(i, 0)
                make_xpad(i, 1)
                make_y(i, 0)
                gate(i, 0)
                scale_carry(i, 1)
                gate_lo(i, 0)
                for g in range(GROUPS):
                    mix(i, GROUPS + g)
                    if g + 2 < GROUPS:
                        scan(i, GROUPS + g + 2)
                    if g == 0 and not last:
                        run_decay(i + 1)
                make_xw(i, 1)
                make_y(i, 1)
                gate(i, 1)
                update_state(i, 1)
                gate_lo(i, 1)

            for free in (y_made, state_made):
                dve.sem_inc(free, AHEAD)
            norm_stats(0)
            normalise(0)
            weight_lo(0)
            weight_lo(1)
            norm_lo(0, 0)
            norm_lo(0, 1)
            for n in range(2, len(pieces)):
                weight_lo(n)
            dve.wait_ge(filled, 2)
            run_decay(0)
            with dve.Fori(0, BLOCKS - 1) as i:
                body(i, False)
            body(BLOCKS - 1, True)

        @block.tensor
        def _(pe):
            def turn_xn(j, b):
                pe.wait_ge(xn_made, 2 * j + b + 1)
                if not (isinstance(j, int) and j == 0):
                    pe.wait_ge(evacuated, PAIRS * j - 1 + b)
                for k in range(KT):
                    made = pe.transpose(ps_proj[b][:, k * P:(k + 1) * P], xin[:, b, k * P:(k + 1) * P], eye1)
                made.then_inc(xn_turned, 1)

            def project(j, e):
                if e < 2:
                    pe.wait_ge(xn_split, 2 * j + 2)
                else:
                    pe.wait_ge(evacuated, PAIRS * j + e - 1)
                for half, m in enumerate(event_tiles(e)):
                    out = ps_proj[e % 2][:, half * TOK:(half + 1) * TOK]
                    cols = slice(m * P, (m + 1) * P)
                    for k in range(KT):
                        pe.matmul(out, win_hi[:, k, cols], xn_hi[:, k, :], start=(k == 0), stop=False)
                        pe.matmul(out, win_hi[:, k, cols], xn_lo[:, k, :], start=False, stop=False)
                        made = pe.matmul(out, win_lo[:, k, cols], xn_hi[:, k, :], start=False, stop=(k == KT - 1))
                made.then_inc(projected, 1)

            def turn_tok(i, b):
                pe.wait_ge(conv_made, CT * i + 2)
                pe.wait_ge(run_made, i + 1)
                if b == 0:
                    pe.wait_ge(gvar_made, AHEAD + 2 * i)
                else:
                    pe.wait_ge(tok_kept, 2 * i + 1)
                pe.transpose(ps_tok[:, 0:P], cx[:, ZT, b, :], eye1)
                pe.transpose(ps_tok[:, P:2 * P], dt_run[:, b * P:(b + 1) * P], eye1)
                pe.matmul(ps_tok[:, 2 * P:3 * P], cx[:, ZT, b, :], cx[:, ZT + 1, b, :], start=True, stop=True).then_inc(tok_turned, 1)

            def turn_x(i, b):
                pe.wait_ge(conv_made, CT * i + CT)
                pe.wait_ge(state_made, AHEAD + 2 * i + b)
                for m in range(ZT):
                    made = pe.transpose(ps_x[:, m * P:(m + 1) * P], cx[:, m, b, :], eye1)
                made.then_inc(x_turned, 1)

            def carry(i, b):
                pe.wait_ge(xpad_made, 2 * (2 * i + b) + 2)
                for h in range(2):
                    made = pe.matmul(ps_x[:, h * 512:(h + 1) * 512], cx[:, ZT + 1, b, :],
                                     state[:, b, h * 512:(h + 1) * 512], start=True, stop=True)
                made.then_inc(carry_made, 1)

            def whole_decay(i):
                pe.wait_ge(tok_kept, 2 * i + 2)
                for b in range(BATCH):
                    at = 3 * P + b * HEADS
                    made = pe.matmul(ps_tok[:, at:at + HEADS], last_row[:], tok[:, b, P + HEADS:2 * P], start=True, stop=True)
                made.then_inc(whole_made, 1)

            def add_carry(i, b):
                c = 2 * i + b
                pe.wait_ge(carry_scaled, c + 1)
                pe.wait_ge(y_made, AHEAD + c)
                for m in range(ZT):
                    made = pe.matmul(ps_y[:, m * P:(m + 1) * P], rows[:, m * P:(m + 1) * P], eye1,
                                     start=(m % 4 == 0), stop=False, skip_group_check=True)
                made.then_inc(carry_added, 1)

            def group(i, n):
                b, g = n // GROUPS, n % GROUPS
                pe.wait_ge(mixed, 2 * GROUPS * i + n + 1)
                for q in range(2):
                    for pair in range(GH // 2):
                        h = 2 * pair + q
                        made = pe.matmul(ps_y[32 * pair:32 * pair + 32, g * P:(g + 1) * P], xpad[:, g * GH + h, :],
                                         ring[:, n % RING, h, :], start=False, stop=(q == 1), skip_group_check=True)
                made.then_inc(ring_free, 1)

            def update(i, b):
                pe.wait_ge(xw_made, 2 * (2 * i + b) + 2)
                for h in range(2):
                    made = pe.matmul(ps_x[:, h * 512:(h + 1) * 512], tok[:, b, 0:P], rows[:, h * 512:(h + 1) * 512],
                                     start=True, stop=True)
                made.then_inc(update_made, 1)

            def project_out(i, b):
                c = 2 * i + b
                pe.wait_ge(g_split, c + 1)
                pe.wait_ge(out_scaled, AHEAD + c)
                for k in range(ZT):
                    pe.matmul(ps_out[:], g_hi[:, k, :], wout_hi[:, k, :], start=(k == 0), stop=False)
                    pe.matmul(ps_out[:], g_hi[:, k, :], wout_lo[:, k, :], start=False, stop=False)
                    made = pe.matmul(ps_out[:], g_lo[:, k, :], wout_hi[:, k, :], start=False, stop=(k == ZT - 1))
                made.then_inc(out_made, 1)

            def sum_squares(i, b):
                pe.wait_ge(sq_summed, 2 * i + b + 1)
                pe.wait_ge(whole_kept, i + 1)
                pe.matmul(ps_tok[:, b:b + 1], gated[:, 0, :], ones[:], start=True, stop=True).then_inc(ss_made, 1)

            def body(i, last):
                turn_tok(i, 0)
                turn_x(i, 0)
                turn_tok(i, 1)
                if not last:
                    turn_xn(i + 1, 0)
                    turn_xn(i + 1, 1)
                carry(i, 0)
                whole_decay(i)
                add_carry(i, 0)
                for g in range(GROUPS):
                    group(i, g)
                    if not last and g < 6:
                        project(i + 1, g)
                update(i, 0)
                turn_x(i, 1)
                carry(i, 1)
                add_carry(i, 1)
                for g in range(GROUPS):
                    group(i, GROUPS + g)
                    if g == 2:
                        project_out(i, 0)
                        sum_squares(i, 0)
                update(i, 1)
                if not last:
                    project(i + 1, 6)
                    project(i + 1, 7)
                project_out(i, 1)
                sum_squares(i, 1)
                if not last:
                    project(i + 1, 8)
                    project(i + 1, 9)

            for free in (out_made, ss_made):
                pe.sem_inc(free, AHEAD)
            pe.wait_ge(filled, 2)
            turn_xn(0, 0)
            turn_xn(0, 1)
            for e in range(PAIRS):
                pe.wait_ge(lo_made, EVENT_PIECE[e] + 1)
                project(0, e)
            with pe.Fori(0, BLOCKS - 1) as i:
                body(i, False)
            body(BLOCKS - 1, True)


def mlp_phase(nc, x1_dram, gate_w, up_w, down_w, packed, down_s, out):
    with ExitStack() as ctx:
        def sb(name, shape, dt=F32):
            return ctx.enter_context(nc.sbuf_tensor(name, shape, dt))

        def sem(name):
            return ctx.enter_context(nc.semaphore(name))

        up = {"gate": (sb("wg_hi", [P, KT, INTER], F32R), sb("wg_lo", [P, KT, INTER], F32R)),
              "up": (sb("wu_hi", [P, KT, INTER], F32R), sb("wu_lo", [P, KT, INTER], F32R))}
        wd_hi, wd_lo = sb("wd_hi", [P, MT, HID], F32R), sb("wd_lo", [P, MT, HID], F32R)
        h_hi, h_lo = sb("h_hi", [P, MT, BT], F32R), sb("h_lo", [P, MT, BT], F32R)
        xn_hi, xn_lo = sb("x1n_hi", [P, KT, BT], F32R), sb("x1n_lo", [P, KT, BT], F32R)
        xin = sb("x1_in_sb", [P, TT, HID])
        res = sb("res", [P, 2, HID])
        silu_g, hidden = sb("silu_g", [P, 2, BT]), sb("hidden", [P, 2, BT])
        raw = sb("raw", [P, 2, BT])
        scale_d = sb("scale_d", [P, HID])
        scales = sb("scales", [P, 2 * MT])
        eye = sb("eye2", [P, P])
        minus_half, eps = sb("minus_half2", [P, TT]), sb("eps2", [P, TT])
        stats, moments = sb("stats2", [P, TT, 6]), sb("moments2", [P, TT, 2])
        spread, rstd = sb("spread2", [P, TT]), sb("rstd2", [P, TT])
        pb = [ctx.enter_context(nc.psum_tensor(f"pb{n}", [P, BT], F32)) for n in range(8)]
        ps_g, ps_u, ps_t, ps_o = pb[0:2], pb[2:4], pb[4:6], pb[6:8]

        raw_in = [sem("raw_in0"), sem("raw_in1")]
        hi_made, lo_made = sem("whi_made"), sem("wlo_made")
        scales_in, x_in, res_in, stored = sem("scales_in"), sem("x1_in"), [sem("res_in0"), sem("res_in1")], [sem("stored0"), sem("stored1")]
        zeroed, filled = sem("zeroed2"), sem("filled2")
        stats_made, stats_seen, moments_made, eps_added, rstd_made = sem("stats2_made"), sem("stats2_seen"), sem("moments2_made"), sem("eps2_added"), sem("rstd2_made")
        xn_made, turned, xhi_made, split = sem("x1n_made"), sem("x1n_turned"), sem("x1n_hi_made"), sem("x1n_split")
        gu_made, silu_made, hidden_made, hhi_made, h_split = sem("gu_made"), sem("silu_made"), sem("hidden_made"), sem("hhi_made"), sem("h_split")
        down_made, down_scaled, out_ready = sem("down_made"), sem("down_scaled"), sem("out_ready")

        tokens = x1_dram.rearrange("b l h -> (b l) h")
        x_by_block = tokens.rearrange("(j t p) h -> j p t h", t=TT, p=P)
        out_by_block = out.rearrange("b l h -> (b l) h").rearrange("(j t p) h -> j p t h", t=TT, p=P)
        gate_t, up_t = gate_w.rearrange("(k p) n -> p k n", p=P), up_w.rearrange("(k p) n -> p k n", p=P)
        down_t = down_w.rearrange("(m p) n -> p m n", p=P)
        pieces = [(kind, m) for m in range(MT) for kind in ("gate", "up")] + [("down", m) for m in range(MT)]

        def piece(n, part):
            kind, m = pieces[n]
            r = raw[:, n % 2, :]
            if kind == "down":
                return (wd_hi, wd_lo)[part][:, m, :], r
            return up[kind][part][:, :, m * P:(m + 1) * P], r.rearrange("p (k n) -> p k n", k=KT)

        def t_cols(t):
            return slice(t * P, (t + 1) * P)

        block = ctx.enter_context(nc.Block())

        @block.sync
        def _(sp):
            def load_x(j):
                sp.dma_start(xin[:], x_by_block[bass.ds(j, 1)].rearrange("a p t h -> (a p) t h")).then_inc(x_in, 16)

            for free in stored:
                sp.sem_inc(free, AHEAD)
            load_x(0)
            sp.dma_start(scales[:], packed).then_inc(scales_in, 16)
            sp.dma_start(scale_d[:], down_s.to_broadcast([P, HID])).then_inc(scales_in, 16)
            for n, (kind, m) in enumerate(pieces):
                if n >= 2:
                    sp.wait_ge(lo_made, n - 1)
                src = down_t[:, m, :] if kind == "down" else (gate_t if kind == "gate" else up_t)[:, :, m * P:(m + 1) * P]
                sp.dma_start(piece(n, 0)[1], src).then_inc(raw_in[n % 2], 16)

            def body(j, last):
                for t in range(TT):
                    if t == 1 and not last:
                        sp.wait_ge(turned, TT * j + TT)
                        load_x(j + 1)
                    sp.wait_ge(stored[t % 2], AHEAD + 16 * (2 * j + t // 2))
                    sp.dma_start(res[:, t % 2, :], x_by_block[bass.ds(j, 1), :, t, :].rearrange("a p h -> (a p) h")).then_inc(res_in[t % 2], 16)
                    if t >= 1:
                        store(j, t - 1)
                store(j, TT - 1)

            def store(j, t):
                sp.wait_ge(out_ready, AHEAD + TT * j + t + 1)
                sp.dma_start(out_by_block[bass.ds(j, 1), :, t, :].rearrange("a p h -> (a p) h"), res[:, t % 2, :]).then_inc(stored[t % 2], 16)

            with sp.Fori(0, NB - 1) as j:
                body(j, False)
            body(NB - 1, True)
            for n in range(2):
                sp.wait_ge(stored[n], AHEAD + 16 * 2 * NB)

        @block.gpsimd
        def _(pool):
            pool.sem_inc(out_ready, AHEAD)
            pool.memset(minus_half[:], -0.5).then_inc(zeroed, 1)
            pool.memset(eps[:], EPS).then_inc(zeroed, 1)
            pool.memset(eye[:], 0.0).then_inc(zeroed, 1)
            pool.wait_ge(zeroed, 3)
            pool.affine_select(out=eye[:], in_=eye[:], compare_op=ALU.not_equal, fill=1.0, base=0,
                               pattern=[[-1, P]], channel_multiplier=1).then_inc(filled, 1)

            def norm_scale(j):
                pool.wait_ge(moments_made, TT * j + TT)
                pool.tensor_tensor(spread[:], moments[:, :, 1], eps[:], ALU.add).then_inc(eps_added, 1)
                pool.wait_ge(eps_added, j + 1)
                pool.tensor_tensor(rstd[:], spread[:], minus_half[:], ALU.pow).then_inc(rstd_made, 1)

            def body(j, last):
                if not last:
                    norm_scale(j + 1)
                for t in range(TT):
                    pool.wait_ge(down_scaled, AHEAD + TT * j + t + 1)
                    pool.wait_ge(res_in[t % 2], 16 * (2 * j + t // 2 + 1))
                    pool.tensor_tensor(res[:, t % 2, :], res[:, t % 2, :], hidden[:, t % 2, :], ALU.add).then_inc(out_ready, 1)

            norm_scale(0)
            for n in range(len(pieces)):
                pool.wait_ge(raw_in[n % 2], 16 * (n // 2 + 1))
                hi, r = piece(n, 0)
                pool.tensor_copy(hi, r).then_inc(hi_made, 1)
                pool.wait_ge(hi_made, n + 1)
                pool.tensor_tensor(piece(n, 1)[0], r, hi, ALU.subtract).then_inc(lo_made, 1)
            with pool.Fori(0, NB - 1) as j:
                body(j, False)
            body(NB - 1, True)

        @block.scalar
        def _(act):
            def norm_hi(j, t):
                act.wait_ge(turned, TT * j + t + 1)
                act.activation(xn_hi[:, :, t_cols(t)], ps_t[t % 2][:].rearrange("p (k t) -> p k t", k=KT), ACT.Copy).then_inc(xhi_made, 1)

            def body(j, last):
                for m in range(MT):
                    n = MT * j + m
                    act.wait_ge(gu_made, n + 1)
                    if m >= 2:
                        act.wait_ge(hidden_made, AHEAD + n - 1)
                    else:
                        act.wait_ge(hidden_made, AHEAD + MT * j)
                    act.activation(silu_g[:, m % 2, :], ps_g[m % 2][:], ACT.Silu, scale=scales[:, m:m + 1]).then_inc(silu_made, 1)
                    act.wait_ge(hidden_made, AHEAD + n + 1)
                    act.activation(h_hi[:, m, :], hidden[:, m % 2, :], ACT.Copy).then_inc(hhi_made, 1)
                if not last:
                    for t in range(TT):
                        norm_hi(j + 1, t)

            act.wait_ge(scales_in, 32)
            for t in range(TT):
                norm_hi(0, t)
            with act.Fori(0, NB - 1) as j:
                body(j, False)
            body(NB - 1, True)

        @block.vector
        def _(dve):
            def norm(j):
                dve.wait_ge(x_in, 16 * j + 16)
                for t in range(TT):
                    dve.bn_stats(stats[:, t, :], xin[:, t, :]).then_inc(stats_made, 1)
                dve.wait_ge(stats_made, TT * j + TT)
                dve.sem_inc(stats_seen, 1)
                for t in range(TT):
                    dve.bn_aggr(moments[:, t, :], stats[:, t, :]).then_inc(moments_made, 1)

            def normalise(j):
                dve.wait_ge(rstd_made, j + 1)
                for t in range(TT):
                    dve.tensor_scalar(xin[:, t, :], xin[:, t, :], moments[:, t, 0:1], rstd[:, t:t + 1],
                                      ALU.subtract, ALU.mult).then_inc(xn_made, 1)

            def norm_lo(j, t):
                dve.wait_ge(xhi_made, TT * j + t + 1)
                dve.tensor_tensor(xn_lo[:, :, t_cols(t)], ps_t[t % 2][:].rearrange("p (k t) -> p k t", k=KT),
                                  xn_hi[:, :, t_cols(t)], ALU.subtract).then_inc(split, 1)

            def scale_down(j, t):
                dve.wait_ge(down_made, TT * j + t + 1)
                if t >= 2:
                    dve.wait_ge(out_ready, AHEAD + TT * j + t - 1)
                dve.tensor_tensor(hidden[:, t % 2, :], ps_o[t % 2][:], scale_d[:], ALU.mult).then_inc(down_scaled, 1)

            def body(j, last):
                for m in range(MT):
                    n = MT * j + m
                    dve.wait_ge(silu_made, n + 1)
                    if m >= 2:
                        dve.wait_ge(h_split, n - 1)
                    else:
                        dve.wait_ge(out_ready, AHEAD + TT * j)
                    dve.scalar_tensor_tensor(hidden[:, m % 2, :], ps_u[m % 2][:], scales[:, MT + m:MT + m + 1],
                                             silu_g[:, m % 2, :], ALU.mult, ALU.mult).then_inc(hidden_made, 1)
                    dve.wait_ge(hhi_made, n + 1)
                    dve.tensor_tensor(h_lo[:, m, :], hidden[:, m % 2, :], h_hi[:, m, :], ALU.subtract).then_inc(h_split, 1)
                    if m == 2 and not last:
                        norm(j + 1)
                    if m == 5 and not last:
                        normalise(j + 1)
                dve.wait_ge(h_split, MT * j + MT)
                scale_down(j, 0)
                scale_down(j, 1)
                if not last:
                    for t in range(TT):
                        norm_lo(j + 1, t)
                scale_down(j, 2)
                scale_down(j, 3)

            for free in (hidden_made, down_scaled):
                dve.sem_inc(free, AHEAD)
            norm(0)
            normalise(0)
            for t in range(TT):
                norm_lo(0, t)
            with dve.Fori(0, NB - 1) as j:
                body(j, False)
            body(NB - 1, True)

        @block.tensor
        def _(pe):
            def turn(j, t):
                pe.wait_ge(xn_made, TT * j + t + 1)
                if t >= 2:
                    pe.wait_ge(split, TT * j + t - 1)
                for k in range(KT):
                    made = pe.transpose(ps_t[t % 2][:, k * P:(k + 1) * P], xin[:, t, k * P:(k + 1) * P], eye[:])
                made.then_inc(turned, 1)

            def product(out_ps, w, cols):
                hi, lo = w
                for k in range(KT):
                    pe.matmul(out_ps, hi[:, k, cols], xn_hi[:, k, :], start=(k == 0), stop=False)
                    pe.matmul(out_ps, hi[:, k, cols], xn_lo[:, k, :], start=False, stop=False)
                    made = pe.matmul(out_ps, lo[:, k, cols], xn_hi[:, k, :], start=False, stop=(k == KT - 1))
                return made

            def down(j, t):
                if t >= 2:
                    pe.wait_ge(down_scaled, AHEAD + TT * j + t - 1)
                else:
                    pe.wait_ge(down_scaled, AHEAD + TT * j)
                for m in range(MT):
                    pe.matmul(ps_o[t % 2][:], h_hi[:, m, t_cols(t)], wd_hi[:, m, :], start=(m == 0), stop=False)
                    pe.matmul(ps_o[t % 2][:], h_hi[:, m, t_cols(t)], wd_lo[:, m, :], start=False, stop=False)
                    made = pe.matmul(ps_o[t % 2][:], h_lo[:, m, t_cols(t)], wd_hi[:, m, :], start=False, stop=(m == MT - 1))
                made.then_inc(down_made, 1)

            def body(j, last):
                pe.wait_ge(split, TT * j + TT)
                for m in range(MT):
                    n = MT * j + m
                    pe.wait_ge(lo_made, 2 * m + 2)
                    if m >= 2:
                        pe.wait_ge(hidden_made, AHEAD + n - 1)
                    else:
                        pe.wait_ge(hidden_made, AHEAD + MT * j)
                    product(ps_g[m % 2][:], up["gate"], slice(m * P, (m + 1) * P))
                    product(ps_u[m % 2][:], up["up"], slice(m * P, (m + 1) * P)).then_inc(gu_made, 1)
                pe.wait_ge(lo_made, len(pieces))
                pe.wait_ge(h_split, MT * j + MT)
                down(j, 0)
                down(j, 1)
                if not last:
                    for t in range(TT):
                        turn(j + 1, t)
                down(j, 2)
                down(j, 3)

            pe.wait_ge(filled, 1)
            for t in range(TT):
                turn(0, t)
            with pe.Fori(0, NB - 1) as j:
                body(j, False)
            body(NB - 1, True)


def kernel(**inputs):
    import concourse.bacc as bacc
    from concourse.bass_utils import run_bass_kernel_spmd

    a = {name: np.ascontiguousarray(v) for name, v in inputs.items()}
    A, M = "L0_attn_", "L0_ffn_"

    def by_tile(v, width=P):
        return v.reshape(-1, width).T

    mup = a[A + "mup_vector"]
    dt_at = 2 * D_SSM + 2 * STATE
    twice = lambda v: np.concatenate([v, v]).reshape(P, 1)
    mixer_consts = np.concatenate([
        by_tile(mup[:dt_at]), twice(mup[dt_at:]),
        a[A + "conv_w"].reshape(CT, P, TAPS).transpose(1, 0, 2).reshape(P, CT * TAPS),
        by_tile(a[A + "conv_b"]), by_tile(np.repeat(a[A + "D"], HEAD)), by_tile(a[A + "norm_w"]),
        twice(a[A + "dt_bias"]), twice(a[A + "A_log"])], axis=1)
    mlp_scales = np.concatenate([by_tile(a[M + "gate_s"]), by_tile(a[M + "up_s"])], axis=1)
    arrays = {
        "x": a[A + "hidden_states"], "w_in": a[A + "W_in"], "w_out": a[A + "W_out"], "mixer_consts": mixer_consts,
        "gate_w": a[M + "gate_w"].T, "up_w": a[M + "up_w"].T, "down_w": a[M + "down_w"].T,
        "mlp_scales": mlp_scales, "down_s": a[M + "down_s"].reshape(1, HID),
    }
    arrays = {name: np.ascontiguousarray(v) for name, v in arrays.items()}

    nc = bacc.Bacc("TRN2", target_bir_lowering=False, num_devices=1, dynamic_dma_scratch_size=2048)
    d = {name: nc.dram_tensor(name, v.shape, mybir.dt.from_np(v.dtype), kind="ExternalInput").ap() for name, v in arrays.items()}
    out = nc.dram_tensor("out", (BATCH, LEN, HID), F32, kind="ExternalOutput").ap()
    decay_dram = nc.dram_tensor("decay_dram", (BLOCKS, BATCH, HEADS, P), F32, kind="Internal").ap()
    x1_dram = nc.dram_tensor("x1_dram", (BATCH, LEN, HID), F32, kind="Internal").ap()
    mixer_phase(nc, d["x"], d["w_in"], d["w_out"], d["mixer_consts"], decay_dram, x1_dram)
    mlp_phase(nc, x1_dram, d["gate_w"], d["up_w"], d["down_w"], d["mlp_scales"], d["down_s"], out)
    r = run_bass_kernel_spmd(nc, [arrays], core_ids=[0])
    return r.results[0]["out"]
```

```python
import concourse.bass as bass
from concourse import mybir
from contextlib import ExitStack
import numpy as np

F32 = mybir.dt.float32
F32R = mybir.dt.float32r
ACT = mybir.ActivationFunctionType
ALU = mybir.AluOpType

P = 128
BATCH, LEN, HID = 2, 1024, 512
D_SSM, STATE, HEADS, TAPS = 1024, 128, 64, 4
HEAD = D_SSM // HEADS
INTER = 1408
EPS = 1e-5

BLOCKS = LEN // P
TOK = BATCH * P
KT = HID // P
ZT = D_SSM // P
CT = ZT + 2
PT = ZT + CT + 1
COLS = PT * P
GROUPS = 8
GH = HEADS // GROUPS
RING = 4
EVENTS = 10
PIECES = EVENTS + ZT // 2
DT_AT = 2 * D_SSM + 2 * STATE
AHEAD = 1
LOGN = 12

C_MUP, C_CW, C_CB, C_D, C_NW, C_DTB, C_ALOG = 0, PT, PT + 4 * CT, PT + 5 * CT, PT + 5 * CT + ZT, PT + 5 * CT + 2 * ZT, PT + 5 * CT + 2 * ZT + 1
C_N = C_ALOG + 1

MT = INTER // P
BT = 512
NB = BATCH * LEN // BT
TT = BT // P
RAW_SLOTS = 3


def log1p_coefficients():
    k = np.arange(LOGN)
    nodes = 0.5 + 0.5 * np.cos(np.pi * (2 * k + 1) / (2 * LOGN))
    cheb = np.polynomial.chebyshev.Chebyshev.fit(nodes, np.log1p(nodes) / nodes, LOGN - 1, domain=[0, 1])
    return [float(c) for c in cheb.convert(kind=np.polynomial.Polynomial, domain=[-1, 1], window=[-1, 1]).coef]


def mixer_phase(nc, x, w_in, w_out, packed, decay_dram, x1_dram):
    with ExitStack() as ctx:
        def sb(name, shape, dt=F32):
            return ctx.enter_context(nc.sbuf_tensor(name, shape, dt))

        def sem(name):
            return ctx.enter_context(nc.semaphore(name))

        win_hi, win_lo = sb("win_hi", [P, KT, COLS], F32R), sb("win_lo", [P, KT, COLS], F32R)
        wout_hi, wout_lo = sb("wout_hi", [P, ZT, HID], F32R), sb("wout_lo", [P, ZT, HID], F32R)
        ring = sb("ring", [P, RING, GH, P])
        eye = sb("eye", [P, GH, P])
        cin = sb("cin", [P, CT, BATCH, P + TAPS - 1])
        cx = sb("cx", [P, CT, BATCH, P])
        sz = sb("sz", [P, ZT, BATCH, P])
        xn_hi, xn_lo = sb("xn_hi", [P, KT, TOK], F32R), sb("xn_lo", [P, KT, TOK], F32R)
        xpad = sb("xpad", [P, HEADS, 2 * HEAD])
        rows = sb("rows", [P, D_SSM])
        state = sb("state", [P, BATCH, D_SSM])
        skip = sb("skip", [P, ZT, P])
        gated = sb("gated", [P, ZT, P])
        g_hi, g_lo = sb("g_hi", [P, ZT, P], F32R), sb("g_lo", [P, ZT, P], F32R)
        xin = sb("xin", [P, BATCH, HID])
        xres = sb("xres", [P, BATCH, HID])
        dt_v, dt_e, dt_p = sb("dt_v", [P, TOK]), sb("dt_e", [P, TOK]), sb("dt_p", [P, TOK])
        dt_run = sb("dt_run", [P, TOK])
        decay = sb("decay", [P, TOK])
        first_decay = sb("first_decay", [P, TOK])
        tok = sb("tok", [P, BATCH, 3 * P])
        to_end = sb("to_end", [P, HEADS])
        whole = sb("whole", [P, BATCH, HEADS])
        consts = sb("consts", [P, C_N])
        neg_a = sb("neg_a", [P, 1])
        stats, moments = sb("stats", [P, BATCH, 6]), sb("moments", [P, BATCH, 2])
        spread, rstd = sb("spread", [P, BATCH]), sb("rstd", [P, BATCH])
        gvar, rs = sb("gvar", [P, BATCH]), sb("rs", [P, BATCH])
        minus_half, eps = sb("minus_half", [P, BATCH]), sb("eps", [P, BATCH])
        ones = sb("ones", [P, 1])
        last_row = sb("last_row", [P, P])

        def pb(name, banks=1):
            return ctx.enter_context(nc.psum_tensor(name, [P, 512 * banks], F32))

        ps_proj = [pb("ps_proj0"), pb("ps_proj1")]
        ps_tok, ps_out = pb("ps_tok"), pb("ps_out")
        ps_x, ps_y = pb("ps_x", 2), pb("ps_y", 2)
        ps_whole, ps_ss = ps_tok[:, 3 * P:3 * P + HEADS], ps_tok[:, 3 * P + HEADS:3 * P + HEADS + 1]

        consts_in = sem("consts_in")
        raw_in = [sem(f"raw_in{n}") for n in range(PIECES)]
        hi_made, lo_made = sem("hi_made"), sem("lo_made")
        zeroed, filled = sem("zeroed"), sem("filled")
        a_made, a_negated = sem("a_made"), sem("a_negated")
        x_in, xres_in = sem("x_in"), [sem(f"xres_in{b}") for b in range(BATCH)]
        ring_in = [sem(f"ring_in{n}") for n in range(RING)]
        decay_out, x1_out = sem("decay_out"), [sem(f"x1_out{b}") for b in range(BATCH)]
        stats_made, stats_seen, moments_made, eps_added, rstd_made = (
            sem("stats_made"), sem("stats_seen"), sem("moments_made"), sem("eps_added"), sem("rstd_made"))
        xn_made, xn_turned, xn_hi_made, xn_split = sem("xn_made"), sem("xn_turned"), sem("xn_hi_made"), sem("xn_split")
        projected, evacuated = sem("projected"), sem("evacuated")
        dt_abs, dt_exp, soft_step, dt_made, decay_made, decay_cut, run_made = (
            sem("dt_abs"), sem("dt_exp"), sem("soft_step"), sem("dt_made"), sem("decay_made"), sem("decay_cut"), sem("run_made"))
        tap_first, tap_made, conv_made, halo_kept = sem("tap_first"), sem("tap_made"), sem("conv_made"), sem("halo_kept")
        tok_turned, x_turned, tok_kept, whole_made, whole_kept = (
            sem("tok_turned"), sem("x_turned"), sem("tok_kept"), sem("whole_made"), sem("whole_kept"))
        xpad_made, carry_made, carry_scaled, carry_added = sem("xpad_made"), sem("carry_made"), sem("carry_scaled"), sem("carry_added")
        scanned, end_kept, mixed, mixed_pool = sem("scanned"), sem("end_kept"), sem("mixed"), sem("mixed_pool")
        ring_free = sem("ring_free")
        xw_made, update_made, state_faded, state_made = sem("xw_made"), sem("update_made"), sem("state_faded"), sem("state_made")
        skip_made, y_made, gate_made, g_hi_made, g_split, squared, sq_step, sq_summed = (
            sem("skip_made"), sem("y_made"), sem("gate_made"), sem("g_hi_made"), sem("g_split"), sem("squared"),
            sem("sq_step"), sem("sq_summed"))
        ss_made, gvar_made, gvar_eps, rs_made, out_made, x1_made = (
            sem("ss_made"), sem("gvar_made"), sem("gvar_eps"), sem("rs_made"), sem("out_made"), sem("x1_made"))

        x_by_block = x.rearrange("b (i p) h -> i p b h", p=P)
        x1_by_block = x1_dram.rearrange("b (i p) h -> i p b h", p=P)
        w_in_t = w_in.rearrange("(k p) n -> p k n", p=P)
        w_out_t = w_out.rearrange("(k p) n -> p k n", p=P)
        log_c = log1p_coefficients()

        def event_tiles(e):
            if e == 0:
                return [PT - 1]
            if e == 1:
                return [2 * ZT, 2 * ZT + 1]
            if e < 6:
                return [ZT + 2 * (e - 2), ZT + 2 * (e - 2) + 1]
            return [2 * (e - 6), 2 * (e - 6) + 1]

        def by_k(t, k):
            return t.rearrange("p (k n) -> p k n", k=k)

        landing = [xres[:, 0, :], rows[:]] + [ring[:, n, :, :].rearrange("p g t -> p (g t)") for n in range(RING)]
        landing += [sz[:, n:n + 4, :, :].rearrange("p m b t -> p (m b t)") for n in (0, 4)]
        landing += [xpad[:, n:n + 32, :].rearrange("p h d -> p (h d)") for n in (0, 32)]
        landing += [state[:, b, :] for b in range(BATCH)] + [t[:].rearrange("p m t -> p (m t)") for t in (skip, gated)]
        LANDED_X = 6

        def piece(n):
            if n < EVENTS:
                tiles = event_tiles(n)
                cols = slice(tiles[0] * P, (tiles[-1] + 1) * P)
                return win_hi[:, :, cols], win_lo[:, :, cols], by_k(landing[n], KT)
            k = slice(2 * (n - EVENTS), 2 * (n - EVENTS) + 2)
            return wout_hi[:, k, :], wout_lo[:, k, :], by_k(landing[n], 2)

        CONV_ORDER = [ZT, ZT + 1] + list(range(ZT))
        CONV_RUNS = [CONV_ORDER[0:2], CONV_ORDER[2:6], CONV_ORDER[6:10]]
        TAP_AT = {mk: n for n, mk in enumerate((m, k) for run in CONV_RUNS for k in range(1, TAPS) for m in run)}
        N_TAPS = len(TAP_AT)

        eye1 = eye[:, 0, :]
        flat = "p g t -> p (g t)"
        SLOT_USES = GROUPS // RING
        POOL_MIXES = GROUPS - 1

        def col(at):
            return consts[:, at:at + 1]

        block = ctx.enter_context(nc.Block())

        @block.sync
        def _(sp):
            sp.dma_start(xin[:], x_by_block[0]).then_inc(x_in, 16)
            sp.dma_start(consts[:], packed).then_inc(consts_in, 16)
            for n in range(PIECES):
                raw = piece(n)[2]
                if n == 0:
                    for half in range(2):
                        sp.dma_start(raw[:, :, half * HEADS:(half + 1) * HEADS],
                                     w_in_t[:, :, DT_AT:DT_AT + HEADS]).then_inc(raw_in[n], 16)
                elif n < EVENTS:
                    at = event_tiles(n)[0] * P
                    sp.dma_start(raw, w_in_t[:, :, at:at + 2 * P]).then_inc(raw_in[n], 16)
                else:
                    k = 2 * (n - EVENTS)
                    sp.dma_start(raw, w_out_t[:, k:k + 2, :]).then_inc(raw_in[n], 16)

            def store_decay(j):
                sp.wait_ge(decay_cut, 2 * j + 2)
                for b in range(BATCH):
                    sp.dma_start(decay_dram[bass.ds(j, 1), b, :, :].rearrange("a h t -> (a h) t"),
                                 decay[0:HEADS, b * P:(b + 1) * P]).then_inc(decay_out, 16)

            def load_decays(i, b, g, opening=False):
                if not opening:
                    sp.wait_ge(ring_free, GROUPS * (2 * i + b) + g - RING + 1)
                src = decay_dram[bass.ds(i, 1), b, g * GH:(g + 1) * GH, :].rearrange("a h t -> a (h t)")
                sp.dma_start(ring[:, g % RING, :, :].rearrange(flat),
                             src.to_broadcast([P, GH * P])).then_inc(ring_in[g % RING], 16)

            def load_res(i, b, first):
                if not first:
                    sp.wait_ge(x1_out[b], 16 * i)
                sp.dma_start(xres[:, b, :], x_by_block[bass.ds(i, 1), :, b, :].rearrange("a p h -> (a p) h")).then_inc(xres_in[b], 16)

            def body(i, first, last):
                if not last:
                    sp.wait_ge(xn_turned, 2 * i + 2)
                    sp.dma_start(xin[:], x_by_block[bass.ds(i + 1, 1)].rearrange("a p b h -> (a p) b h")).then_inc(x_in, 16)
                for g in range(RING, GROUPS):
                    load_decays(i, 0, g)
                load_res(i, 0, first)
                for g in range(RING):
                    load_decays(i, 1, g)
                if not last:
                    store_decay(i + 1)
                for g in range(RING, GROUPS):
                    load_decays(i, 1, g)
                load_res(i, 1, first)
                if not last:
                    sp.wait_ge(decay_out, 32 * i + 64)
                    for g in range(RING):
                        load_decays(i + 1, 0, g)

            sp.wait_ge(lo_made, LANDED_X)
            store_decay(0)
            sp.wait_ge(decay_out, 32)
            for g in range(RING):
                load_decays(0, 0, g, opening=True)
            body(0, True, False)
            with sp.Fori(1, BLOCKS - 1) as i:
                body(i, False, False)
            body(BLOCKS - 1, False, True)

        @block.gpsimd
        def _(pool):
            pool.memset(minus_half[:], -0.5).then_inc(zeroed, 1)
            pool.memset(eye[:], 0.0).then_inc(zeroed, 1)
            pool.memset(last_row[:], 0.0).then_inc(zeroed, 1)
            pool.memset(cin[:, :, :, 0:TAPS - 1], 0.0).then_inc(zeroed, 1)
            pool.memset(first_decay[:], 0.0).then_inc(zeroed, 1)
            pool.memset(ones[:], 1.0).then_inc(zeroed, 1)
            pool.memset(eps[:], EPS).then_inc(zeroed, 1)
            pool.wait_ge(zeroed, 7)
            pool.affine_select(out=eye[:], in_=eye[:], compare_op=ALU.not_equal, fill=1.0, base=0,
                               pattern=[[0, GH], [-1, P]], channel_multiplier=1).then_inc(filled, 1)

            def norm_scale(j):
                pool.wait_ge(moments_made, 2 * j + 2)
                pool.tensor_tensor(spread[:], moments[:, :, 1], eps[:], ALU.add).then_inc(eps_added, 1)
                pool.wait_ge(eps_added, j + 1)
                pool.tensor_tensor(rstd[:], spread[:], minus_half[:], ALU.pow).then_inc(rstd_made, 1)

            norm_scale(0)
            pool.affine_select(out=last_row[:], in_=last_row[:], compare_op=ALU.not_equal, fill=1.0, base=1 - P,
                               pattern=[[0, P]], channel_multiplier=1).then_inc(filled, 1)
            pool.wait_ge(a_made, 1)
            pool.tensor_scalar(neg_a[:], neg_a[:], -1.0, None, ALU.mult).then_inc(a_negated, 1)
            pool.wait_ge(lo_made, PIECES)
            pool.memset(xpad[:], 0.0).then_inc(zeroed, 1)
            pool.memset(state[:], 0.0).then_inc(zeroed, 1)

            def mix(i, b, g):
                c = 2 * i + b
                slot = ring[:, g % RING, :, :]
                pool.wait_ge(end_kept, GROUPS * c + g + 1)
                pool.wait_ge(tok_kept, c + 1)
                pool.tensor_tensor(slot, slot, tok[:, b, 2 * P:].unsqueeze(1).to_broadcast([P, GH, P]),
                                   ALU.mult).then_inc(mixed_pool, 1)

            def fade_state(i, b):
                pool.wait_ge(whole_kept, 2 * i + b + 1)
                pool.wait_ge(carry_made, 2 * i + b + 1)
                s = state[:, b, :].rearrange("p (h d) -> p h d", h=HEADS)
                pool.tensor_tensor(s, s, whole[:, b, :].unsqueeze(2).to_broadcast([P, HEADS, HEAD]),
                                   ALU.mult).then_inc(state_faded, 1)

            def square_sum(c):
                pool.wait_ge(squared, c + 1)
                pool.tensor_tensor(gated[:, 0:4, :], gated[:, 0:4, :], gated[:, 4:8, :], ALU.add).then_inc(sq_step, 1)
                pool.wait_ge(sq_step, 2 * c + 1)
                pool.tensor_tensor(gated[:, 0:2, :], gated[:, 0:2, :], gated[:, 2:4, :], ALU.add).then_inc(sq_step, 1)
                pool.wait_ge(sq_step, 2 * c + 2)
                pool.tensor_tensor(gated[:, 0, :], gated[:, 0, :], gated[:, 1, :], ALU.add).then_inc(sq_summed, 1)

            def rms_scale(c, b):
                pool.wait_ge(gvar_made, c + 1)
                pool.tensor_tensor(gvar[:, b:b + 1], gvar[:, b:b + 1], eps[:, 0:1], ALU.add).then_inc(gvar_eps, 1)
                pool.wait_ge(gvar_eps, c + 1)
                pool.tensor_tensor(rs[:, b:b + 1], gvar[:, b:b + 1], minus_half[:, 0:1], ALU.pow).then_inc(rs_made, 1)

            def body(i, first, last):
                for b in range(BATCH):
                    prev = 2 * i + b - 1
                    opening = first and b == 0
                    for g in range(RING):
                        mix(i, b, g)
                        if g == 1 and b == 0 and not last:
                            norm_scale(i + 1)
                    if not last:
                        fade_state(i, b)
                    if not opening:
                        square_sum(prev)
                    for g in range(RING, POOL_MIXES):
                        mix(i, b, g)
                        if g == RING + 1 and not opening:
                            rms_scale(prev, 1 - b)

            body(0, True, False)
            with pool.Fori(1, BLOCKS - 1) as i:
                body(i, False, False)
            body(BLOCKS - 1, False, True)
            square_sum(2 * BLOCKS - 1)
            rms_scale(2 * BLOCKS - 1, 1)

        @block.scalar
        def _(act):
            act.wait_ge(consts_in, 16)
            act.activation(neg_a[:], col(C_ALOG), ACT.Exp).then_inc(a_made, 1)

            def weight_hi(n):
                act.wait_ge(raw_in[n], 32 if n == 0 else 16)
                hi, lo, raw = piece(n)
                if n < EVENTS:
                    act.activation(hi, raw, ACT.Copy).then_inc(hi_made, 1)
                    return
                for k in range(2):
                    made = act.activation(hi[:, k, :], raw[:, k, :], ACT.Copy, scale=col(C_NW + 2 * (n - EVENTS) + k))
                made.then_inc(hi_made, 1)

            def norm_hi(j, b):
                act.wait_ge(xn_turned, 2 * j + b + 1)
                act.activation(xn_hi[:, :, b * P:(b + 1) * P], ps_proj[b][:].rearrange("p (k t) -> p k t", k=KT),
                               ACT.Copy).then_inc(xn_hi_made, 1)

            def evacuate(j, e):
                act.wait_ge(projected, EVENTS * j + e + 1)
                if e == 0:
                    act.wait_ge(dt_made, j)
                    v = dict(bias=col(C_DTB), scale=col(C_MUP + PT - 1))
                    act.activation(dt_e[:], ps_proj[0][:, 0:TOK], ACT.Abs, **v).then_inc(dt_abs, 1)
                    act.activation(dt_v[:], ps_proj[0][:, 0:TOK], ACT.Relu, **v).then_inc(evacuated, 1)
                    act.wait_ge(dt_abs, j + 1)
                    act.activation(dt_e[:], dt_e[:], ACT.Exp, scale=-1.0).then_inc(dt_exp, 1)
                    return
                if e == 1:
                    act.wait_ge(halo_kept, j)
                if e == 6:
                    act.wait_ge(gate_made, 2 * j)
                for half, m in enumerate(event_tiles(e)):
                    src = ps_proj[e % 2][:, half * TOK:(half + 1) * TOK].rearrange("p (b t) -> p b t", b=BATCH)
                    if m < ZT:
                        made = act.activation(sz[:, m, :, :], src, ACT.Silu, scale=col(C_MUP + m))
                    else:
                        made = act.activation(cin[:, m - ZT, :, TAPS - 1:], src, ACT.Copy, scale=col(C_MUP + m))
                made.then_inc(evacuated, 1)

            def make_decay(j):
                act.wait_ge(dt_made, j + 1)
                act.wait_ge(decay_out, 32 * j)
                act.wait_ge(run_made, j)
                act.activation(decay[:], dt_run[:], ACT.Exp, scale=neg_a[:]).then_inc(decay_made, 1)

            def first_taps(j, run):
                for m in CONV_RUNS[run]:
                    if m >= ZT:
                        act.wait_ge(evacuated, EVENTS * j + 2)
                        act.wait_ge(tok_turned, 2 * j)
                        act.wait_ge(carry_made, 2 * j)
                    else:
                        act.wait_ge(evacuated, EVENTS * j + 3 + m // 2)
                        act.wait_ge(x_turned, 2 * j)
                        act.wait_ge(skip_made, 2 * j)
                    act.activation(cx[:, m, :, :], cin[:, m, :, 0:P], ACT.Identity, bias=col(C_CB + m),
                                   scale=col(C_CW + 4 * m)).then_inc(tap_first, 1)

            def conv_silu(j, run):
                for m in CONV_RUNS[run]:
                    act.wait_ge(tap_made, N_TAPS * j + TAP_AT[m, TAPS - 1] + 1)
                    act.activation(cx[:, m, :, :], cx[:, m, :, :], ACT.Silu).then_inc(conv_made, 1)

            def keep_halo(j):
                act.wait_ge(tap_made, N_TAPS * (j + 1))
                act.activation(cin[:, :, :, 0:TAPS - 1], cin[:, :, :, P:], ACT.Copy).then_inc(halo_kept, 1)

            def keep_tok(i, b):
                act.wait_ge(tok_turned, 2 * i + b + 1)
                act.activation(tok[:, b, :], ps_tok[:, 0:3 * P], ACT.Copy).then_inc(tok_kept, 1)

            def keep_whole(i, b, first):
                act.wait_ge(whole_made, 2 * i + b + 1)
                if not first:
                    act.wait_ge(state_faded, 2 * i + b - 1)
                act.activation(whole[:, b, :], ps_whole, ACT.Copy).then_inc(whole_kept, 1)

            def make_skip(i, b):
                act.wait_ge(conv_made, CT * (i + 1))
                act.wait_ge(y_made, 2 * i + b)
                for m in range(ZT):
                    made = act.activation(skip[:, m, :], cx[:, m, b, :], ACT.Copy, scale=col(C_D + m))
                made.then_inc(skip_made, 1)

            def gate_hi(c):
                act.wait_ge(gate_made, c + 1)
                act.wait_ge(out_made, c)
                act.activation(g_hi[:], gated[:], ACT.Copy).then_inc(g_hi_made, 1)

            def square(c):
                act.wait_ge(g_split, c + 1)
                act.activation(gated[:], gated[:], ACT.Square).then_inc(squared, 1)

            def mean_square(c, b):
                act.wait_ge(ss_made, c + 1)
                act.wait_ge(rs_made, c)
                act.activation(gvar[:, b:b + 1], ps_ss, ACT.Copy, scale=1.0 / D_SSM).then_inc(gvar_made, 1)

            def store_x1(i, b, c):
                act.wait_ge(x1_made, c + 1)
                act.dma_start(x1_by_block[bass.ds(i, 1), :, b, :].rearrange("a p h -> (a p) h"),
                              xres[:, b, :]).then_inc(x1_out[b], 16)

            def body(i, first, last):
                c = 2 * i
                keep_tok(i, 0)
                if not first:
                    gate_hi(c - 1)
                evacuate(i, 6)
                make_skip(i, 0)
                evacuate(i, 7)
                if not first:
                    square(c - 1)
                keep_whole(i, 0, first)
                evacuate(i, 8)
                evacuate(i, 9)
                if not first:
                    mean_square(c - 1, 1)
                if not last:
                    norm_hi(i + 1, 0)
                    norm_hi(i + 1, 1)
                    evacuate(i + 1, 0)
                    evacuate(i + 1, 1)
                if not first:
                    store_x1(i - 1, 1, c - 1)
                keep_tok(i, 1)
                gate_hi(c)
                if not last:
                    evacuate(i + 1, 2)
                make_skip(i, 1)
                if not last:
                    evacuate(i + 1, 3)
                square(c)
                keep_whole(i, 1, first)
                if not last:
                    make_decay(i + 1)
                    first_taps(i + 1, 0)
                    first_taps(i + 1, 1)
                    evacuate(i + 1, 4)
                    evacuate(i + 1, 5)
                    first_taps(i + 1, 2)
                mean_square(c, 0)
                if not last:
                    for run in range(3):
                        conv_silu(i + 1, run)
                    keep_halo(i + 1)
                store_x1(i, 0, c)

            for n in range(3):
                weight_hi(n)
            norm_hi(0, 0)
            norm_hi(0, 1)
            act.wait_ge(zeroed, 7)
            for e in range(6):
                evacuate(0, e)
                if e + 3 < 6:
                    weight_hi(e + 3)
            act.wait_ge(a_negated, 1)
            make_decay(0)
            for run in range(3):
                first_taps(0, run)
            for n in range(6, PIECES):
                weight_hi(n)
            for run in range(3):
                conv_silu(0, run)
            keep_halo(0)
            act.wait_ge(lo_made, PIECES)
            body(0, True, False)
            with act.Fori(1, BLOCKS - 1) as i:
                body(i, False, False)
            body(BLOCKS - 1, False, True)
            c = 2 * BLOCKS - 1
            gate_hi(c)
            square(c)
            mean_square(c, 1)
            store_x1(BLOCKS - 1, 1, c)
            for b in range(BATCH):
                act.wait_ge(x1_out[b], 16 * BLOCKS)

        @block.vector
        def _(dve):
            def weight_lo(n):
                dve.wait_ge(hi_made, n + 1)
                hi, lo, raw = piece(n)
                if n < EVENTS:
                    dve.tensor_tensor(lo, raw, hi, ALU.subtract).then_inc(lo_made, 1)
                    return
                for k in range(2):
                    made = dve.scalar_tensor_tensor(lo[:, k, :], raw[:, k, :], col(C_NW + 2 * (n - EVENTS) + k),
                                                    hi[:, k, :], ALU.mult, ALU.subtract)
                made.then_inc(lo_made, 1)

            def norm_stats(j):
                dve.wait_ge(x_in, 16 * j + 16)
                for b in range(BATCH):
                    dve.bn_stats(stats[:, b, :], xin[:, b, :]).then_inc(stats_made, 1)
                dve.wait_ge(stats_made, 2 * j + 2)
                dve.sem_inc(stats_seen, 1)
                for b in range(BATCH):
                    dve.bn_aggr(moments[:, b, :], stats[:, b, :]).then_inc(moments_made, 1)

            def normalise(j):
                dve.wait_ge(rstd_made, j + 1)
                for b in range(BATCH):
                    dve.tensor_scalar(xin[:, b, :], xin[:, b, :], moments[:, b, 0:1], rstd[:, b:b + 1],
                                      ALU.subtract, ALU.mult).then_inc(xn_made, 1)

            def norm_lo(j, b):
                dve.wait_ge(xn_hi_made, 2 * j + b + 1)
                t = slice(b * P, (b + 1) * P)
                dve.tensor_tensor(xn_lo[:, :, t], ps_proj[b][:].rearrange("p (k t) -> p k t", k=KT), xn_hi[:, :, t],
                                  ALU.subtract).then_inc(xn_split, 1)

            def softplus(j):
                dve.wait_ge(dt_exp, j + 1)
                dve.tensor_scalar(dt_p[:], dt_e[:], log_c[-1], None, ALU.mult).then_inc(soft_step, 1)
                for n, c in enumerate(reversed(log_c[:-1])):
                    dve.wait_ge(soft_step, LOGN * j + n + 1)
                    dve.scalar_tensor_tensor(dt_p[:], dt_p[:], c, dt_e[:], ALU.add, ALU.mult).then_inc(soft_step, 1)
                dve.wait_ge(soft_step, LOGN * (j + 1))
                dve.wait_ge(tok_turned, 2 * j)
                dve.tensor_tensor(dt_run[:], dt_v[:], dt_p[:], ALU.add).then_inc(dt_made, 1)

            def cut_decay(j):
                dve.wait_ge(decay_made, j + 1)
                starts = decay[:].rearrange("p (b t) -> p b t", b=BATCH)[:, :, 0:1]
                kept = first_decay[:].rearrange("p (b t) -> p b t", b=BATCH)[:, :, 0:1]
                dve.tensor_copy(kept, starts).then_inc(decay_cut, 1)
                dve.wait_ge(decay_cut, 2 * j + 1)
                dve.memset(starts, 0.0).then_inc(decay_cut, 1)
                dve.wait_ge(decay_cut, 2 * j + 2)
                h = slice(HEADS, P)
                dve.tensor_tensor_scan(dt_run[h, :], decay[h, :], first_decay[h, :], 0.0, ALU.mult, ALU.add).then_inc(run_made, 1)

            def conv_taps(j, run):
                for k in range(1, TAPS):
                    for m in CONV_RUNS[run]:
                        if k == 1:
                            dve.wait_ge(tap_first, CT * j + CONV_ORDER.index(m) + 1)
                        else:
                            dve.wait_ge(tap_made, N_TAPS * j + TAP_AT[m, k - 1] + 1)
                        dve.scalar_tensor_tensor(cx[:, m, :, :], cin[:, m, :, k:k + P], col(C_CW + 4 * m + k),
                                                 cx[:, m, :, :], ALU.mult, ALU.add).then_inc(tap_made, 1)

            by_pair = xpad[:].rearrange("p (q o) d -> p q (o d)", o=2)
            PAIR = HEADS // 2

            def xpad_half(odd):
                at = odd * 3 * HEAD
                return by_pair[:, :, at:at + HEAD]

            def pick(by_head, odd):
                v = by_head.rearrange("p (q o) -> p q o", o=2)[:, :, odd:odd + 1]
                return v.to_broadcast([P, PAIR, HEAD])

            def by_head_half(t, odd):
                return t.rearrange("p (q o d) -> p q o d", o=2, d=HEAD)[:, :, odd, :]

            def make_xpad(i, b):
                c = 2 * i + b
                dve.wait_ge(x_turned, c + 1)
                dve.wait_ge(tok_kept, c + 1)
                dve.wait_ge(ring_free, GROUPS * c)
                for odd in range(2):
                    dve.tensor_tensor(xpad_half(odd), by_head_half(ps_x[:], odd), pick(tok[:, b, P:P + HEADS], odd),
                                      ALU.mult).then_inc(xpad_made, 1)

            def scale_carry(i, b):
                dve.wait_ge(carry_made, 2 * i + b + 1)
                v = "p (h d) -> p h d"
                run = tok[:, b, P + HEADS:2 * P].unsqueeze(2).to_broadcast([P, HEADS, HEAD])
                dve.tensor_tensor(rows[:].rearrange(v, d=HEAD), ps_x[:].rearrange(v, d=HEAD), run,
                                  ALU.mult).then_inc(carry_scaled, 1)

            def scan(i, b, g):
                dve.wait_ge(ring_in[g % RING], 16 * (SLOT_USES * (2 * i + b) + g // RING + 1))
                slot = ring[:, g % RING, :, :].rearrange(flat)
                dve.tensor_tensor_scan(slot, slot, eye[:].rearrange(flat), 0.0, ALU.mult, ALU.add).then_inc(scanned, 1)

            def keep_end(i, b, g):
                dve.wait_ge(scanned, GROUPS * (2 * i + b) + g + 1)
                dve.tensor_copy(to_end[:, g * GH:(g + 1) * GH], ring[:, g % RING, :, P - 1]).then_inc(end_kept, 1)

            def mix(i, b, g):
                c = 2 * i + b
                slot = ring[:, g % RING, :, :]
                dve.wait_ge(end_kept, GROUPS * c + g + 1)
                dve.tensor_tensor(slot, slot, tok[:, b, 2 * P:].unsqueeze(1).to_broadcast([P, GH, P]),
                                  ALU.mult).then_inc(mixed, 1)

            def make_xw(i, b):
                c = 2 * i + b
                dve.wait_ge(end_kept, GROUPS * (c + 1))
                dve.wait_ge(carry_added, c + 1)
                for odd in range(2):
                    dve.tensor_tensor(by_head_half(rows[:], odd), xpad_half(odd), pick(to_end[:], odd),
                                      ALU.mult).then_inc(xw_made, 1)

            def update_state(c, b):
                dve.wait_ge(update_made, c + 1)
                dve.wait_ge(state_faded, c + 1)
                dve.tensor_tensor(state[:, b, :], state[:, b, :], ps_x[:], ALU.add).then_inc(state_made, 1)

            def make_y(c):
                dve.wait_ge(ring_free, GROUPS * (c + 1))
                dve.wait_ge(skip_made, c + 1)
                dve.wait_ge(ss_made, c)
                dve.tensor_tensor(gated[:].rearrange("p m t -> p (m t)"), skip[:].rearrange("p m t -> p (m t)"), ps_y[:],
                                  ALU.add).then_inc(y_made, 1)

            def gate(i, b, c):
                dve.wait_ge(y_made, c + 1)
                dve.wait_ge(evacuated, EVENTS * i + EVENTS)
                dve.tensor_tensor(gated[:], gated[:], sz[:, :, b, :], ALU.mult).then_inc(gate_made, 1)

            def gate_lo(c):
                dve.wait_ge(g_hi_made, c + 1)
                dve.tensor_tensor(g_lo[:], gated[:], g_hi[:], ALU.subtract).then_inc(g_split, 1)

            def make_x1(i, b, c):
                dve.wait_ge(out_made, c + 1)
                dve.wait_ge(rs_made, c + 1)
                dve.wait_ge(xres_in[b], 16 * i + 16)
                dve.scalar_tensor_tensor(xres[:, b, :], ps_out[:], rs[:, b:b + 1], xres[:, b, :],
                                         ALU.mult, ALU.add).then_inc(x1_made, 1)

            def turn_over(i, b, before, faded):
                prev = 2 * i + b - 1
                scan(i, b, 0)
                scan(i, b, 1)
                keep_end(i, b, 0)
                keep_end(i, b, 1)
                if before:
                    make_y(prev)
                    gate(*before, prev)
                    if faded:
                        update_state(prev, before[1])
                scan(i, b, 2)
                keep_end(i, b, 2)
                make_xpad(i, b)
                if before:
                    gate_lo(prev)
                scan(i, b, 3)
                keep_end(i, b, 3)

            def body(i, first, last):
                turn_over(i, 0, None if first else (i - 1, 1), True)
                if not last:
                    norm_stats(i + 1)
                scale_carry(i, 0)
                if not last:
                    normalise(i + 1)
                scan(i, 0, 4)
                keep_end(i, 0, 4)
                scan(i, 0, 5)
                keep_end(i, 0, 5)
                if not last:
                    norm_lo(i + 1, 0)
                    norm_lo(i + 1, 1)
                for g in range(6, GROUPS):
                    scan(i, 0, g)
                    keep_end(i, 0, g)
                if not first:
                    make_x1(i - 1, 1, 2 * i - 1)
                for g in range(POOL_MIXES, GROUPS):
                    mix(i, 0, g)
                make_xw(i, 0)
                turn_over(i, 1, (i, 0), not last)
                scale_carry(i, 1)
                if not last:
                    softplus(i + 1)
                    conv_taps(i + 1, 0)
                    cut_decay(i + 1)
                scan(i, 1, 4)
                keep_end(i, 1, 4)
                if not last:
                    conv_taps(i + 1, 1)
                scan(i, 1, 5)
                keep_end(i, 1, 5)
                scan(i, 1, 6)
                keep_end(i, 1, 6)
                if not last:
                    conv_taps(i + 1, 2)
                scan(i, 1, 7)
                keep_end(i, 1, 7)
                make_x1(i, 0, 2 * i)
                for g in range(POOL_MIXES, GROUPS):
                    mix(i, 1, g)
                if not last:
                    make_xw(i, 1)

            norm_stats(0)
            normalise(0)
            weight_lo(0)
            weight_lo(1)
            weight_lo(2)
            norm_lo(0, 0)
            norm_lo(0, 1)
            for n in range(3, 6):
                weight_lo(n)
            softplus(0)
            dve.wait_ge(filled, 2)
            cut_decay(0)
            for run in range(3):
                conv_taps(0, run)
            for n in range(6, PIECES):
                weight_lo(n)
            dve.wait_ge(zeroed, 9)
            body(0, True, False)
            with dve.Fori(1, BLOCKS - 1) as i:
                body(i, False, False)
            body(BLOCKS - 1, False, True)
            c = 2 * BLOCKS - 1
            make_y(c)
            gate(BLOCKS - 1, 1, c)
            gate_lo(c)
            make_x1(BLOCKS - 1, 1, c)

        @block.tensor
        def _(pe):
            def turn_xn(j, b, opening=False):
                pe.wait_ge(xn_made, 2 * j + b + 1)
                if not opening:
                    pe.wait_ge(evacuated, EVENTS * j - 1 + b)
                for k in range(KT):
                    made = pe.transpose(ps_proj[b][:, k * P:(k + 1) * P], xin[:, b, k * P:(k + 1) * P], eye1)
                made.then_inc(xn_turned, 1)

            def project(j, e):
                if e < 2:
                    pe.wait_ge(xn_split, 2 * j + 2)
                else:
                    pe.wait_ge(evacuated, EVENTS * j + e - 1)
                for half, m in enumerate(event_tiles(e)):
                    out = ps_proj[e % 2][:, half * TOK:(half + 1) * TOK]
                    cols = slice(m * P, (m + 1) * P)
                    for k in range(KT):
                        pe.matmul(out, win_hi[:, k, cols], xn_hi[:, k, :], start=(k == 0), stop=False)
                        pe.matmul(out, win_hi[:, k, cols], xn_lo[:, k, :], start=False, stop=False)
                        made = pe.matmul(out, win_lo[:, k, cols], xn_hi[:, k, :], start=False, stop=(k == KT - 1))
                made.then_inc(projected, 1)

            def turn_tok(i, b, opening=False):
                c = 2 * i + b
                pe.wait_ge(conv_made, CT * i + 2)
                pe.wait_ge(run_made, i + 1)
                if not opening:
                    pe.wait_ge(gvar_made, c - 1)
                    pe.wait_ge(whole_kept, c)
                pe.transpose(ps_tok[:, 0:P], cx[:, ZT, b, :], eye1)
                pe.transpose(ps_tok[:, P:2 * P], dt_run[:, b * P:(b + 1) * P], eye1)
                pe.matmul(ps_tok[:, 2 * P:3 * P], cx[:, ZT, b, :], cx[:, ZT + 1, b, :], start=True, stop=True).then_inc(tok_turned, 1)

            def turn_x(i, b, updated):
                pe.wait_ge(conv_made, CT * (i + 1))
                if updated:
                    pe.wait_ge(state_made, 2 * i + b)
                else:
                    pe.wait_ge(carry_scaled, 2 * i + b)
                for m in range(ZT):
                    made = pe.transpose(ps_x[:, m * P:(m + 1) * P], cx[:, m, b, :], eye1)
                made.then_inc(x_turned, 1)

            def carry(i, b):
                pe.wait_ge(xpad_made, 2 * (2 * i + b) + 2)
                for h in range(2):
                    made = pe.matmul(ps_x[:, h * 512:(h + 1) * 512], cx[:, ZT + 1, b, :],
                                     state[:, b, h * 512:(h + 1) * 512], start=True, stop=True)
                made.then_inc(carry_made, 1)

            def whole_decay(i, b):
                pe.wait_ge(tok_kept, 2 * i + b + 1)
                pe.matmul(ps_whole, last_row[:], tok[:, b, P + HEADS:2 * P], start=True, stop=True).then_inc(whole_made, 1)

            def add_carry(i, b):
                c = 2 * i + b
                pe.wait_ge(carry_scaled, c + 1)
                pe.wait_ge(y_made, c)
                for m in range(ZT):
                    made = pe.matmul(ps_y[:, m * P:(m + 1) * P], rows[:, m * P:(m + 1) * P], eye1,
                                     start=(m % 4 == 0), stop=False, skip_group_check=True)
                made.then_inc(carry_added, 1)

            def group(i, b, g):
                c = 2 * i + b
                if g < POOL_MIXES:
                    pe.wait_ge(mixed_pool, POOL_MIXES * c + g + 1)
                else:
                    pe.wait_ge(mixed, (GROUPS - POOL_MIXES) * c + g - POOL_MIXES + 1)
                for q in range(2):
                    for pair in range(GH // 2):
                        h = 2 * pair + q
                        made = pe.matmul(ps_y[32 * pair:32 * pair + 32, g * P:(g + 1) * P], xpad[:, g * GH + h, :],
                                         ring[:, g % RING, h, :], start=False, stop=(q == 1), skip_group_check=True)
                made.then_inc(ring_free, 1)

            def update(c, b):
                pe.wait_ge(xw_made, 2 * c + 2)
                for h in range(2):
                    made = pe.matmul(ps_x[:, h * 512:(h + 1) * 512], tok[:, b, 0:P], rows[:, h * 512:(h + 1) * 512],
                                     start=True, stop=True)
                made.then_inc(update_made, 1)

            def project_out(c):
                pe.wait_ge(g_split, c + 1)
                pe.wait_ge(x1_made, c)
                for k in range(ZT):
                    pe.matmul(ps_out[:], g_hi[:, k, :], wout_hi[:, k, :], start=(k == 0), stop=False)
                    pe.matmul(ps_out[:], g_hi[:, k, :], wout_lo[:, k, :], start=False, stop=False)
                    made = pe.matmul(ps_out[:], g_lo[:, k, :], wout_hi[:, k, :], start=False, stop=(k == ZT - 1))
                made.then_inc(out_made, 1)

            def sum_squares(c):
                pe.wait_ge(sq_summed, c + 1)
                if not (isinstance(c, int) and c == 2 * BLOCKS - 1):
                    pe.wait_ge(whole_kept, c + 2)
                pe.matmul(ps_ss, gated[:, 0, :], ones[:], start=True, stop=True).then_inc(ss_made, 1)

            def body(i, first, last):
                c = 2 * i
                turn_tok(i, 0, first)
                if not first:
                    update(c - 1, 1)
                project(i, 6)
                turn_x(i, 0, True)
                project(i, 7)
                carry(i, 0)
                whole_decay(i, 0)
                add_carry(i, 0)
                group(i, 0, 0)
                group(i, 0, 1)
                project(i, 8)
                group(i, 0, 2)
                project(i, 9)
                group(i, 0, 3)
                if not first:
                    sum_squares(c - 1)
                if not last:
                    turn_xn(i + 1, 0)
                    turn_xn(i + 1, 1)
                if not first:
                    project_out(c - 1)
                group(i, 0, 4)
                if not last:
                    project(i + 1, 0)
                group(i, 0, 5)
                if not last:
                    project(i + 1, 1)
                group(i, 0, 6)
                group(i, 0, 7)
                turn_tok(i, 1)
                if not last:
                    update(c, 0)
                    project(i + 1, 2)
                turn_x(i, 1, not last)
                if not last:
                    project(i + 1, 3)
                carry(i, 1)
                whole_decay(i, 1)
                add_carry(i, 1)
                group(i, 1, 0)
                group(i, 1, 1)
                if not last:
                    project(i + 1, 4)
                group(i, 1, 2)
                if not last:
                    project(i + 1, 5)
                group(i, 1, 3)
                sum_squares(c)
                group(i, 1, 4)
                project_out(c)
                for g in range(5, GROUPS):
                    group(i, 1, g)

            pe.wait_ge(filled, 1)
            turn_xn(0, 0, True)
            turn_xn(0, 1, True)
            for e in range(6):
                pe.wait_ge(lo_made, e + 1)
                project(0, e)
            pe.wait_ge(filled, 2)
            pe.wait_ge(lo_made, PIECES)
            body(0, True, False)
            with pe.Fori(1, BLOCKS - 1) as i:
                body(i, False, False)
            body(BLOCKS - 1, False, True)
            c = 2 * BLOCKS - 1
            sum_squares(c)
            project_out(c)


def mlp_phase(nc, x1_dram, gate_w, up_w, down_w, packed, down_s, out):
    with ExitStack() as ctx:
        def sb(name, shape, dt=F32):
            return ctx.enter_context(nc.sbuf_tensor(name, shape, dt))

        def sem(name):
            return ctx.enter_context(nc.semaphore(name))

        up = {"gate": (sb("wg_hi", [P, KT, INTER], F32R), sb("wg_lo", [P, KT, INTER], F32R)),
              "up": (sb("wu_hi", [P, KT, INTER], F32R), sb("wu_lo", [P, KT, INTER], F32R))}
        wd_hi, wd_lo = sb("wd_hi", [P, MT, HID], F32R), sb("wd_lo", [P, MT, HID], F32R)
        h_hi, h_lo = sb("h_hi", [P, MT, BT], F32R), sb("h_lo", [P, MT, BT], F32R)
        xn_hi, xn_lo = sb("x1n_hi", [P, KT, BT], F32R), sb("x1n_lo", [P, KT, BT], F32R)
        xin = sb("x1_in_sb", [P, TT, HID])
        res = sb("res", [P, 2, HID])
        silu_g, hidden = sb("silu_g", [P, 2, BT]), sb("hidden", [P, 2, BT])
        raw = sb("raw", [P, RAW_SLOTS, BT])
        scale_d = sb("scale_d", [P, HID])
        scales = sb("scales", [P, 2 * MT])
        eye = sb("eye2", [P, P])
        minus_half, eps = sb("minus_half2", [P, TT]), sb("eps2", [P, TT])
        stats, moments = sb("stats2", [P, TT, 6]), sb("moments2", [P, TT, 2])
        spread, rstd = sb("spread2", [P, TT]), sb("rstd2", [P, TT])
        pb = [ctx.enter_context(nc.psum_tensor(f"pb{n}", [P, BT], F32)) for n in range(8)]
        ps_g, ps_u, ps_t, ps_o = pb[0:2], pb[2:4], pb[4:6], pb[6:8]

        raw_in = [sem(f"wraw_in{n}") for n in range(RAW_SLOTS)]
        hi_made, lo_made = sem("whi_made"), sem("wlo_made")
        scales_in, x_in, res_in, stored = sem("scales_in"), sem("x1_in"), [sem("res_in0"), sem("res_in1")], [sem("stored0"), sem("stored1")]
        zeroed, filled = sem("zeroed2"), sem("filled2")
        stats_made, stats_seen, moments_made, eps_added, rstd_made = sem("stats2_made"), sem("stats2_seen"), sem("moments2_made"), sem("eps2_added"), sem("rstd2_made")
        xn_made, turned, xhi_made, split = sem("x1n_made"), sem("x1n_turned"), sem("x1n_hi_made"), sem("x1n_split")
        gu_made, silu_made, hidden_made, hhi_made, h_split = sem("gu_made"), sem("silu_made"), sem("hidden_made"), sem("hhi_made"), sem("h_split")
        down_made, down_scaled, out_ready = sem("down_made"), sem("down_scaled"), sem("out_ready")

        tokens = x1_dram.rearrange("b l h -> (b l) h")
        x_by_block = tokens.rearrange("(j t p) h -> j p t h", t=TT, p=P)
        out_by_block = out.rearrange("b l h -> (b l) h").rearrange("(j t p) h -> j p t h", t=TT, p=P)
        gate_t, up_t = gate_w.rearrange("(k p) n -> p k n", p=P), up_w.rearrange("(k p) n -> p k n", p=P)
        down_t = down_w.rearrange("(m p) n -> p m n", p=P)
        pieces = [("gate", 0), ("up", 0), ("gate", 1), ("up", 1)]
        ahead = len(pieces)
        with_tile = []
        for m in range(MT):
            more = [("gate", m + 2), ("up", m + 2)] if m + 2 < MT else []
            with_tile.append(range(len(pieces), len(pieces) + len(more) + 1))
            pieces += more + [("down", m)]

        def piece(n, part):
            kind, m = pieces[n]
            r = raw[:, n % RAW_SLOTS, :]
            if kind == "down":
                return (wd_hi, wd_lo)[part][:, m, :], r
            return up[kind][part][:, :, m * P:(m + 1) * P], r.rearrange("p (k n) -> p k n", k=KT)

        def t_cols(t):
            return slice(t * P, (t + 1) * P)

        block = ctx.enter_context(nc.Block())

        @block.sync
        def _(sp):
            def load_x(j):
                sp.dma_start(xin[:], x_by_block[bass.ds(j, 1)].rearrange("a p t h -> (a p) t h")).then_inc(x_in, 16)

            for free in stored:
                sp.sem_inc(free, AHEAD)
            load_x(0)
            sp.dma_start(scales[:], packed).then_inc(scales_in, 16)
            sp.dma_start(scale_d[:], down_s.to_broadcast([P, HID])).then_inc(scales_in, 16)
            for n, (kind, m) in enumerate(pieces):
                if n == 2 * ahead:
                    sp.wait_ge(turned, TT)
                    load_x(1)
                if n >= RAW_SLOTS:
                    sp.wait_ge(lo_made, n - RAW_SLOTS + 1)
                src = down_t[:, m, :] if kind == "down" else (gate_t if kind == "gate" else up_t)[:, :, m * P:(m + 1) * P]
                sp.dma_start(piece(n, 0)[1], src).then_inc(raw_in[n % RAW_SLOTS], 16)

            def body(j, first, last):
                for t in range(TT):
                    if t == 1 and not (first or last):
                        sp.wait_ge(turned, TT * j + TT)
                        load_x(j + 1)
                    sp.wait_ge(stored[t % 2], AHEAD + 16 * (2 * j + t // 2))
                    sp.dma_start(res[:, t % 2, :], x_by_block[bass.ds(j, 1), :, t, :].rearrange("a p h -> (a p) h")).then_inc(res_in[t % 2], 16)
                    if t >= 1:
                        store(j, t - 1)
                store(j, TT - 1)

            def store(j, t):
                sp.wait_ge(out_ready, AHEAD + TT * j + t + 1)
                sp.dma_start(out_by_block[bass.ds(j, 1), :, t, :].rearrange("a p h -> (a p) h"), res[:, t % 2, :]).then_inc(stored[t % 2], 16)

            body(0, True, False)
            with sp.Fori(1, NB - 1) as j:
                body(j, False, False)
            body(NB - 1, False, True)
            for n in range(2):
                sp.wait_ge(stored[n], AHEAD + 16 * 2 * NB)

        @block.gpsimd
        def _(pool):
            pool.sem_inc(out_ready, AHEAD)
            pool.memset(minus_half[:], -0.5).then_inc(zeroed, 1)
            pool.memset(eps[:], EPS).then_inc(zeroed, 1)
            pool.memset(eye[:], 0.0).then_inc(zeroed, 1)
            pool.wait_ge(zeroed, 3)
            pool.affine_select(out=eye[:], in_=eye[:], compare_op=ALU.not_equal, fill=1.0, base=0,
                               pattern=[[-1, P]], channel_multiplier=1).then_inc(filled, 1)

            def norm_scale(j):
                pool.wait_ge(moments_made, TT * j + TT)
                pool.tensor_tensor(spread[:], moments[:, :, 1], eps[:], ALU.add).then_inc(eps_added, 1)
                pool.wait_ge(eps_added, j + 1)
                pool.tensor_tensor(rstd[:], spread[:], minus_half[:], ALU.pow).then_inc(rstd_made, 1)

            def body(j, last):
                if not last:
                    norm_scale(j + 1)
                for t in range(TT):
                    pool.wait_ge(down_scaled, AHEAD + TT * j + t + 1)
                    pool.wait_ge(res_in[t % 2], 16 * (2 * j + t // 2 + 1))
                    pool.tensor_tensor(res[:, t % 2, :], res[:, t % 2, :], hidden[:, t % 2, :], ALU.add).then_inc(out_ready, 1)

            norm_scale(0)
            with pool.Fori(0, NB - 1) as j:
                body(j, False)
            body(NB - 1, True)

        @block.scalar
        def _(act):
            def weight_hi(n):
                act.wait_ge(raw_in[n % RAW_SLOTS], 16 * (n // RAW_SLOTS + 1))
                hi, r = piece(n, 0)
                act.activation(hi, r, ACT.Copy).then_inc(hi_made, 1)

            def norm_hi(j, t):
                act.wait_ge(turned, TT * j + t + 1)
                act.activation(xn_hi[:, :, t_cols(t)], ps_t[t % 2][:].rearrange("p (k t) -> p k t", k=KT), ACT.Copy).then_inc(xhi_made, 1)

            def body(j, first, last):
                for m in range(MT):
                    n = MT * j + m
                    if first:
                        for w in with_tile[m]:
                            weight_hi(w)
                    act.wait_ge(gu_made, n + 1)
                    if m >= 2:
                        act.wait_ge(hidden_made, AHEAD + n - 1)
                    else:
                        act.wait_ge(hidden_made, AHEAD + MT * j)
                    act.activation(silu_g[:, m % 2, :], ps_g[m % 2][:], ACT.Silu, scale=scales[:, m:m + 1]).then_inc(silu_made, 1)
                    act.wait_ge(hidden_made, AHEAD + n + 1)
                    act.activation(h_hi[:, m, :], hidden[:, m % 2, :], ACT.Copy).then_inc(hhi_made, 1)
                if not last:
                    for t in range(TT):
                        norm_hi(j + 1, t)

            for n in range(ahead):
                weight_hi(n)
            act.wait_ge(scales_in, 32)
            for t in range(TT):
                norm_hi(0, t)
            body(0, True, False)
            with act.Fori(1, NB - 1) as j:
                body(j, False, False)
            body(NB - 1, False, True)

        @block.vector
        def _(dve):
            def norm(j):
                dve.wait_ge(x_in, 16 * j + 16)
                for t in range(TT):
                    dve.bn_stats(stats[:, t, :], xin[:, t, :]).then_inc(stats_made, 1)
                dve.wait_ge(stats_made, TT * j + TT)
                dve.sem_inc(stats_seen, 1)
                for t in range(TT):
                    dve.bn_aggr(moments[:, t, :], stats[:, t, :]).then_inc(moments_made, 1)

            def normalise(j):
                dve.wait_ge(rstd_made, j + 1)
                for t in range(TT):
                    dve.tensor_scalar(xin[:, t, :], xin[:, t, :], moments[:, t, 0:1], rstd[:, t:t + 1],
                                      ALU.subtract, ALU.mult).then_inc(xn_made, 1)

            def norm_lo(j, t):
                dve.wait_ge(xhi_made, TT * j + t + 1)
                dve.tensor_tensor(xn_lo[:, :, t_cols(t)], ps_t[t % 2][:].rearrange("p (k t) -> p k t", k=KT),
                                  xn_hi[:, :, t_cols(t)], ALU.subtract).then_inc(split, 1)

            def scale_down(j, t):
                dve.wait_ge(down_made, TT * j + t + 1)
                if t >= 2:
                    dve.wait_ge(out_ready, AHEAD + TT * j + t - 1)
                dve.tensor_tensor(hidden[:, t % 2, :], ps_o[t % 2][:], scale_d[:], ALU.mult).then_inc(down_scaled, 1)

            def weight_lo(n):
                dve.wait_ge(hi_made, n + 1)
                lo, r = piece(n, 1)
                dve.tensor_tensor(lo, r, piece(n, 0)[0], ALU.subtract).then_inc(lo_made, 1)

            def body(j, first, last):
                for m in range(MT):
                    n = MT * j + m
                    if first:
                        for w in with_tile[m]:
                            weight_lo(w)
                    dve.wait_ge(silu_made, n + 1)
                    if m >= 2:
                        dve.wait_ge(h_split, n - 1)
                    else:
                        dve.wait_ge(out_ready, AHEAD + TT * j)
                    dve.scalar_tensor_tensor(hidden[:, m % 2, :], ps_u[m % 2][:], scales[:, MT + m:MT + m + 1],
                                             silu_g[:, m % 2, :], ALU.mult, ALU.mult).then_inc(hidden_made, 1)
                    dve.wait_ge(hhi_made, n + 1)
                    dve.tensor_tensor(h_lo[:, m, :], hidden[:, m % 2, :], h_hi[:, m, :], ALU.subtract).then_inc(h_split, 1)
                    if m == 2 and not last:
                        norm(j + 1)
                    if m == 5 and not last:
                        normalise(j + 1)
                dve.wait_ge(h_split, MT * j + MT)
                scale_down(j, 0)
                scale_down(j, 1)
                if not last:
                    for t in range(TT):
                        norm_lo(j + 1, t)
                scale_down(j, 2)
                scale_down(j, 3)

            for free in (hidden_made, down_scaled):
                dve.sem_inc(free, AHEAD)
            norm(0)
            normalise(0)
            for n in range(ahead):
                weight_lo(n)
            for t in range(TT):
                norm_lo(0, t)
            body(0, True, False)
            with dve.Fori(1, NB - 1) as j:
                body(j, False, False)
            body(NB - 1, False, True)

        @block.tensor
        def _(pe):
            def turn(j, t):
                pe.wait_ge(xn_made, TT * j + t + 1)
                if t >= 2:
                    pe.wait_ge(split, TT * j + t - 1)
                for k in range(KT):
                    made = pe.transpose(ps_t[t % 2][:, k * P:(k + 1) * P], xin[:, t, k * P:(k + 1) * P], eye[:])
                made.then_inc(turned, 1)

            def product(out_ps, w, cols):
                hi, lo = w
                for k in range(KT):
                    pe.matmul(out_ps, hi[:, k, cols], xn_hi[:, k, :], start=(k == 0), stop=False)
                    pe.matmul(out_ps, hi[:, k, cols], xn_lo[:, k, :], start=False, stop=False)
                    made = pe.matmul(out_ps, lo[:, k, cols], xn_hi[:, k, :], start=False, stop=(k == KT - 1))
                return made

            def down(j, t):
                if t >= 2:
                    pe.wait_ge(down_scaled, AHEAD + TT * j + t - 1)
                else:
                    pe.wait_ge(down_scaled, AHEAD + TT * j)
                for m in range(MT):
                    pe.matmul(ps_o[t % 2][:], h_hi[:, m, t_cols(t)], wd_hi[:, m, :], start=(m == 0), stop=False)
                    pe.matmul(ps_o[t % 2][:], h_hi[:, m, t_cols(t)], wd_lo[:, m, :], start=False, stop=False)
                    made = pe.matmul(ps_o[t % 2][:], h_lo[:, m, t_cols(t)], wd_hi[:, m, :], start=False, stop=(m == MT - 1))
                made.then_inc(down_made, 1)

            def body(j, first, last):
                pe.wait_ge(split, TT * j + TT)
                for m in range(MT):
                    n = MT * j + m
                    if first:
                        pe.wait_ge(lo_made, pieces.index(("up", m)) + 1)
                    if m >= 2:
                        pe.wait_ge(hidden_made, AHEAD + n - 1)
                    else:
                        pe.wait_ge(hidden_made, AHEAD + MT * j)
                    product(ps_g[m % 2][:], up["gate"], slice(m * P, (m + 1) * P))
                    product(ps_u[m % 2][:], up["up"], slice(m * P, (m + 1) * P)).then_inc(gu_made, 1)
                if first:
                    pe.wait_ge(lo_made, len(pieces))
                pe.wait_ge(h_split, MT * j + MT)
                down(j, 0)
                down(j, 1)
                if not last:
                    for t in range(TT):
                        turn(j + 1, t)
                down(j, 2)
                down(j, 3)

            pe.wait_ge(filled, 1)
            for t in range(TT):
                turn(0, t)
            body(0, True, False)
            with pe.Fori(1, NB - 1) as j:
                body(j, False, False)
            body(NB - 1, False, True)


def kernel(**inputs):
    import concourse.bacc as bacc
    from concourse.bass_utils import run_bass_kernel_spmd

    a = {name: np.ascontiguousarray(v) for name, v in inputs.items()}
    A, M = "L0_attn_", "L0_ffn_"

    def by_tile(v, width=P):
        return v.reshape(-1, width).T

    mup = a[A + "mup_vector"]
    dt_at = 2 * D_SSM + 2 * STATE
    twice = lambda v: np.concatenate([v, v]).reshape(P, 1)
    mixer_consts = np.concatenate([
        by_tile(mup[:dt_at]), twice(mup[dt_at:]),
        a[A + "conv_w"].reshape(CT, P, TAPS).transpose(1, 0, 2).reshape(P, CT * TAPS),
        by_tile(a[A + "conv_b"]), by_tile(np.repeat(a[A + "D"], HEAD)), by_tile(a[A + "norm_w"]),
        twice(a[A + "dt_bias"]), twice(a[A + "A_log"])], axis=1)
    mlp_scales = np.concatenate([by_tile(a[M + "gate_s"]), by_tile(a[M + "up_s"])], axis=1)
    arrays = {
        "x": a[A + "hidden_states"], "w_in": a[A + "W_in"], "w_out": a[A + "W_out"], "mixer_consts": mixer_consts,
        "gate_w": a[M + "gate_w"].T, "up_w": a[M + "up_w"].T, "down_w": a[M + "down_w"].T,
        "mlp_scales": mlp_scales, "down_s": a[M + "down_s"].reshape(1, HID),
    }
    arrays = {name: np.ascontiguousarray(v) for name, v in arrays.items()}

    nc = bacc.Bacc("TRN2", target_bir_lowering=False, num_devices=1, dynamic_dma_scratch_size=2048)
    d = {name: nc.dram_tensor(name, v.shape, mybir.dt.from_np(v.dtype), kind="ExternalInput").ap() for name, v in arrays.items()}
    out = nc.dram_tensor("out", (BATCH, LEN, HID), F32, kind="ExternalOutput").ap()
    decay_dram = nc.dram_tensor("decay_dram", (BLOCKS, BATCH, HEADS, P), F32, kind="Internal").ap()
    x1_dram = nc.dram_tensor("x1_dram", (BATCH, LEN, HID), F32, kind="Internal").ap()
    mixer_phase(nc, d["x"], d["w_in"], d["w_out"], d["mixer_consts"], decay_dram, x1_dram)
    mlp_phase(nc, x1_dram, d["gate_w"], d["up_w"], d["down_w"], d["mlp_scales"], d["down_s"], out)
    r = run_bass_kernel_spmd(nc, [arrays], core_ids=[0])
    return r.results[0]["out"]
```

```python
import concourse.bass as bass
from concourse import mybir
from contextlib import ExitStack
import numpy as np

F32 = mybir.dt.float32
F32R = mybir.dt.float32r
I32 = mybir.dt.int32
I16 = mybir.dt.int16
ACT = mybir.ActivationFunctionType
ALU = mybir.AluOpType

P = 128
BATCH, LEN, HID = 2, 1024, 512
D_SSM, STATE, HEADS, TAPS = 1024, 128, 64, 4
HEAD = D_SSM // HEADS
INTER = 1408
EPS = 1e-5

BLOCKS = LEN // P
TOK = BATCH * P
KT = HID // P
ZT = D_SSM // P
CT = ZT + 2
PT = ZT + CT + 1
COLS = PT * P
GROUPS = 8
GH = HEADS // GROUPS
POOL_TILES = 3
RING = 4
EVENTS = 10
PIECES = EVENTS + ZT // 2
DT_AT = 2 * D_SSM + 2 * STATE
AHEAD = 1
LOGN = 12

C_MUP, C_CW, C_CB, C_D, C_NW, C_DTB, C_ALOG = 0, PT, PT + 4 * CT, PT + 5 * CT, PT + 5 * CT + ZT, PT + 5 * CT + 2 * ZT, PT + 5 * CT + 2 * ZT + 1
C_N = C_ALOG + 1

MT = INTER // P
BT = 512
NB = BATCH * LEN // BT
TT = BT // P
PIECES2 = 3 * MT
LANDED = 14
RAW_SLOTS = 3
EARLY_TILES = (LANDED + RAW_SLOTS) // 2


def log1p_coefficients():
    k = np.arange(LOGN)
    nodes = 0.5 + 0.5 * np.cos(np.pi * (2 * k + 1) / (2 * LOGN))
    cheb = np.polynomial.chebyshev.Chebyshev.fit(nodes, np.log1p(nodes) / nodes, LOGN - 1, domain=[0, 1])
    return [float(c) for c in cheb.convert(kind=np.polynomial.Polynomial, domain=[-1, 1], window=[-1, 1]).coef]


class Handover:

    def __init__(self, nc, ctx, x1_dram, gate_w, up_w, down_w):
        def sb(ctx, name, shape, dt=F32):
            return ctx.enter_context(nc.sbuf_tensor(name, shape, dt))

        with ExitStack() as place:
            self.win_hi, self.win_lo = (sb(place, name, [P, KT, COLS], F32R) for name in ("win_hi", "win_lo"))
        with ExitStack() as place:
            self.h_raw = [sb(place, f"h_raw{n}", [P, MT, BT]) for n in range(2)]
        self.h_hi, self.h_lo = (sb(ctx, name, [P, MT, BT], F32R) for name in ("h_hi", "h_lo"))
        self.raw = sb(ctx, "raw", [P, RAW_SLOTS, BT])
        self.xin = sb(ctx, "x1_in_sb", [P, TT, HID])
        self.xn_hi = sb(ctx, "x1n_hi", [P, KT, BT], F32R)
        self.silu_g, self.hidden = sb(ctx, "silu_g", [P, 2, BT]), sb(ctx, "hidden", [P, 2, BT])
        self.scale_d = sb(ctx, "scale_d", [P, HID])
        assert 2 * KT * COLS <= 2 * MT * BT + RAW_SLOTS * BT + TT * HID + KT * BT + 2 * BT + 2 * BT + HID
        self.res = sb(ctx, "res", [P, 2, HID])

        self.x_in = ctx.enter_context(nc.semaphore("x1_in"))
        self.low_max = sb(ctx, "low_max", [P, 4])
        self.low_row, self.low_any = sb(ctx, "low_row", [1, P]), sb(ctx, "low_any", [1, 1])
        self.low_max_made, self.low_in = ctx.enter_context(nc.semaphore("low_max_made")), ctx.enter_context(nc.semaphore("low_in"))
        self.raw_in = [ctx.enter_context(nc.semaphore(f"wraw_in{n}")) for n in range(PIECES2)]
        self.x1_out = [ctx.enter_context(nc.semaphore(f"x1_out{b}")) for b in range(BATCH)]

        self.x1_by_block = x1_dram.rearrange("b l h -> (b l) h").rearrange("(j t p) h -> j p t h", t=TT, p=P)
        self.sources = {"gate": gate_w.rearrange("(k p) n -> p k n", p=P), "up": up_w.rearrange("(k p) n -> p k n", p=P),
                        "down": down_w.rearrange("(m p) n -> p m n", p=P)}
        self.pieces = [(kind, m) for m in range(MT) for kind in ("gate", "up")] + [("down", m) for m in range(MT)]
        self.first_pieces = 10
        self.with_tile = [range(min(self.first_pieces + 3 * m, PIECES2), min(self.first_pieces + 3 * (m + 1), PIECES2)) for m in range(MT)]
        assert all(self.pieces[n][1] > m for m in range(MT) for n in self.with_tile[m] if n < 2 * MT)
        assert all(n >= LANDED or MT - 1 - n // 2 > m for m in range(MT) for n in self.with_tile[m])

    def raw_piece(self, n):
        kind, m = self.pieces[n]
        r = self.h_raw[n % 2][:, MT - 1 - n // 2, :] if n < LANDED else self.raw[:, (n - LANDED) % RAW_SLOTS, :]
        if kind == "down":
            return r, self.sources[kind][:, m, :]
        return r.rearrange("p (k n) -> p k n", k=KT), self.sources[kind][:, :, m * P:(m + 1) * P]


def mixer_phase(nc, x, w_in, w_out, packed, decay_dram, x1_dram, hand):
    with ExitStack() as ctx:
        def sb(name, shape, dt=F32):
            return ctx.enter_context(nc.sbuf_tensor(name, shape, dt))

        def sem(name):
            return ctx.enter_context(nc.semaphore(name))

        win_hi, win_lo = hand.win_hi, hand.win_lo
        wout_hi, wout_lo = sb("wout_hi", [P, ZT, HID], F32R), sb("wout_lo", [P, ZT, HID], F32R)
        ring = sb("ring", [P, RING, GH, P])
        eye = sb("eye", [P, GH, P])
        cin = sb("cin", [P, CT, BATCH, P + TAPS - 1])
        cx = sb("cx", [P, CT, BATCH, P])
        tap = sb("tap", [P, POOL_TILES, BATCH, P])
        sz = sb("sz", [P, ZT, BATCH, P])
        xn_hi, xn_lo = sb("xn_hi", [P, KT, TOK], F32R), sb("xn_lo", [P, KT, TOK], F32R)
        xpad = sb("xpad", [P, HEADS, 2 * HEAD])
        rows = sb("rows", [P, D_SSM])
        state = sb("state", [P, BATCH, D_SSM])
        skip = sb("skip", [P, ZT, P])
        gated = sb("gated", [P, ZT, P])
        g_hi, g_lo = sb("g_hi", [P, ZT, P], F32R), sb("g_lo", [P, ZT, P], F32R)
        xin = sb("xin", [P, BATCH, HID])
        xres = hand.res
        dt_v, dt_e, dt_p = sb("dt_v", [P, P]), sb("dt_e", [P, P]), sb("dt_p", [P, P])
        dt_run = sb("dt_run", [P, 2, P])
        decay = sb("decay", [P, P])
        tok = sb("tok", [P, 6 * P])
        to_end = sb("to_end", [P, HEADS])
        whole = sb("whole", [P, BATCH, HEADS])
        consts = sb("consts", [P, C_N])
        neg_a = sb("neg_a", [P, 1])
        stats, moments = sb("stats", [P, BATCH, 6]), sb("moments", [P, BATCH, 2])
        spread, rstd = sb("spread", [P, BATCH]), sb("rstd", [P, BATCH])
        gvar, rs = sb("gvar", [P, BATCH]), sb("rs", [P, BATCH])
        minus_half, eps = sb("minus_half", [P, BATCH]), sb("eps", [P, BATCH])
        ones, zero = sb("ones", [P, 1]), sb("zero", [P, 1])
        last_row = sb("last_row", [P, P])

        def pb(name, banks=1):
            return ctx.enter_context(nc.psum_tensor(name, [P, 512 * banks], F32))

        ps_proj = [pb("ps_proj0"), pb("ps_proj1")]
        ps_tok, ps_out = pb("ps_tok"), pb("ps_out")
        ps_x, ps_y = pb("ps_x", 2), pb("ps_y", 2)
        ps_whole, ps_ss = ps_tok[:, 2 * P:3 * P], ps_tok[:, 3 * P:3 * P + 1]
        tok_b = [tok[:, at:at + P] for at in (0, 4 * P)]
        tok_cb = [tok[:, at:at + P] for at in (P, 5 * P)]
        tok_dt = [tok[:, 2 * P + b * HEADS:2 * P + (b + 1) * HEADS] for b in range(BATCH)]
        tok_run = [tok[:, 3 * P + b * HEADS:3 * P + (b + 1) * HEADS] for b in range(BATCH)]

        consts_in = sem("consts_in")
        raw_in = [sem(f"raw_in{n}") for n in range(PIECES)]
        hi_made, lo_made = sem("hi_made"), sem("lo_made")
        zeroed, filled = sem("zeroed"), sem("filled")
        tap_scaled, tap_added = sem("tap_scaled"), sem("tap_added")
        a_made, a_negated = sem("a_made"), sem("a_negated")
        x_in, xres_in = sem("x_in"), [sem(f"xres_in{b}") for b in range(BATCH)]
        ring_in = [sem(f"ring_in{n}") for n in range(RING)]
        decay_out, x1_out = sem("decay_out"), hand.x1_out
        stats_made, stats_seen, moments_made, eps_added, rstd_made = (
            sem("stats_made"), sem("stats_seen"), sem("moments_made"), sem("eps_added"), sem("rstd_made"))
        xn_made, xn_turned, xn_hi_made, xn_split = sem("xn_made"), sem("xn_turned"), sem("xn_hi_made"), sem("xn_split")
        projected, evacuated = sem("projected"), sem("evacuated")
        dt_abs, dt_exp, soft_step, dt_made, decay_made, decay_cut, run_made = (
            sem("dt_abs"), sem("dt_exp"), sem("soft_step"), sem("dt_made"), sem("decay_made"), sem("decay_cut"), sem("run_made"))
        tap_first, tap_made, conv_made, halo_kept = sem("tap_first"), sem("tap_made"), sem("conv_made"), sem("halo_kept")
        tok_turned, x_turned, tok_kept, whole_made, whole_kept = (
            sem("tok_turned"), sem("x_turned"), sem("tok_kept"), sem("whole_made"), sem("whole_kept"))
        xpad_made, carry_made, carry_scaled, carry_added = sem("xpad_made"), sem("carry_made"), sem("carry_scaled"), sem("carry_added")
        scanned, end_kept, mixed, mixed_pool = sem("scanned"), sem("end_kept"), sem("mixed"), sem("mixed_pool")
        ring_free = sem("ring_free")
        xw_made, update_made, state_faded, state_made = sem("xw_made"), sem("update_made"), sem("state_faded"), sem("state_made")
        skip_made, y_made, gate_made, g_hi_made, g_split, squared, sq_folded = (
            sem("skip_made"), sem("y_made"), sem("gate_made"), sem("g_hi_made"), sem("g_split"), sem("squared"),
            sem("sq_folded"))
        ss_made, gvar_made, gvar_eps, rs_made, out_made, x1_made = (
            sem("ss_made"), sem("gvar_made"), sem("gvar_eps"), sem("rs_made"), sem("out_made"), sem("x1_made"))

        x_by_block = x.rearrange("b (i p) h -> i p b h", p=P)
        x1_by_block = x1_dram.rearrange("b (i p) h -> i p b h", p=P)
        w_in_t = w_in.rearrange("(k p) n -> p k n", p=P)
        w_out_t = w_out.rearrange("(k p) n -> p k n", p=P)
        log_c = log1p_coefficients()

        def event_tiles(e):
            if e == 0:
                return [PT - 1]
            if e == 1:
                return [2 * ZT, 2 * ZT + 1]
            if e < 6:
                return [ZT + 2 * (e - 2), ZT + 2 * (e - 2) + 1]
            return [2 * (e - 6), 2 * (e - 6) + 1]

        def by_k(t, k):
            return t.rearrange("p (k n) -> p k n", k=k)

        landing = [tap[:, 0:2, :, :].rearrange("p m b t -> p (m b t)"), rows[:]] + [ring[:, n, :, :].rearrange("p g t -> p (g t)") for n in range(RING)]
        landing += [sz[:, n:n + 4, :, :].rearrange("p m b t -> p (m b t)") for n in (0, 4)]
        landing += [xpad[:, n:n + 32, :].rearrange("p h d -> p (h d)") for n in (0, 32)]
        landing += [state[:, 0, :]] + [t[:].rearrange("p m t -> p (m t)") for t in (xres, skip, gated)]
        LANDED_X, EARLY, LANDED_XRES = 6, EVENTS + 1, EVENTS + 2

        def piece(n):
            if n < EVENTS:
                tiles = event_tiles(n)
                cols = slice(tiles[0] * P, (tiles[-1] + 1) * P)
                return win_hi[:, :, cols], win_lo[:, :, cols], by_k(landing[n], KT)
            k = slice(2 * (n - EVENTS), 2 * (n - EVENTS) + 2)
            return wout_hi[:, k, :], wout_lo[:, k, :], by_k(landing[n], 2)

        CONV_RUNS = [[ZT, ZT + 1], list(range(POOL_TILES)), list(range(POOL_TILES, ZT))]
        CONV_ORDER = [m for run in CONV_RUNS for m in run]
        TAP_AT = {mk: n for n, mk in enumerate((m, k) for run in (0, 2) for k in range(1, TAPS) for m in CONV_RUNS[run])}
        N_TAPS = len(TAP_AT)

        eye1 = eye[:, 0, :]
        flat = "p g t -> p (g t)"
        SLOT_USES = GROUPS // RING
        POOL_MIXES = (GROUPS - 3, GROUPS - 1)
        POOL_BLOCK = sum(POOL_MIXES)
        DVE_BLOCK = BATCH * GROUPS - POOL_BLOCK

        def col(at):
            return consts[:, at:at + 1]

        block = ctx.enter_context(nc.Block())

        @block.sync
        def _(sp):
            sp.dma_start(xin[:], x_by_block[0]).then_inc(x_in, 16)
            sp.dma_start(consts[:], packed).then_inc(consts_in, 16)
            for n in range(PIECES):
                raw = piece(n)[2]
                if n == 0:
                    for half in range(2):
                        sp.dma_start(raw[:, :, half * HEADS:(half + 1) * HEADS],
                                     w_in_t[:, :, DT_AT:DT_AT + HEADS]).then_inc(raw_in[n], 16)
                elif n < EVENTS:
                    at = event_tiles(n)[0] * P
                    sp.dma_start(raw, w_in_t[:, :, at:at + 2 * P]).then_inc(raw_in[n], 16)
                else:
                    k = 2 * (n - EVENTS)
                    sp.dma_start(raw, w_out_t[:, k:k + 2, :]).then_inc(raw_in[n], 16)

            def store_decay(j):
                sp.wait_ge(decay_cut, j + 1)
                sp.dma_start(decay_dram[bass.ds(j, 1), :, :, :].rearrange("a b h t -> (a b h) t"), decay[:]).then_inc(decay_out, 16)

            def load_decays(i, b, g, opening=False):
                if not opening:
                    sp.wait_ge(ring_free, GROUPS * (2 * i + b) + g - RING + 1)
                src = decay_dram[bass.ds(i, 1), b, g * GH:(g + 1) * GH, :].rearrange("a h t -> a (h t)")
                sp.dma_start(ring[:, g % RING, :, :].rearrange(flat),
                             src.to_broadcast([P, GH * P])).then_inc(ring_in[g % RING], 16)

            def load_res(i, b, first):
                if first:
                    sp.wait_ge(lo_made, LANDED_XRES)
                else:
                    sp.wait_ge(x1_out[b], 16 * i)
                sp.dma_start(xres[:, b, :], x_by_block[bass.ds(i, 1), :, b, :].rearrange("a p h -> (a p) h")).then_inc(xres_in[b], 16)

            def body(i, first, last):
                if not last:
                    sp.wait_ge(xn_turned, 2 * i + 2)
                    sp.dma_start(xin[:], x_by_block[bass.ds(i + 1, 1)].rearrange("a p b h -> (a p) b h")).then_inc(x_in, 16)
                for g in range(RING, GROUPS):
                    load_decays(i, 0, g)
                load_res(i, 0, first)
                for g in range(RING):
                    load_decays(i, 1, g)
                for g in range(RING, GROUPS):
                    load_decays(i, 1, g)
                load_res(i, 1, first)
                if not last:
                    store_decay(i + 1)
                    sp.wait_ge(decay_out, 16 * i + 32)
                    for g in range(RING):
                        load_decays(i + 1, 0, g)

            sp.wait_ge(lo_made, LANDED_X)
            store_decay(0)
            sp.wait_ge(decay_out, 16)
            for g in range(RING):
                load_decays(0, 0, g, opening=True)
            body(0, True, False)
            with sp.Fori(1, BLOCKS - 1) as i:
                body(i, False, False)
            body(BLOCKS - 1, False, True)
            sp.wait_ge(projected, EVENTS * BLOCKS)
            sp.dma_start(hand.xin[:], hand.x1_by_block[0]).then_inc(hand.x_in, 16)
            for n in range(LANDED + RAW_SLOTS):
                sp.dma_start(*hand.raw_piece(n)).then_inc(hand.raw_in[n], 16)
            sp.wait_ge(hand.low_max_made, 4)
            sp.dma_start(hand.low_row[:], hand.low_max[:, 3:]).then_inc(hand.low_in, 16)

        @block.gpsimd
        def _(pool):
            pool.memset(minus_half[:], -0.5).then_inc(zeroed, 1)
            pool.memset(eye[:], 0.0).then_inc(zeroed, 1)
            pool.memset(last_row[:], 0.0).then_inc(zeroed, 1)
            pool.memset(cin[:, :, :, 0:TAPS - 1], 0.0).then_inc(zeroed, 1)
            pool.memset(zero[:], 0.0).then_inc(zeroed, 1)
            pool.memset(ones[:], 1.0).then_inc(zeroed, 1)
            pool.memset(eps[:], EPS).then_inc(zeroed, 1)
            pool.wait_ge(zeroed, 7)
            pool.affine_select(out=eye[:], in_=eye[:], compare_op=ALU.not_equal, fill=1.0, base=0,
                               pattern=[[0, GH], [-1, P]], channel_multiplier=1).then_inc(filled, 1)

            def norm_scale(j):
                pool.wait_ge(moments_made, 2 * j + 2)
                pool.tensor_tensor(spread[:], moments[:, :, 1], eps[:], ALU.add).then_inc(eps_added, 1)
                pool.wait_ge(eps_added, j + 1)
                pool.tensor_tensor(rstd[:], spread[:], minus_half[:], ALU.pow).then_inc(rstd_made, 1)

            def add_taps(j, k):
                n = (TAPS - 1) * j + k - 1
                pool.wait_ge(tap_scaled, n + 1)
                pool.wait_ge(tap_added, n)
                if k == 1:
                    pool.wait_ge(tap_first, CT * j + 2 + POOL_TILES)
                sums = cx[:, 0:POOL_TILES, :, :].rearrange("p m b t -> p (m b t)")
                pool.tensor_tensor(sums, sums, tap[:].rearrange("p m b t -> p (m b t)"), ALU.add).then_inc(tap_added, 1)

            norm_scale(0)
            pool.affine_select(out=last_row[:], in_=last_row[:], compare_op=ALU.not_equal, fill=1.0, base=1 - P,
                               pattern=[[0, P]], channel_multiplier=1).then_inc(filled, 1)
            pool.wait_ge(a_made, 1)
            pool.tensor_scalar(neg_a[:], neg_a[:], -1.0, None, ALU.mult).then_inc(a_negated, 1)
            for k in range(1, TAPS):
                add_taps(0, k)
            pool.wait_ge(lo_made, EARLY)
            pool.memset(xpad[:], 0.0).then_inc(zeroed, 1)
            pool.memset(state[:], 0.0).then_inc(zeroed, 1)

            def mix(i, b, g):
                c = 2 * i + b
                slot = ring[:, g % RING, :, :]
                pool.wait_ge(end_kept, GROUPS * c + g + 1)
                pool.wait_ge(tok_kept, c + 1)
                pool.tensor_tensor(slot, slot, tok_cb[b].unsqueeze(1).to_broadcast([P, GH, P]),
                                   ALU.mult).then_inc(mixed_pool, 1)

            def fade_state(i, b):
                pool.wait_ge(whole_kept, i + 1)
                pool.wait_ge(carry_made, 2 * i + b + 1)
                s = state[:, b, :].rearrange("p (h d) -> p h d", h=HEADS)
                pool.tensor_tensor(s, s, whole[:, b, :].unsqueeze(2).to_broadcast([P, HEADS, HEAD]),
                                   ALU.mult).then_inc(state_faded, 1)

            def fold_squares(c):
                pool.wait_ge(squared, c + 1)
                half = ZT // 2
                pool.tensor_tensor(gated[:, 0:half, :], gated[:, 0:half, :], gated[:, half:, :], ALU.add).then_inc(sq_folded, 1)

            def rms_scale(c, b):
                pool.wait_ge(gvar_made, c + 1)
                pool.tensor_tensor(gvar[:, b:b + 1], gvar[:, b:b + 1], eps[:, 0:1], ALU.add).then_inc(gvar_eps, 1)
                pool.wait_ge(gvar_eps, c + 1)
                pool.tensor_tensor(rs[:, b:b + 1], gvar[:, b:b + 1], minus_half[:, 0:1], ALU.pow).then_inc(rs_made, 1)

            def body(i, first, last):
                for b in range(BATCH):
                    prev = 2 * i + b - 1
                    opening = first and b == 0
                    for g in range(RING):
                        mix(i, b, g)
                        if g == 1 and b == 0 and not last:
                            norm_scale(i + 1)
                    if not last:
                        fade_state(i, b)
                    if not opening:
                        fold_squares(prev)
                    for g in range(RING, GROUPS):
                        if g < POOL_MIXES[b]:
                            mix(i, b, g)
                        if b == 1 and g < RING + TAPS - 1 and not last:
                            add_taps(i + 1, g - RING + 1)
                        if g == (RING if b == 0 else RING + 2) and not opening:
                            rms_scale(prev, 1 - b)

            body(0, True, False)
            with pool.Fori(1, BLOCKS - 1) as i:
                body(i, False, False)
            body(BLOCKS - 1, False, True)
            fold_squares(2 * BLOCKS - 1)
            rms_scale(2 * BLOCKS - 1, 1)

        @block.scalar
        def _(act):
            act.wait_ge(consts_in, 16)
            act.activation(neg_a[:], col(C_ALOG), ACT.Exp).then_inc(a_made, 1)

            def weight_hi(n):
                act.wait_ge(raw_in[n], 32 if n == 0 else 16)
                hi, lo, raw = piece(n)
                if n < EVENTS:
                    act.activation(hi, raw, ACT.Copy).then_inc(hi_made, 1)
                    return
                for k in range(2):
                    made = act.activation(hi[:, k, :], raw[:, k, :], ACT.Copy, scale=col(C_NW + 2 * (n - EVENTS) + k))
                made.then_inc(hi_made, 1)

            def norm_hi(j, b):
                act.wait_ge(xn_turned, 2 * j + b + 1)
                act.activation(xn_hi[:, :, b * P:(b + 1) * P], ps_proj[b][:].rearrange("p (k t) -> p k t", k=KT),
                               ACT.Copy).then_inc(xn_hi_made, 1)

            def evacuate(j, e):
                act.wait_ge(projected, EVENTS * j + e + 1)
                if e == 0:
                    act.wait_ge(dt_made, j)
                    for made, part, f in ((dt_abs, dt_e, ACT.Abs), (evacuated, dt_v, ACT.Relu)):
                        for b in range(BATCH):
                            r = slice(b * HEADS, (b + 1) * HEADS)
                            last = act.activation(part[r, :], ps_proj[0][r, b * P:(b + 1) * P], f,
                                                  bias=consts[r, C_DTB:C_DTB + 1], scale=consts[r, C_MUP + PT - 1:C_MUP + PT])
                        last.then_inc(made, 1)
                    act.wait_ge(dt_abs, j + 1)
                    act.activation(dt_e[:], dt_e[:], ACT.Exp, scale=-1.0).then_inc(dt_exp, 1)
                    return
                if e == 1:
                    act.wait_ge(halo_kept, j)
                if e == 6:
                    act.wait_ge(gate_made, 2 * j)
                for half, m in enumerate(event_tiles(e)):
                    src = ps_proj[e % 2][:, half * TOK:(half + 1) * TOK].rearrange("p (b t) -> p b t", b=BATCH)
                    if m < ZT:
                        made = act.activation(sz[:, m, :, :], src, ACT.Silu, scale=col(C_MUP + m))
                    else:
                        made = act.activation(cin[:, m - ZT, :, TAPS - 1:], src, ACT.Copy, scale=col(C_MUP + m))
                made.then_inc(evacuated, 1)

            def make_decay(j):
                act.wait_ge(dt_made, j + 1)
                act.wait_ge(decay_out, 16 * j)
                act.activation(decay[:], dt_run[:, 0, :], ACT.Exp, scale=neg_a[:]).then_inc(decay_made, 1)

            def first_taps(j, run):
                for m in CONV_RUNS[run]:
                    if m >= ZT:
                        act.wait_ge(evacuated, EVENTS * j + 2)
                        act.wait_ge(tok_turned, 2 * j)
                        act.wait_ge(carry_made, 2 * j)
                    else:
                        act.wait_ge(evacuated, EVENTS * j + 3 + m // 2)
                        act.wait_ge(x_turned, 2 * j)
                        act.wait_ge(skip_made, 2 * j)
                    act.activation(cx[:, m, :, :], cin[:, m, :, 0:P], ACT.Identity, bias=col(C_CB + m),
                                   scale=col(C_CW + 4 * m)).then_inc(tap_first, 1)

            def scale_taps(j, k):
                n = (TAPS - 1) * j + k - 1
                act.wait_ge(tap_added, n)
                for m in CONV_RUNS[1]:
                    made = act.activation(tap[:, m, :, :], cin[:, m, :, k:k + P], ACT.Copy, scale=col(C_CW + 4 * m + k))
                made.then_inc(tap_scaled, 1)

            def conv_silu(j, run):
                for m in CONV_RUNS[run]:
                    if run == 1:
                        act.wait_ge(tap_added, (TAPS - 1) * (j + 1))
                    else:
                        act.wait_ge(tap_made, N_TAPS * j + TAP_AT[m, TAPS - 1] + 1)
                    act.activation(cx[:, m, :, :], cx[:, m, :, :], ACT.Silu).then_inc(conv_made, 1)

            def keep_halo(j):
                act.wait_ge(tap_made, N_TAPS * (j + 1))
                act.wait_ge(tap_scaled, (TAPS - 1) * (j + 1))
                act.activation(cin[:, :, :, 0:TAPS - 1], cin[:, :, :, P:], ACT.Copy).then_inc(halo_kept, 1)

            def keep_tok(i, b):
                act.wait_ge(tok_turned, 2 * i + b + 1)
                at, width = (0, 4 * P) if b == 0 else (4 * P, 2 * P)
                act.activation(tok[:, at:at + width], ps_tok[:, 0:width], ACT.Copy).then_inc(tok_kept, 1)

            def keep_whole(i):
                act.wait_ge(whole_made, i + 1)
                act.wait_ge(state_faded, 2 * i)
                act.activation(whole[:].rearrange("p b h -> p (b h)"), ps_whole, ACT.Copy).then_inc(whole_kept, 1)

            def make_skip(i, b):
                act.wait_ge(conv_made, CT * (i + 1))
                act.wait_ge(y_made, 2 * i + b)
                for m in range(ZT):
                    made = act.activation(skip[:, m, :], cx[:, m, b, :], ACT.Copy, scale=col(C_D + m))
                made.then_inc(skip_made, 1)

            def gate_hi(c):
                act.wait_ge(gate_made, c + 1)
                act.wait_ge(out_made, c)
                act.activation(g_hi[:], gated[:], ACT.Copy).then_inc(g_hi_made, 1)

            def square(c):
                act.wait_ge(g_split, c + 1)
                act.activation(gated[:], gated[:], ACT.Square).then_inc(squared, 1)

            def mean_square(c, b):
                act.wait_ge(ss_made, c + 1)
                act.wait_ge(rs_made, c)
                act.activation(gvar[:, b:b + 1], ps_ss, ACT.Copy, scale=1.0 / D_SSM).then_inc(gvar_made, 1)

            def store_x1(i, b, c):
                act.wait_ge(x1_made, c + 1)
                act.dma_start(x1_by_block[bass.ds(i, 1), :, b, :].rearrange("a p h -> (a p) h"),
                              xres[:, b, :]).then_inc(x1_out[b], 16)

            def body(i, first, last):
                c = 2 * i
                keep_tok(i, 0)
                if not first:
                    gate_hi(c - 1)
                evacuate(i, 6)
                if not first:
                    make_skip(i, 0)
                evacuate(i, 7)
                if not first:
                    square(c - 1)
                    store_x1(i - 1, 0, c - 2)
                keep_whole(i)
                if first:
                    for n in range(EARLY, PIECES):
                        weight_hi(n)
                evacuate(i, 8)
                evacuate(i, 9)
                if not last:
                    norm_hi(i + 1, 0)
                    norm_hi(i + 1, 1)
                if not first:
                    mean_square(c - 1, 1)
                else:
                    act.wait_ge(lo_made, PIECES)
                    make_skip(i, 0)
                if not last:
                    evacuate(i + 1, 0)
                keep_tok(i, 1)
                gate_hi(c)
                if not last:
                    evacuate(i + 1, 1)
                make_skip(i, 1)
                square(c)
                if not first:
                    store_x1(i - 1, 1, c - 1)
                if not last:
                    evacuate(i + 1, 2)
                    first_taps(i + 1, 0)
                    make_decay(i + 1)
                    evacuate(i + 1, 3)
                    first_taps(i + 1, 1)
                    scale_taps(i + 1, 1)
                    evacuate(i + 1, 4)
                    scale_taps(i + 1, 2)
                    evacuate(i + 1, 5)
                    first_taps(i + 1, 2)
                    scale_taps(i + 1, 3)
                mean_square(c, 0)
                if not last:
                    for run in range(3):
                        conv_silu(i + 1, run)
                    keep_halo(i + 1)

            for n in range(3):
                weight_hi(n)
            norm_hi(0, 0)
            norm_hi(0, 1)
            weight_hi(3)
            weight_hi(4)
            act.wait_ge(zeroed, 7)
            evacuate(0, 0)
            weight_hi(5)
            evacuate(0, 1)
            first_taps(0, 0)
            act.wait_ge(a_negated, 1)
            make_decay(0)
            weight_hi(6)
            evacuate(0, 2)
            weight_hi(7)
            weight_hi(8)
            evacuate(0, 3)
            first_taps(0, 1)
            scale_taps(0, 1)
            evacuate(0, 4)
            weight_hi(9)
            weight_hi(10)
            scale_taps(0, 2)
            evacuate(0, 5)
            first_taps(0, 2)
            scale_taps(0, 3)
            for run in range(3):
                conv_silu(0, run)
            keep_halo(0)
            act.wait_ge(lo_made, EVENTS)
            body(0, True, False)
            with act.Fori(1, BLOCKS - 1) as i:
                body(i, False, False)
            body(BLOCKS - 1, False, True)
            c = 2 * BLOCKS - 1
            store_x1(BLOCKS - 1, 0, c - 1)
            gate_hi(c)
            square(c)
            mean_square(c, 1)
            store_x1(BLOCKS - 1, 1, c)

        @block.vector
        def _(dve):
            def weight_lo(n):
                dve.wait_ge(hi_made, n + 1)
                hi, lo, raw = piece(n)
                if n < EVENTS:
                    dve.tensor_tensor(lo, raw, hi, ALU.subtract).then_inc(lo_made, 1)
                    return
                for k in range(2):
                    made = dve.scalar_tensor_tensor(lo[:, k, :], raw[:, k, :], col(C_NW + 2 * (n - EVENTS) + k),
                                                    hi[:, k, :], ALU.mult, ALU.subtract)
                made.then_inc(lo_made, 1)

            def norm_stats(j):
                dve.wait_ge(x_in, 16 * j + 16)
                for b in range(BATCH):
                    dve.bn_stats(stats[:, b, :], xin[:, b, :]).then_inc(stats_made, 1)
                dve.wait_ge(stats_made, 2 * j + 2)
                dve.sem_inc(stats_seen, 1)
                for b in range(BATCH):
                    dve.bn_aggr(moments[:, b, :], stats[:, b, :]).then_inc(moments_made, 1)

            def normalise(j):
                dve.wait_ge(rstd_made, j + 1)
                for b in range(BATCH):
                    dve.tensor_scalar(xin[:, b, :], xin[:, b, :], moments[:, b, 0:1], rstd[:, b:b + 1],
                                      ALU.subtract, ALU.mult).then_inc(xn_made, 1)

            def norm_lo(j, b):
                dve.wait_ge(xn_hi_made, 2 * j + b + 1)
                t = slice(b * P, (b + 1) * P)
                dve.tensor_tensor(xn_lo[:, :, t], ps_proj[b][:].rearrange("p (k t) -> p k t", k=KT), xn_hi[:, :, t],
                                  ALU.subtract).then_inc(xn_split, 1)

            def softplus(j, opening=False):
                dve.wait_ge(dt_exp, j + 1)
                dve.tensor_scalar(dt_p[:], dt_e[:], log_c[-1], None, ALU.mult).then_inc(soft_step, 1)
                for n, c in enumerate(reversed(log_c[:-1])):
                    dve.wait_ge(soft_step, LOGN * j + n + 1)
                    dve.scalar_tensor_tensor(dt_p[:], dt_p[:], c, dt_e[:], ALU.add, ALU.mult).then_inc(soft_step, 1)
                dve.wait_ge(soft_step, LOGN * (j + 1))
                if not opening:
                    dve.wait_ge(tok_turned, 2 * j - 1)
                dve.tensor_tensor(dt_run[:, 0, :], dt_v[:], dt_p[:], ALU.add).then_inc(dt_made, 1)

            def run_decay(j):
                dve.wait_ge(decay_made, j + 1)
                dve.tensor_tensor_scan(dt_run[:, 1, :], decay[:], zero[:].to_broadcast([P, P]), 1.0,
                                       ALU.mult, ALU.add).then_inc(run_made, 1)
                dve.wait_ge(run_made, j + 1)
                dve.memset(decay[:, 0:1], 0.0).then_inc(decay_cut, 1)

            def conv_taps(j, run):
                for k in range(1, TAPS):
                    for m in CONV_RUNS[run]:
                        if k == 1:
                            dve.wait_ge(tap_first, CT * j + CONV_ORDER.index(m) + 1)
                        else:
                            dve.wait_ge(tap_made, N_TAPS * j + TAP_AT[m, k - 1] + 1)
                        dve.scalar_tensor_tensor(cx[:, m, :, :], cin[:, m, :, k:k + P], col(C_CW + 4 * m + k),
                                                 cx[:, m, :, :], ALU.mult, ALU.add).then_inc(tap_made, 1)

            by_pair = xpad[:].rearrange("p (q o) d -> p q (o d)", o=2)
            PAIR = HEADS // 2

            def xpad_half(odd):
                at = odd * 3 * HEAD
                return by_pair[:, :, at:at + HEAD]

            def pick(by_head, odd):
                v = by_head.rearrange("p (q o) -> p q o", o=2)[:, :, odd:odd + 1]
                return v.to_broadcast([P, PAIR, HEAD])

            def by_head_half(t, odd):
                return t.rearrange("p (q o d) -> p q o d", o=2, d=HEAD)[:, :, odd, :]

            def make_xpad(i, b):
                c = 2 * i + b
                dve.wait_ge(x_turned, c + 1)
                dve.wait_ge(tok_kept, c + 1)
                dve.wait_ge(ring_free, GROUPS * c)
                for odd in range(2):
                    dve.tensor_tensor(xpad_half(odd), by_head_half(ps_x[:], odd), pick(tok_dt[b], odd),
                                      ALU.mult).then_inc(xpad_made, 1)

            def scale_carry(i, b):
                dve.wait_ge(carry_made, 2 * i + b + 1)
                v = "p (h d) -> p h d"
                run = tok_run[b].unsqueeze(2).to_broadcast([P, HEADS, HEAD])
                dve.tensor_tensor(rows[:].rearrange(v, d=HEAD), ps_x[:].rearrange(v, d=HEAD), run,
                                  ALU.mult).then_inc(carry_scaled, 1)

            def scan(i, b, g):
                dve.wait_ge(ring_in[g % RING], 16 * (SLOT_USES * (2 * i + b) + g // RING + 1))
                slot = ring[:, g % RING, :, :].rearrange(flat)
                dve.tensor_tensor_scan(slot, slot, eye[:].rearrange(flat), 0.0, ALU.mult, ALU.add).then_inc(scanned, 1)

            def keep_end(i, b, g):
                dve.wait_ge(scanned, GROUPS * (2 * i + b) + g + 1)
                dve.tensor_copy(to_end[:, g * GH:(g + 1) * GH], ring[:, g % RING, :, P - 1]).then_inc(end_kept, 1)

            def mix(i, b, g):
                c = 2 * i + b
                slot = ring[:, g % RING, :, :]
                dve.wait_ge(end_kept, GROUPS * c + g + 1)
                dve.tensor_tensor(slot, slot, tok_cb[b].unsqueeze(1).to_broadcast([P, GH, P]),
                                  ALU.mult).then_inc(mixed, 1)

            def make_xw(i, b):
                c = 2 * i + b
                dve.wait_ge(end_kept, GROUPS * (c + 1))
                dve.wait_ge(carry_added, c + 1)
                for odd in range(2):
                    dve.tensor_tensor(by_head_half(rows[:], odd), xpad_half(odd), pick(to_end[:], odd),
                                      ALU.mult).then_inc(xw_made, 1)

            def update_state(c, b):
                dve.wait_ge(update_made, c + 1)
                dve.wait_ge(state_faded, c + 1)
                dve.tensor_tensor(state[:, b, :], state[:, b, :], ps_x[:], ALU.add).then_inc(state_made, 1)

            def make_y(c):
                dve.wait_ge(ring_free, GROUPS * (c + 1))
                dve.wait_ge(skip_made, c + 1)
                dve.wait_ge(ss_made, c)
                dve.tensor_tensor(gated[:].rearrange("p m t -> p (m t)"), skip[:].rearrange("p m t -> p (m t)"), ps_y[:],
                                  ALU.add).then_inc(y_made, 1)

            def gate(i, b, c):
                dve.wait_ge(y_made, c + 1)
                dve.wait_ge(evacuated, EVENTS * i + EVENTS)
                dve.tensor_tensor(gated[:], gated[:], sz[:, :, b, :], ALU.mult).then_inc(gate_made, 1)

            def gate_lo(c):
                dve.wait_ge(g_hi_made, c + 1)
                dve.tensor_tensor(g_lo[:], gated[:], g_hi[:], ALU.subtract).then_inc(g_split, 1)

            def make_x1(i, b, c):
                dve.wait_ge(out_made, c + 1)
                dve.wait_ge(rs_made, c + 1)
                dve.wait_ge(xres_in[b], 16 * i + 16)
                dve.scalar_tensor_tensor(xres[:, b, :], ps_out[:], rs[:, b:b + 1], xres[:, b, :],
                                         ALU.mult, ALU.add).then_inc(x1_made, 1)

            def scan_keep(i, b, g):
                scan(i, b, g)
                keep_end(i, b, g)

            def turn_over(i, b, first, last):
                opening = first and b == 0
                prev = 2 * i + b - 1
                scan_keep(i, b, 0)
                if not opening:
                    make_y(prev)
                    if not (last and b == 1):
                        update_state(prev, 1 - b)
                    gate(i if b else i - 1, 1 - b, prev)
                make_xpad(i, b)
                scan_keep(i, b, 1)
                scale_carry(i, b)
                if b == 0 and not last:
                    norm_stats(i + 1)
                if not first:
                    make_x1(i - 1, b, prev - 1)
                if not opening:
                    gate_lo(prev)
                scan_keep(i, b, 2)
                scan_keep(i, b, 3)

            def body(i, first, last):
                turn_over(i, 0, first, last)
                if not last:
                    normalise(i + 1)
                scan_keep(i, 0, 4)
                scan_keep(i, 0, 5)
                if first:
                    for n in range(EARLY, PIECES):
                        weight_lo(n)
                scan_keep(i, 0, 6)
                scan_keep(i, 0, 7)
                if not last:
                    norm_lo(i + 1, 0)
                    norm_lo(i + 1, 1)
                for g in range(POOL_MIXES[0], GROUPS):
                    mix(i, 0, g)
                make_xw(i, 0)
                turn_over(i, 1, first, last)
                if not last:
                    softplus(i + 1)
                scan_keep(i, 1, 4)
                if not last:
                    conv_taps(i + 1, 0)
                    run_decay(i + 1)
                for g in range(5, GROUPS):
                    scan_keep(i, 1, g)
                for g in range(POOL_MIXES[1], GROUPS):
                    mix(i, 1, g)
                if not last:
                    conv_taps(i + 1, 2)
                    make_xw(i, 1)

            def low_halves_max(at, landed, raw):
                for n in landed:
                    dve.wait_ge(hand.raw_in[n], 16)
                low = raw.bitcast(I16).rearrange("p n (t half) -> p n t half", half=2)[:, :, :, 0]
                dve.tensor_reduce(hand.low_max[:, at:at + 1], low, mybir.AxisListType.XY, ALU.max,
                                  apply_absolute_value=True).then_inc(hand.low_max_made, 1)

            norm_stats(0)
            normalise(0)
            weight_lo(0)
            weight_lo(1)
            weight_lo(2)
            norm_lo(0, 0)
            norm_lo(0, 1)
            weight_lo(3)
            weight_lo(4)
            softplus(0, opening=True)
            weight_lo(5)
            conv_taps(0, 0)
            dve.wait_ge(filled, 2)
            run_decay(0)
            for n in range(6, EARLY):
                weight_lo(n)
            conv_taps(0, 2)
            dve.wait_ge(zeroed, 9)
            body(0, True, False)
            with dve.Fori(1, BLOCKS - 1) as i:
                body(i, False, False)
            body(BLOCKS - 1, False, True)
            c = 2 * BLOCKS - 1
            make_y(c)
            make_x1(BLOCKS - 1, 0, c - 1)
            gate(BLOCKS - 1, 1, c)
            gate_lo(c)
            low_halves_max(0, range(0, LANDED, 2), hand.h_raw[0][:, MT - LANDED // 2:, :])
            low_halves_max(1, range(1, LANDED, 2), hand.h_raw[1][:, MT - LANDED // 2:, :])
            low_halves_max(2, range(LANDED, 2 * EARLY_TILES), hand.raw[:, 0:2 * EARLY_TILES - LANDED, :])
            dve.wait_ge(hand.low_max_made, 3)
            dve.tensor_reduce(hand.low_max[:, 3:], hand.low_max[:, 0:3], mybir.AxisListType.X, ALU.max,
                              apply_absolute_value=True).then_inc(hand.low_max_made, 1)
            make_x1(BLOCKS - 1, 1, c)

        @block.tensor
        def _(pe):
            def turn_xn(j, b, opening=False):
                pe.wait_ge(xn_made, 2 * j + b + 1)
                if not opening:
                    pe.wait_ge(evacuated, EVENTS * j - 1 + b)
                for k in range(KT):
                    made = pe.transpose(ps_proj[b][:, k * P:(k + 1) * P], xin[:, b, k * P:(k + 1) * P], eye1)
                made.then_inc(xn_turned, 1)

            def project(j, e, halves=(0, 1)):
                tiles = event_tiles(e)
                for half in halves[:len(tiles)]:
                    if half == 0 and e < 2:
                        pe.wait_ge(xn_split, 2 * j + 2)
                    elif half == 0:
                        pe.wait_ge(evacuated, EVENTS * j + e - 1)
                    m = tiles[half]
                    out = ps_proj[e % 2][:, half * TOK:(half + 1) * TOK]
                    cols = slice(m * P, (m + 1) * P)
                    for k in range(KT):
                        pe.matmul(out, win_hi[:, k, cols], xn_hi[:, k, :], start=(k == 0), stop=False)
                        pe.matmul(out, win_hi[:, k, cols], xn_lo[:, k, :], start=False, stop=False)
                        made = pe.matmul(out, win_lo[:, k, cols], xn_hi[:, k, :], start=False, stop=(k == KT - 1))
                    if m == tiles[-1]:
                        made.then_inc(projected, 1)

            def turn_tok(i, b, opening=False):
                pe.wait_ge(conv_made, CT * i + 2)
                pe.wait_ge(tok_kept, 2 * i + b)
                if not opening:
                    pe.wait_ge(gvar_made, 2 * i + b - 1)
                pe.transpose(ps_tok[:, 0:P], cx[:, ZT, b, :], eye1)
                if b == 0:
                    pe.wait_ge(run_made, i + 1)
                    pe.transpose(ps_tok[:, 2 * P:3 * P], dt_run[:, 0, :], eye1)
                    pe.transpose(ps_tok[:, 3 * P:4 * P], dt_run[:, 1, :], eye1)
                else:
                    pe.wait_ge(whole_kept, i + 1)
                pe.matmul(ps_tok[:, P:2 * P], cx[:, ZT, b, :], cx[:, ZT + 1, b, :], start=True, stop=True).then_inc(tok_turned, 1)

            def turn_x(i, b, updated):
                pe.wait_ge(conv_made, CT * (i + 1))
                if updated:
                    pe.wait_ge(state_made, 2 * i + b)
                else:
                    pe.wait_ge(carry_scaled, 2 * i + b)
                for m in range(ZT):
                    made = pe.transpose(ps_x[:, m * P:(m + 1) * P], cx[:, m, b, :], eye1)
                made.then_inc(x_turned, 1)

            def carry(i, b):
                pe.wait_ge(xpad_made, 2 * (2 * i + b) + 2)
                for h in range(2):
                    made = pe.matmul(ps_x[:, h * 512:(h + 1) * 512], cx[:, ZT + 1, b, :],
                                     state[:, b, h * 512:(h + 1) * 512], start=True, stop=True)
                made.then_inc(carry_made, 1)

            def whole_decay(i):
                pe.wait_ge(tok_kept, 2 * i + 1)
                pe.matmul(ps_whole, last_row[:], tok[:, 3 * P:4 * P], start=True, stop=True).then_inc(whole_made, 1)

            def add_carry(i, b):
                c = 2 * i + b
                pe.wait_ge(carry_scaled, c + 1)
                pe.wait_ge(y_made, c)
                for m in range(ZT):
                    made = pe.matmul(ps_y[:, m * P:(m + 1) * P], rows[:, m * P:(m + 1) * P], eye1,
                                     start=(m % 4 == 0), stop=False, skip_group_check=True)
                made.then_inc(carry_added, 1)

            def group(i, b, g):
                c = 2 * i + b
                if g < POOL_MIXES[b]:
                    pe.wait_ge(mixed_pool, POOL_BLOCK * i + b * POOL_MIXES[0] + g + 1)
                else:
                    pe.wait_ge(mixed, DVE_BLOCK * i + b * (GROUPS - POOL_MIXES[0]) + g - POOL_MIXES[b] + 1)
                for q in range(2):
                    for pair in range(GH // 2):
                        h = 2 * pair + q
                        made = pe.matmul(ps_y[32 * pair:32 * pair + 32, g * P:(g + 1) * P], xpad[:, g * GH + h, :],
                                         ring[:, g % RING, h, :], start=False, stop=(q == 1), skip_group_check=True)
                made.then_inc(ring_free, 1)

            def update(c, b):
                pe.wait_ge(xw_made, 2 * c + 2)
                for h in range(2):
                    made = pe.matmul(ps_x[:, h * 512:(h + 1) * 512], tok_b[b], rows[:, h * 512:(h + 1) * 512],
                                     start=True, stop=True)
                made.then_inc(update_made, 1)

            def project_out(c, tiles=range(ZT)):
                if tiles[0] == 0:
                    pe.wait_ge(g_split, c + 1)
                    pe.wait_ge(x1_made, c)
                    if isinstance(c, int) and c == 0:
                        pe.wait_ge(lo_made, PIECES)
                for k in tiles:
                    pe.matmul(ps_out[:], g_hi[:, k, :], wout_hi[:, k, :], start=(k == 0), stop=False)
                    pe.matmul(ps_out[:], g_hi[:, k, :], wout_lo[:, k, :], start=False, stop=False)
                    made = pe.matmul(ps_out[:], g_lo[:, k, :], wout_hi[:, k, :], start=False, stop=(k == ZT - 1))
                if tiles[-1] == ZT - 1:
                    made.then_inc(out_made, 1)

            def sum_squares(c, i, kept):
                pe.wait_ge(sq_folded, c + 1)
                pe.wait_ge(tok_kept, kept)
                pe.wait_ge(whole_kept, i + 1)
                for m in range(ZT // 2):
                    made = pe.matmul(ps_ss, gated[:, m, :], ones[:], start=(m == 0), stop=(m == ZT // 2 - 1))
                made.then_inc(ss_made, 1)

            def body(i, first, last):
                c = 2 * i
                turn_tok(i, 0, first)
                if not first:
                    update(c - 1, 1)
                project(i, 6, [0])
                turn_x(i, 0, True)
                project(i, 6, [1])
                carry(i, 0)
                whole_decay(i)
                project(i, 7, [0])
                add_carry(i, 0)
                group(i, 0, 0)
                project(i, 7, [1])
                group(i, 0, 1)
                project(i, 8)
                group(i, 0, 2)
                project(i, 9)
                group(i, 0, 3)
                if not last:
                    turn_xn(i + 1, 0)
                    turn_xn(i + 1, 1)
                if not first:
                    project_out(c - 1, range(ZT // 2))
                group(i, 0, 4)
                if not first:
                    project_out(c - 1, range(ZT // 2, ZT))
                    sum_squares(c - 1, i, c + 1)
                group(i, 0, 5)
                if not last:
                    project(i + 1, 0)
                group(i, 0, 6)
                group(i, 0, 7)
                turn_tok(i, 1)
                if not last:
                    update(c, 0)
                    project(i + 1, 1, [0])
                turn_x(i, 1, not last)
                if not last:
                    project(i + 1, 1, [1])
                carry(i, 1)
                if not last:
                    project(i + 1, 2, [0])
                add_carry(i, 1)
                group(i, 1, 0)
                if not last:
                    project(i + 1, 2, [1])
                group(i, 1, 1)
                if not last:
                    project(i + 1, 3)
                group(i, 1, 2)
                if not last:
                    project(i + 1, 4)
                group(i, 1, 3)
                if not last:
                    project(i + 1, 5)
                sum_squares(c, i, c + 2)
                group(i, 1, 4)
                project_out(c)
                for g in range(5, GROUPS):
                    group(i, 1, g)

            pe.wait_ge(filled, 1)
            turn_xn(0, 0, True)
            turn_xn(0, 1, True)
            for e in range(6):
                pe.wait_ge(lo_made, e + 1)
                project(0, e)
            pe.wait_ge(filled, 2)
            pe.wait_ge(lo_made, EVENTS)
            body(0, True, False)
            with pe.Fori(1, BLOCKS - 1) as i:
                body(i, False, False)
            body(BLOCKS - 1, False, True)
            c = 2 * BLOCKS - 1
            project_out(c, range(ZT // 2))
            sum_squares(c, BLOCKS - 1, c + 1)
            project_out(c, range(ZT // 2, ZT))


def mlp_phase(nc, packed, down_s, out, hand):
    with ExitStack() as ctx:
        def sb(name, shape, dt=F32):
            return ctx.enter_context(nc.sbuf_tensor(name, shape, dt))

        def sem(name):
            return ctx.enter_context(nc.semaphore(name))

        up = {"gate": (sb("wg_hi", [P, KT, INTER], F32R), sb("wg_lo", [P, KT, INTER], F32R)),
              "up": (sb("wu_hi", [P, KT, INTER], F32R), sb("wu_lo", [P, KT, INTER], F32R))}
        wd_hi, wd_lo = sb("wd_hi", [P, MT, HID], F32R), sb("wd_lo", [P, MT, HID], F32R)
        h_hi, h_lo, silu_g, hidden = hand.h_hi, hand.h_lo, hand.silu_g, hand.hidden
        xn_hi, xn_lo = hand.xn_hi, sb("x1n_lo", [P, KT, BT], F32R)
        xin = hand.xin
        res = hand.res
        scale_d = hand.scale_d
        scales = sb("scales", [P, 2 * MT])
        eye = sb("eye2", [P, P])
        lo_max = sb("lo_max", [P, PIECES2 + 1])
        lo_row, lo_any = hand.low_row, sb("lo_any", [1, 1])
        minus_half, eps = sb("minus_half2", [P, TT]), sb("eps2", [P, TT])
        stats, moments = sb("stats2", [P, TT, 6]), sb("moments2", [P, TT, 2])
        spread, rstd = sb("spread2", [P, TT]), sb("rstd2", [P, TT])
        pb = [ctx.enter_context(nc.psum_tensor(f"pb{n}", [P, BT], F32)) for n in range(8)]
        ps_g, ps_u, ps_t, ps_o = pb[0:2], pb[2:4], pb[4:6], pb[6:8]

        x_in, raw_in, x1_out = hand.x_in, hand.raw_in, hand.x1_out
        hi_made, lo_made = sem("whi_made"), sem("wlo_made")
        max_made, row_in, any_made, low_any_made = sem("max_made"), sem("row_in"), sem("any_made"), sem("low_any_made")
        scales_in, res_in, stored = sem("scales_in"), [sem("res_in0"), sem("res_in1")], [sem("stored0"), sem("stored1")]
        zeroed, filled = sem("zeroed2"), sem("filled2")
        stats_made, stats_seen, moments_made, eps_added, rstd_made = sem("stats2_made"), sem("stats2_seen"), sem("moments2_made"), sem("eps2_added"), sem("rstd2_made")
        xn_made, turned, xhi_made, split = sem("x1n_made"), sem("x1n_turned"), sem("x1n_hi_made"), sem("x1n_split")
        gu_made, silu_made, hidden_made, hhi_made, h_split = sem("gu_made"), sem("silu_made"), sem("hidden_made"), sem("hhi_made"), sem("h_split")
        down_made, down_scaled, out_ready = sem("down_made"), sem("down_scaled"), sem("out_ready")

        x_by_block = hand.x1_by_block
        out_by_block = out.rearrange("b l h -> (b l) h").rearrange("(j t p) h -> j p t h", t=TT, p=P)
        pieces, first_pieces, with_tile = hand.pieces, hand.first_pieces, hand.with_tile

        def piece(n, part):
            kind, m = pieces[n]
            raw = hand.raw_piece(n)[0]
            if kind == "down":
                return (wd_hi, wd_lo)[part][:, m, :], raw
            return up[kind][part][:, :, m * P:(m + 1) * P], raw

        FIRST_MAX = 4

        def landed_in(m, part):
            n = 2 * (MT - 1 - m) + part
            return n if n < LANDED else -1

        def t_cols(t):
            return slice(t * P, (t + 1) * P)

        block = ctx.enter_context(nc.Block())

        @block.sync
        def _(sp):
            def load_x(j):
                sp.dma_start(xin[:], x_by_block[bass.ds(j, 1)].rearrange("a p t h -> (a p) t h")).then_inc(x_in, 16)

            for free in stored:
                sp.sem_inc(free, AHEAD)
            sp.dma_start(scales[:], packed).then_inc(scales_in, 16)
            sp.dma_start(scale_d[:], down_s.to_broadcast([P, HID])).then_inc(scales_in, 16)
            for b in range(BATCH):
                sp.wait_ge(x1_out[b], 16 * BLOCKS)
            sp.wait_ge(turned, TT)
            load_x(1)
            for n in range(LANDED + RAW_SLOTS, PIECES2):
                sp.wait_ge(lo_made, n - RAW_SLOTS + 1)
                sp.dma_start(*hand.raw_piece(n)).then_inc(raw_in[n], 16)

            def body(j, first, last):
                for t in range(TT):
                    if t == 1 and not (first or last):
                        sp.wait_ge(turned, TT * j + TT)
                        load_x(j + 1)
                    sp.wait_ge(stored[t % 2], AHEAD + 16 * (2 * j + t // 2))
                    sp.dma_start(res[:, t % 2, :], x_by_block[bass.ds(j, 1), :, t, :].rearrange("a p h -> (a p) h")).then_inc(res_in[t % 2], 16)
                    if t >= 1:
                        store(j, t - 1)
                store(j, TT - 1)

            def store(j, t):
                sp.wait_ge(out_ready, AHEAD + TT * j + t + 1)
                sp.dma_start(out_by_block[bass.ds(j, 1), :, t, :].rearrange("a p h -> (a p) h"), res[:, t % 2, :]).then_inc(stored[t % 2], 16)

            sp.wait_ge(low_any_made, 1)
            sp.wait_ge(max_made, PIECES2 + 1)
            sp.dma_start(lo_row[:], lo_max[:, PIECES2:]).then_inc(row_in, 16)
            body(0, True, False)
            with sp.Fori(1, NB - 1) as j:
                body(j, False, False)
            body(NB - 1, False, True)
            for n in range(2):
                sp.wait_ge(stored[n], AHEAD + 16 * 2 * NB)

        @block.gpsimd
        def _(pool):
            pool.sem_inc(out_ready, AHEAD)
            pool.memset(minus_half[:], -0.5).then_inc(zeroed, 1)
            pool.memset(eps[:], EPS).then_inc(zeroed, 1)
            pool.memset(eye[:], 0.0).then_inc(zeroed, 1)
            pool.wait_ge(zeroed, 3)
            pool.affine_select(out=eye[:], in_=eye[:], compare_op=ALU.not_equal, fill=1.0, base=0,
                               pattern=[[-1, P]], channel_multiplier=1).then_inc(filled, 1)

            def norm_scale(j):
                pool.wait_ge(moments_made, TT * j + TT)
                pool.tensor_tensor(spread[:], moments[:, :, 1], eps[:], ALU.add).then_inc(eps_added, 1)
                pool.wait_ge(eps_added, j + 1)
                pool.tensor_tensor(rstd[:], spread[:], minus_half[:], ALU.pow).then_inc(rstd_made, 1)

            def body(j, first, last):
                if not (first or last):
                    norm_scale(j + 1)
                for t in range(TT):
                    pool.wait_ge(down_scaled, AHEAD + TT * j + t + 1)
                    pool.wait_ge(res_in[t % 2], 16 * (2 * j + t // 2 + 1))
                    pool.tensor_tensor(res[:, t % 2, :], res[:, t % 2, :], hidden[:, t % 2, :], ALU.add).then_inc(out_ready, 1)

            norm_scale(0)
            for n in range(PIECES2):
                if n == 2 * MT:
                    norm_scale(1)
                pool.wait_ge(hi_made, n + 1)
                lo, r = piece(n, 1)
                pool.tensor_tensor(lo, r, piece(n, 0)[0], ALU.subtract).then_inc(lo_made, 1)
            body(0, True, False)
            with pool.Fori(1, NB - 1) as j:
                body(j, False, False)
            body(NB - 1, False, True)

        @block.scalar
        def _(act):
            def weight_hi(n):
                act.wait_ge(raw_in[n], 16)
                hi, r = piece(n, 0)
                act.activation(hi, r, ACT.Copy).then_inc(hi_made, 1)

            def norm_hi(j, t):
                act.wait_ge(turned, TT * j + t + 1)
                act.activation(xn_hi[:, :, t_cols(t)], ps_t[t % 2][:].rearrange("p (k t) -> p k t", k=KT), ACT.Copy).then_inc(xhi_made, 1)

            def body(j, first, last):
                for m in range(MT):
                    n = MT * j + m
                    act.wait_ge(gu_made, n + 1)
                    if m >= 2:
                        act.wait_ge(hidden_made, AHEAD + n - 1)
                    else:
                        act.wait_ge(hidden_made, AHEAD + MT * j)
                    act.activation(silu_g[:, m % 2, :], ps_g[m % 2][:], ACT.Silu, scale=scales[:, m:m + 1]).then_inc(silu_made, 1)
                    if first:
                        for w in with_tile[m]:
                            weight_hi(w)
                    act.wait_ge(hidden_made, AHEAD + n + 1)
                    if first and landed_in(m, 0) >= 0:
                        act.wait_ge(lo_made, landed_in(m, 0) + 1)
                    act.activation(h_hi[:, m, :], hidden[:, m % 2, :], ACT.Copy).then_inc(hhi_made, 1)
                if not last:
                    for t in range(TT):
                        norm_hi(j + 1, t)

            for n in range(first_pieces):
                weight_hi(n)
            for t in range(TT):
                norm_hi(0, t)
            act.wait_ge(scales_in, 32)
            body(0, True, False)
            with act.Fori(1, NB - 1) as j:
                body(j, False, False)
            body(NB - 1, False, True)

        @block.vector
        def _(dve):
            def norm(j):
                dve.wait_ge(x_in, 16 * j + 16)
                for t in range(TT):
                    dve.bn_stats(stats[:, t, :], xin[:, t, :]).then_inc(stats_made, 1)
                dve.wait_ge(stats_made, TT * j + TT)
                dve.sem_inc(stats_seen, 1)
                for t in range(TT):
                    dve.bn_aggr(moments[:, t, :], stats[:, t, :]).then_inc(moments_made, 1)

            def normalise(j):
                dve.wait_ge(rstd_made, j + 1)
                for t in range(TT):
                    dve.tensor_scalar(xin[:, t, :], xin[:, t, :], moments[:, t, 0:1], rstd[:, t:t + 1],
                                      ALU.subtract, ALU.mult).then_inc(xn_made, 1)

            def norm_lo(j, t):
                dve.wait_ge(xhi_made, TT * j + t + 1)
                dve.tensor_tensor(xn_lo[:, :, t_cols(t)], ps_t[t % 2][:].rearrange("p (k t) -> p k t", k=KT),
                                  xn_hi[:, :, t_cols(t)], ALU.subtract).then_inc(split, 1)

            def scale_down(j, t):
                dve.wait_ge(down_made, TT * j + t + 1)
                if t >= 2:
                    dve.wait_ge(out_ready, AHEAD + TT * j + t - 1)
                dve.tensor_tensor(hidden[:, t % 2, :], ps_o[t % 2][:], scale_d[:], ALU.mult).then_inc(down_scaled, 1)

            def lo_part_max(n):
                dve.wait_ge(lo_made, n + 1)
                lo = piece(n, 1)[0].bitcast(I32)
                dve.tensor_reduce(lo_max[:, n:n + 1], lo, mybir.AxisListType.X if pieces[n][0] == "down" else mybir.AxisListType.XY,
                                  ALU.max, apply_absolute_value=True).then_inc(max_made, 1)

            def body(j, first, last):
                for m in range(MT):
                    n = MT * j + m
                    if first and m == MT - 1:
                        dve.wait_ge(row_in, 16)
                        dve.tensor_reduce(lo_any[:], lo_row[:], mybir.AxisListType.X, ALU.max, apply_absolute_value=True).then_inc(any_made, 1)
                    dve.wait_ge(silu_made, n + 1)
                    if m >= 2:
                        dve.wait_ge(h_split, n - 1)
                    else:
                        dve.wait_ge(out_ready, AHEAD + TT * j)
                    dve.scalar_tensor_tensor(hidden[:, m % 2, :], ps_u[m % 2][:], scales[:, MT + m:MT + m + 1],
                                             silu_g[:, m % 2, :], ALU.mult, ALU.mult).then_inc(hidden_made, 1)
                    if first:
                        for w in range(min(FIRST_MAX + 3 * m, PIECES2), min(FIRST_MAX + 3 * (m + 1), PIECES2)):
                            lo_part_max(w)
                        if m == MT - 2:
                            dve.wait_ge(max_made, PIECES2)
                            dve.tensor_reduce(lo_max[:, PIECES2:], lo_max[:, 0:PIECES2], mybir.AxisListType.X,
                                              ALU.max, apply_absolute_value=True).then_inc(max_made, 1)
                    dve.wait_ge(hhi_made, n + 1)
                    if first and landed_in(m, 1) >= 0:
                        dve.wait_ge(lo_made, landed_in(m, 1) + 1)
                    dve.tensor_tensor(h_lo[:, m, :], hidden[:, m % 2, :], h_hi[:, m, :], ALU.subtract).then_inc(h_split, 1)
                    if m == 2 and not last:
                        norm(j + 1)
                    if m == 5 and not last:
                        normalise(j + 1)
                dve.wait_ge(h_split, MT * j + MT)
                scale_down(j, 0)
                scale_down(j, 1)
                if not last:
                    for t in range(TT):
                        norm_lo(j + 1, t)
                scale_down(j, 2)
                scale_down(j, 3)

            for free in (hidden_made, down_scaled):
                dve.sem_inc(free, AHEAD)
            norm(0)
            dve.wait_ge(hand.low_in, 16)
            dve.tensor_reduce(hand.low_any[:], hand.low_row[:], mybir.AxisListType.X, ALU.max,
                              apply_absolute_value=True).then_inc(low_any_made, 1)
            normalise(0)
            for t in range(TT):
                norm_lo(0, t)
            for n in range(FIRST_MAX):
                lo_part_max(n)
            body(0, True, False)
            with dve.Fori(1, NB - 1) as j:
                body(j, False, False)
            body(NB - 1, False, True)

        @block.tensor
        def _(pe):
            def turn(j, t):
                pe.wait_ge(xn_made, TT * j + t + 1)
                if t >= 2:
                    pe.wait_ge(split, TT * j + t - 1)
                for k in range(KT):
                    made = pe.transpose(ps_t[t % 2][:, k * P:(k + 1) * P], xin[:, t, k * P:(k + 1) * P], eye[:])
                made.then_inc(turned, 1)

            def product(out_ps, w, cols, with_lo):
                hi, lo = w
                for k in range(KT):
                    pe.matmul(out_ps, hi[:, k, cols], xn_hi[:, k, :], start=(k == 0), stop=False)
                    made = pe.matmul(out_ps, hi[:, k, cols], xn_lo[:, k, :], start=False, stop=(not with_lo and k == KT - 1))
                    if with_lo:
                        made = pe.matmul(out_ps, lo[:, k, cols], xn_hi[:, k, :], start=False, stop=(k == KT - 1))
                return made

            def down(j, t, with_lo):
                if t >= 2:
                    pe.wait_ge(down_scaled, AHEAD + TT * j + t - 1)
                else:
                    pe.wait_ge(down_scaled, AHEAD + TT * j)
                for m in range(MT):
                    if t == 0 and m >= MT - 2:
                        pe.wait_ge(h_split, MT * j + m + 1)
                    pe.matmul(ps_o[t % 2][:], h_hi[:, m, t_cols(t)], wd_hi[:, m, :], start=(m == 0), stop=False)
                    if with_lo:
                        pe.matmul(ps_o[t % 2][:], h_hi[:, m, t_cols(t)], wd_lo[:, m, :], start=False, stop=False)
                    made = pe.matmul(ps_o[t % 2][:], h_lo[:, m, t_cols(t)], wd_hi[:, m, :], start=False, stop=(m == MT - 1))
                made.then_inc(down_made, 1)

            def gate_up(j, first, with_lo, tiles=range(MT)):
                pe.wait_ge(split, TT * j + TT)
                for m in tiles:
                    n = MT * j + m
                    if first:
                        pe.wait_ge(lo_made, pieces.index(("up", m)) + 1)
                    if m >= 2:
                        pe.wait_ge(hidden_made, AHEAD + n - 1)
                    else:
                        pe.wait_ge(hidden_made, AHEAD + MT * j)
                    product(ps_g[m % 2][:], up["gate"], slice(m * P, (m + 1) * P), with_lo)
                    product(ps_u[m % 2][:], up["up"], slice(m * P, (m + 1) * P), with_lo).then_inc(gu_made, 1)

            def finish(j, last, with_lo):
                pe.wait_ge(h_split, MT * j + MT - 2)
                down(j, 0, with_lo)
                down(j, 1, with_lo)
                if not last:
                    for t in range(TT):
                        turn(j + 1, t)
                down(j, 2, with_lo)
                down(j, 3, with_lo)

            def rest(with_lo):
                finish(0, False, with_lo)
                with pe.Fori(1, NB - 1) as j:
                    gate_up(j, False, with_lo)
                    finish(j, False, with_lo)
                gate_up(NB - 1, False, with_lo)
                finish(NB - 1, True, with_lo)

            pe.wait_ge(filled, 1)
            for t in range(TT):
                turn(0, t)
            pe.wait_ge(low_any_made, 1)
            with pe.If(pe.value_load(hand.low_any[:].bitcast(I32)) != 0):
                gate_up(0, True, True, range(EARLY_TILES))
            with pe.Else():
                gate_up(0, True, False, range(EARLY_TILES))
            gate_up(0, True, True, range(EARLY_TILES, MT))
            pe.wait_ge(lo_made, PIECES2)
            pe.wait_ge(any_made, 1)
            with pe.If(pe.value_load(lo_any[:].bitcast(I32)) != 0):
                rest(True)
            with pe.Else():
                rest(False)


def kernel(**inputs):
    import concourse.bacc as bacc
    from concourse.bass_utils import run_bass_kernel_spmd

    a = {name: np.ascontiguousarray(v) for name, v in inputs.items()}
    A, M = "L0_attn_", "L0_ffn_"

    def by_tile(v, width=P):
        return v.reshape(-1, width).T

    mup = a[A + "mup_vector"]
    dt_at = 2 * D_SSM + 2 * STATE
    twice = lambda v: np.concatenate([v, v]).reshape(P, 1)
    mixer_consts = np.concatenate([
        by_tile(mup[:dt_at]), twice(mup[dt_at:]),
        a[A + "conv_w"].reshape(CT, P, TAPS).transpose(1, 0, 2).reshape(P, CT * TAPS),
        by_tile(a[A + "conv_b"]), by_tile(np.repeat(a[A + "D"], HEAD)), by_tile(a[A + "norm_w"]),
        twice(a[A + "dt_bias"]), twice(a[A + "A_log"])], axis=1)
    mlp_scales = np.concatenate([by_tile(a[M + "gate_s"]), by_tile(a[M + "up_s"])], axis=1)
    arrays = {
        "x": a[A + "hidden_states"], "w_in": a[A + "W_in"], "w_out": a[A + "W_out"], "mixer_consts": mixer_consts,
        "gate_w": a[M + "gate_w"].T, "up_w": a[M + "up_w"].T, "down_w": a[M + "down_w"].T,
        "mlp_scales": mlp_scales, "down_s": a[M + "down_s"].reshape(1, HID),
    }
    arrays = {name: np.ascontiguousarray(v) for name, v in arrays.items()}

    nc = bacc.Bacc("TRN2", target_bir_lowering=False, num_devices=1, dynamic_dma_scratch_size=2048)
    d = {name: nc.dram_tensor(name, v.shape, mybir.dt.from_np(v.dtype), kind="ExternalInput").ap() for name, v in arrays.items()}
    out = nc.dram_tensor("out", (BATCH, LEN, HID), F32, kind="ExternalOutput").ap()
    decay_dram = nc.dram_tensor("decay_dram", (BLOCKS, BATCH, HEADS, P), F32, kind="Internal").ap()
    x1_dram = nc.dram_tensor("x1_dram", (BATCH, LEN, HID), F32, kind="Internal").ap()
    with ExitStack() as ctx:
        hand = Handover(nc, ctx, x1_dram, d["gate_w"], d["up_w"], d["down_w"])
        mixer_phase(nc, d["x"], d["w_in"], d["w_out"], d["mixer_consts"], decay_dram, x1_dram, hand)
        mlp_phase(nc, d["mlp_scales"], d["down_s"], out, hand)
    r = run_bass_kernel_spmd(nc, [arrays], core_ids=[0])
    return r.results[0]["out"]
```
